# Optimizing a Trainium2 kernel written in Bass

```python
import numpy as np
import jax
import jax.numpy as jnp

def _softmax(x, axis=-1):
    return jax.nn.softmax(x, axis=axis)

def _gelu(x):
    return jax.nn.gelu(x, approximate=True)

def _silu(x):
    return jax.nn.silu(x)

def _sigmoid(x):
    return jax.nn.sigmoid(x)

def _layernorm(x, axis=-1, eps=1e-05):
    m = jnp.mean(x, axis=axis, keepdims=True)
    v = jnp.var(x, axis=axis, keepdims=True)
    return (x - m) / jnp.sqrt(v + eps)

def _scatter_add(tgt, idx, src, axis=0):
    return tgt.at[idx].add(src)

def _segment_sum(src, seg, n):
    return jax.ops.segment_sum(src, seg, n)
kernel_name = 'mk_cond_seq_d4_seqx_r4_9128f4'

def setup_inputs(seed: int=0):
    np.random.seed(seed)
    _w = jnp.asarray

    def _rec_inputs():
        import jax
        import jax.numpy as jnp
        _rk = jax.random.key(seed)
        x = -0.0002928 + 1 * jax.random.normal(jax.random.fold_in(_rk, 1), (64, 64, 256), jnp.float32)
        _lenS = 64 - jax.random.randint(jax.random.fold_in(_rk, 7), (64,), 0, max(1, 64 // 4) + 1, jnp.int32)
        _lenS2 = 64 - jax.random.randint(jax.random.fold_in(_rk, 8), (64,), 0, max(1, 64 // 4) + 1, jnp.int32)
        cond_1024 = 0.0061147 + 1.02565 * jax.random.normal(jax.random.fold_in(_rk, 11), (64, 256), jnp.float32)
        fside_BxSx3_0 = jax.random.uniform(jax.random.fold_in(_rk, 12), (64, 64, 3), jnp.float32, 0.0, 0.999943)
        return (x, cond_1024, fside_BxSx3_0)
    x, cond_1024, fside_BxSx3_0 = _rec_inputs()

    def _L0_cond_setup():
        import jax, jax.numpy as jnp
        import numpy as np
        B, T, DIM = (4, 256, 256)
        COND = 256
        HEADS, DH = (16, 64)
        INNER = HEADS * DH
        MLP = 1024
        EPS = 1e-05

        def _layernorm(x):
            mu = jnp.mean(x, axis=-1, keepdims=True)
            var = jnp.mean(jnp.square(x - mu), axis=-1, keepdims=True)
            return (x - mu) * jax.lax.rsqrt(var + EPS)

        def _modulate(x, shift, scale):
            return x * (1.0 + scale) + shift

        def _attention(x, W_qkv, W_out, b_out):
            Bq, Tq, _ = x.shape
            qkv = x @ W_qkv
            q, k, v = jnp.split(qkv, 3, axis=-1)
            q = q.reshape(Bq, Tq, HEADS, DH)
            k = k.reshape(Bq, Tq, HEADS, DH)
            v = v.reshape(Bq, Tq, HEADS, DH)
            scale = DH ** (-0.5)
            attn = jnp.einsum('bqhd,bkhd->bhqk', q, k) * scale
            attn = jax.nn.softmax(attn, axis=-1)
            out = jnp.einsum('bhqk,bkhd->bqhd', attn, v).reshape(Bq, Tq, INNER)
            return out @ W_out + b_out

        def _ff(x, W1, b1, W2, b2):
            return jax.nn.gelu(x @ W1 + b1, approximate=False) @ W2 + b2
        key = jax.random.key(seed)
        ks = jax.random.split(key, 12)
        s = 0.02
        return {'x': jax.random.normal(ks[0], (B, T, DIM), jnp.float32), 'c': jax.random.normal(ks[1], (B, 1, COND), jnp.float32), 'W_mod': jax.random.normal(ks[2], (COND, 6 * DIM), jnp.float32) * s, 'b_mod': jax.random.normal(ks[3], (6 * DIM,), jnp.float32) * s, 'W_qkv': jax.random.normal(ks[4], (DIM, 3 * INNER), jnp.float32) * s, 'W_out': jax.random.normal(ks[5], (INNER, DIM), jnp.float32) * s, 'b_out': jax.random.normal(ks[6], (DIM,), jnp.float32) * s, 'W1': jax.random.normal(ks[7], (DIM, MLP), jnp.float32) * s, 'b1': jax.random.normal(ks[8], (MLP,), jnp.float32) * s, 'W2': jax.random.normal(ks[9], (MLP, DIM), jnp.float32) * s, 'b2': jax.random.normal(ks[10], (DIM,), jnp.float32) * s}
    _L0_cond_all = _L0_cond_setup()
    _L0_cond_in = {k: v for k, v in _L0_cond_all.items() if k in ('W_mod', 'b_mod', 'W_qkv', 'W_out', 'b_out', 'W1', 'b1', 'W2', 'b2')}
    del _L0_cond_all

    def _L1_cond_setup():
        import jax, jax.numpy as jnp
        import numpy as np
        HID = 256
        HEADS = 16
        HEAD_DIM = HID // HEADS
        ROPE_DIM = HEAD_DIM // 6 * 6
        HALF = ROPE_DIM // 3 // 2
        SWIGLU_HID = int(2 * (HID * 4) / 3)
        EPS = 1e-06
        THETA = 10000.0

        def rmsnorm(x, w, eps=EPS):
            xf = x.astype(jnp.float32)
            v = jnp.mean(xf * xf, axis=-1, keepdims=True)
            return w * (xf * jax.lax.rsqrt(v + eps)).astype(x.dtype)

        def modulate(x, shift, scale):
            return x * (1.0 + scale) + shift

        def rope_freqs():
            return 1.0 / THETA ** (jnp.arange(HALF, dtype=jnp.float32) / HALF)

        def apply_rope3d(q, k, positions):
            freqs = rope_freqs()
            ang = positions[..., :, None] * freqs
            ang = ang.reshape(ang.shape[0], ang.shape[1], -1)
            cos = jnp.cos(ang)[:, :, None, :]
            sin = jnp.sin(ang)[:, :, None, :]

            def rot(t):
                B, N, H, D = t.shape
                tr = t.reshape(B, N, H, D // 2, 2)
                t0, t1 = (tr[..., 0], tr[..., 1])
                out = jnp.stack([t0 * cos - t1 * sin, t0 * sin + t1 * cos], axis=-1)
                return out.reshape(B, N, H, D)
            return (rot(q), rot(k))
        key = jax.random.key(seed)
        ks = jax.random.split(key, 12)
        B, N = (2, 512)
        s = 0.02
        return {'x': jax.random.normal(ks[0], (B, N, HID), jnp.float32), 'c': jax.random.normal(ks[1], (B, HID), jnp.float32), 'positions': jax.random.uniform(ks[2], (B, N, 3), jnp.float32), 'norm1_w': jnp.ones((HID,), jnp.float32), 'qkv_w': jax.random.normal(ks[3], (3 * HID, HID), jnp.float32) * s, 'q_norm_w': jnp.ones((HEAD_DIM,), jnp.float32), 'k_norm_w': jnp.ones((HEAD_DIM,), jnp.float32), 'proj_w': jax.random.normal(ks[4], (HID, HID), jnp.float32) * s, 'proj_b': jnp.zeros((HID,), jnp.float32), 'norm2_w': jnp.ones((HID,), jnp.float32), 'w1': jax.random.normal(ks[5], (SWIGLU_HID, HID), jnp.float32) * s, 'w3': jax.random.normal(ks[6], (SWIGLU_HID, HID), jnp.float32) * s, 'w2': jax.random.normal(ks[7], (HID, SWIGLU_HID), jnp.float32) * s, 'ada_w': jax.random.normal(ks[8], (6 * HID, HID), jnp.float32) * s, 'ada_b': jnp.zeros((6 * HID,), jnp.float32)}
    _L1_cond_all = _L1_cond_setup()
    _L1_cond_in = {k: v for k, v in _L1_cond_all.items() if k in ('norm1_w', 'qkv_w', 'q_norm_w', 'k_norm_w', 'proj_w', 'proj_b', 'norm2_w', 'w1', 'w3', 'w2', 'ada_w', 'ada_b')}
    del _L1_cond_all

    def _L2_cond_setup():
        import jax, jax.numpy as jnp
        import numpy as np
        DIM = 256
        HEADS = 16
        DH = DIM // HEADS
        EPS = 1e-06

        def _ln(x):
            mu = jnp.mean(x, axis=-1, keepdims=True)
            var = jnp.mean((x - mu) ** 2, axis=-1, keepdims=True)
            return (x - mu) / jnp.sqrt(var + EPS)

        def _rotate_half(x):
            x1, x2 = (x[..., :x.shape[-1] // 2], x[..., x.shape[-1] // 2:])
            return jnp.concatenate((-x2, x1), axis=-1)
        key = jax.random.key(seed)
        ks = jax.random.split(key, 18)
        B, T, D = (4, 256, DIM)
        s = 0.02
        inp = {'x': jax.random.normal(ks[0], (B, T, D), jnp.float32), 'cond': jax.random.normal(ks[1], (B, D), jnp.float32), 'in_proj_w': jax.random.normal(ks[2], (3 * D, D), jnp.float32) * s, 'in_proj_b': jax.random.normal(ks[3], (3 * D,), jnp.float32) * s, 'out_w': jax.random.normal(ks[4], (D, D), jnp.float32) * s, 'out_b': jax.random.normal(ks[5], (D,), jnp.float32) * s, 'mlp_w1': jax.random.normal(ks[6], (4 * D, D), jnp.float32) * s, 'mlp_b1': jax.random.normal(ks[7], (4 * D,), jnp.float32) * s, 'mlp_w2': jax.random.normal(ks[8], (D, 4 * D), jnp.float32) * s, 'mlp_b2': jax.random.normal(ks[9], (D,), jnp.float32) * s, 'film_w': jax.random.normal(ks[10], (6 * D, D), jnp.float32) * s, 'film_b': jax.random.normal(ks[11], (6 * D,), jnp.float32) * s, 'tg_fc_w': jax.random.normal(ks[12], (4 * D, D), jnp.float32) * s, 'tg_fc_b': jax.random.normal(ks[13], (4 * D,), jnp.float32) * s, 'tg_out_w': jax.random.normal(ks[14], (D, 2 * D), jnp.float32) * s, 'tg_out_b': jax.random.normal(ks[15], (D,), jnp.float32) * s}
        return inp
    _L2_cond_all = _L2_cond_setup()
    _L2_cond_in = {k: v for k, v in _L2_cond_all.items() if k in ('in_proj_w', 'in_proj_b', 'out_w', 'out_b', 'mlp_w1', 'mlp_b1', 'mlp_w2', 'mlp_b2', 'film_w', 'film_b', 'tg_fc_w', 'tg_fc_b', 'tg_out_w', 'tg_out_b')}
    del _L2_cond_all

    def _L3_cond_setup():
        import jax, jax.numpy as jnp
        import numpy as np
        FEAT = 256
        ADA = 256
        INTER = 256
        RANK = 8
        EPS = 1e-05

        def _layernorm(a, g, b):
            mu = jnp.mean(a, axis=-1, keepdims=True)
            var = jnp.mean(jnp.square(a - mu), axis=-1, keepdims=True)
            return (a - mu) * jax.lax.rsqrt(var + EPS) * g + b
        key = jax.random.key(seed)
        ks = jax.random.split(key, 6)
        B, T = (16, 256)
        x = jax.random.normal(ks[0], (B, T, FEAT), dtype=jnp.float32)
        ada_emb = jax.random.normal(ks[1], (B, ADA), dtype=jnp.float32)
        W1 = jax.random.normal(ks[2], (ADA, INTER), dtype=jnp.float32) / np.sqrt(ADA)
        b1 = jnp.zeros((INTER,), dtype=jnp.float32)
        W2 = jax.random.normal(ks[3], (INTER, FEAT * RANK * 4), dtype=jnp.float32) * (0.1 / np.sqrt(INTER))
        b2 = jnp.zeros((FEAT * RANK * 4,), dtype=jnp.float32)
        ln_g = jnp.ones((ADA,), dtype=jnp.float32)
        ln_b = jnp.zeros((ADA,), dtype=jnp.float32)
        return {'x': x, 'ada_emb': ada_emb, 'ln_g': ln_g, 'ln_b': ln_b, 'W1': W1, 'b1': b1, 'W2': W2, 'b2': b2}
    _L3_cond_all = _L3_cond_setup()
    _L3_cond_in = {k: v for k, v in _L3_cond_all.items() if k in ('ln_g', 'ln_b', 'W1', 'b1', 'W2', 'b2')}
    del _L3_cond_all
    return {'x': x, 'cond_1024': cond_1024, 'fside_BxSx3_0': fside_BxSx3_0, 'L0_cond_W_mod': _L0_cond_in['W_mod'], 'L0_cond_b_mod': _L0_cond_in['b_mod'], 'L0_cond_W_qkv': _L0_cond_in['W_qkv'], 'L0_cond_W_out': _L0_cond_in['W_out'], 'L0_cond_b_out': _L0_cond_in['b_out'], 'L0_cond_W1': _L0_cond_in['W1'], 'L0_cond_b1': _L0_cond_in['b1'], 'L0_cond_W2': _L0_cond_in['W2'], 'L0_cond_b2': _L0_cond_in['b2'], 'L1_cond_norm1_w': _L1_cond_in['norm1_w'], 'L1_cond_qkv_w': _L1_cond_in['qkv_w'], 'L1_cond_q_norm_w': _L1_cond_in['q_norm_w'], 'L1_cond_k_norm_w': _L1_cond_in['k_norm_w'], 'L1_cond_proj_w': _L1_cond_in['proj_w'], 'L1_cond_proj_b': _L1_cond_in['proj_b'], 'L1_cond_norm2_w': _L1_cond_in['norm2_w'], 'L1_cond_w1': _L1_cond_in['w1'], 'L1_cond_w3': _L1_cond_in['w3'], 'L1_cond_w2': _L1_cond_in['w2'], 'L1_cond_ada_w': _L1_cond_in['ada_w'], 'L1_cond_ada_b': _L1_cond_in['ada_b'], 'L2_cond_in_proj_w': _L2_cond_in['in_proj_w'], 'L2_cond_in_proj_b': _L2_cond_in['in_proj_b'], 'L2_cond_out_w': _L2_cond_in['out_w'], 'L2_cond_out_b': _L2_cond_in['out_b'], 'L2_cond_mlp_w1': _L2_cond_in['mlp_w1'], 'L2_cond_mlp_b1': _L2_cond_in['mlp_b1'], 'L2_cond_mlp_w2': _L2_cond_in['mlp_w2'], 'L2_cond_mlp_b2': _L2_cond_in['mlp_b2'], 'L2_cond_film_w': _L2_cond_in['film_w'], 'L2_cond_film_b': _L2_cond_in['film_b'], 'L2_cond_tg_fc_w': _L2_cond_in['tg_fc_w'], 'L2_cond_tg_fc_b': _L2_cond_in['tg_fc_b'], 'L2_cond_tg_out_w': _L2_cond_in['tg_out_w'], 'L2_cond_tg_out_b': _L2_cond_in['tg_out_b'], 'L3_cond_ln_g': _L3_cond_in['ln_g'], 'L3_cond_ln_b': _L3_cond_in['ln_b'], 'L3_cond_W1': _L3_cond_in['W1'], 'L3_cond_b1': _L3_cond_in['b1'], 'L3_cond_W2': _L3_cond_in['W2'], 'L3_cond_b2': _L3_cond_in['b2']}

def reference(x, cond_1024, fside_BxSx3_0, L0_cond_W_mod, L0_cond_b_mod, L0_cond_W_qkv, L0_cond_W_out, L0_cond_b_out, L0_cond_W1, L0_cond_b1, L0_cond_W2, L0_cond_b2, L1_cond_norm1_w, L1_cond_qkv_w, L1_cond_q_norm_w, L1_cond_k_norm_w, L1_cond_proj_w, L1_cond_proj_b, L1_cond_norm2_w, L1_cond_w1, L1_cond_w3, L1_cond_w2, L1_cond_ada_w, L1_cond_ada_b, L2_cond_in_proj_w, L2_cond_in_proj_b, L2_cond_out_w, L2_cond_out_b, L2_cond_mlp_w1, L2_cond_mlp_b1, L2_cond_mlp_w2, L2_cond_mlp_b2, L2_cond_film_w, L2_cond_film_b, L2_cond_tg_fc_w, L2_cond_tg_fc_b, L2_cond_tg_out_w, L2_cond_tg_out_b, L3_cond_ln_g, L3_cond_ln_b, L3_cond_W1, L3_cond_b1, L3_cond_W2, L3_cond_b2):
    import jax
    import jax.numpy as jnp

    def _L0_cond_ref(x, c, W_mod, b_mod, W_qkv, W_out, b_out, W1, b1, W2, b2):
        import jax, jax.numpy as jnp
        import numpy as np
        B, T, DIM = (4, 256, 256)
        COND = 256
        HEADS, DH = (16, 64)
        INNER = HEADS * DH
        MLP = 1024
        EPS = 1e-05

        def _layernorm(x):
            mu = jnp.mean(x, axis=-1, keepdims=True)
            var = jnp.mean(jnp.square(x - mu), axis=-1, keepdims=True)
            return (x - mu) * jax.lax.rsqrt(var + EPS)

        def _modulate(x, shift, scale):
            return x * (1.0 + scale) + shift

        def _attention(x, W_qkv, W_out, b_out):
            Bq, Tq, _ = x.shape
            qkv = x @ W_qkv
            q, k, v = jnp.split(qkv, 3, axis=-1)
            q = q.reshape(Bq, Tq, HEADS, DH)
            k = k.reshape(Bq, Tq, HEADS, DH)
            v = v.reshape(Bq, Tq, HEADS, DH)
            scale = DH ** (-0.5)
            attn = jnp.einsum('bqhd,bkhd->bhqk', q, k) * scale
            attn = jax.nn.softmax(attn, axis=-1)
            out = jnp.einsum('bhqk,bkhd->bqhd', attn, v).reshape(Bq, Tq, INNER)
            return out @ W_out + b_out

        def _ff(x, W1, b1, W2, b2):
            return jax.nn.gelu(x @ W1 + b1, approximate=False) @ W2 + b2
        mod = jax.nn.silu(c) @ W_mod + b_mod
        sh_msa, sc_msa, g_msa, sh_mlp, sc_mlp, g_mlp = jnp.split(mod, 6, axis=-1)
        x = x + g_msa * _attention(_modulate(_layernorm(x), sh_msa, sc_msa), W_qkv, W_out, b_out)
        x = x + g_mlp * _ff(_modulate(_layernorm(x), sh_mlp, sc_mlp), W1, b1, W2, b2)
        return x

    def _L1_cond_ref(x, c, positions, norm1_w, qkv_w, q_norm_w, k_norm_w, proj_w, proj_b, norm2_w, w1, w3, w2, ada_w, ada_b):
        import jax, jax.numpy as jnp
        import numpy as np
        HID = 256
        HEADS = 16
        HEAD_DIM = HID // HEADS
        ROPE_DIM = HEAD_DIM // 6 * 6
        HALF = ROPE_DIM // 3 // 2
        SWIGLU_HID = int(2 * (HID * 4) / 3)
        EPS = 1e-06
        THETA = 10000.0

        def rmsnorm(x, w, eps=EPS):
            xf = x.astype(jnp.float32)
            v = jnp.mean(xf * xf, axis=-1, keepdims=True)
            return w * (xf * jax.lax.rsqrt(v + eps)).astype(x.dtype)

        def modulate(x, shift, scale):
            return x * (1.0 + scale) + shift

        def rope_freqs():
            return 1.0 / THETA ** (jnp.arange(HALF, dtype=jnp.float32) / HALF)

        def apply_rope3d(q, k, positions):
            freqs = rope_freqs()
            ang = positions[..., :, None] * freqs
            ang = ang.reshape(ang.shape[0], ang.shape[1], -1)
            cos = jnp.cos(ang)[:, :, None, :]
            sin = jnp.sin(ang)[:, :, None, :]

            def rot(t):
                B, N, H, D = t.shape
                tr = t.reshape(B, N, H, D // 2, 2)
                t0, t1 = (tr[..., 0], tr[..., 1])
                out = jnp.stack([t0 * cos - t1 * sin, t0 * sin + t1 * cos], axis=-1)
                return out.reshape(B, N, H, D)
            return (rot(q), rot(k))
        B, N, C = x.shape
        H, D = (HEADS, HEAD_DIM)
        mod = (c @ ada_w.T + ada_b)[:, None, :]
        sh_msa, sc_msa, g_msa, sh_mlp, sc_mlp, g_mlp = jnp.split(mod, 6, axis=-1)
        h = modulate(rmsnorm(x, norm1_w), sh_msa, sc_msa)
        qkv = (h @ qkv_w.T).reshape(B, N, 3, H, D)
        q, k, v = (qkv[:, :, 0], qkv[:, :, 1], qkv[:, :, 2])
        q = rmsnorm(q, q_norm_w)
        k = rmsnorm(k, k_norm_w)
        q_r, k_r = apply_rope3d(q[..., :ROPE_DIM], k[..., :ROPE_DIM], positions)
        q = jnp.concatenate([q_r, q[..., ROPE_DIM:]], axis=-1)
        k = jnp.concatenate([k_r, k[..., ROPE_DIM:]], axis=-1)
        scale = D ** (-0.5)
        attn = jnp.einsum('bnhd,bmhd->bhnm', q, k) * scale
        attn = jax.nn.softmax(attn, axis=-1)
        o = jnp.einsum('bhnm,bmhd->bnhd', attn, v).reshape(B, N, C)
        o = o @ proj_w.T + proj_b
        x = x + g_msa * o
        h2 = modulate(rmsnorm(x, norm2_w), sh_mlp, sc_mlp)
        ff = jax.nn.silu(h2 @ w1.T) * (h2 @ w3.T) @ w2.T
        x = x + g_mlp * ff
        return x

    def _L2_cond_ref(x, cond, in_proj_w, in_proj_b, out_w, out_b, mlp_w1, mlp_b1, mlp_w2, mlp_b2, film_w, film_b, tg_fc_w, tg_fc_b, tg_out_w, tg_out_b):
        import jax, jax.numpy as jnp
        import numpy as np
        DIM = 256
        HEADS = 16
        DH = DIM // HEADS
        EPS = 1e-06

        def _ln(x):
            mu = jnp.mean(x, axis=-1, keepdims=True)
            var = jnp.mean((x - mu) ** 2, axis=-1, keepdims=True)
            return (x - mu) / jnp.sqrt(var + EPS)

        def _rotate_half(x):
            x1, x2 = (x[..., :x.shape[-1] // 2], x[..., x.shape[-1] // 2:])
            return jnp.concatenate((-x2, x1), axis=-1)
        B, T, D = x.shape
        H, Dh = (HEADS, D // HEADS)
        film = (jax.nn.silu(cond) @ film_w.T + film_b)[:, None, :]
        shift_msa, scale_msa, gate_msa, shift_mlp, scale_mlp, gate_mlp = jnp.split(film, 6, axis=-1)
        h = _ln(x) * (1.0 + scale_msa) + shift_msa
        qw, kw, vw = jnp.split(in_proj_w, 3, axis=0)
        qb, kb, vb = jnp.split(in_proj_b, 3, axis=0)
        q = (h @ qw.T + qb).reshape(B, T, H, Dh).transpose(0, 2, 1, 3)
        k = (h @ kw.T + kb).reshape(B, T, H, Dh).transpose(0, 2, 1, 3)
        v = (h @ vw.T + vb).reshape(B, T, H, Dh).transpose(0, 2, 1, 3)
        inv_freq = 1.0 / 10000.0 ** (jnp.arange(0, Dh, 2, dtype=jnp.float32) / Dh)
        freqs = jnp.arange(T, dtype=jnp.float32)[:, None] * inv_freq[None, :]
        angles = jnp.concatenate((freqs, freqs), axis=-1)
        cos, sin = (jnp.cos(angles)[None, None], jnp.sin(angles)[None, None])
        q = q * cos + _rotate_half(q) * sin
        k = k * cos + _rotate_half(k) * sin
        scores = jnp.einsum('bhtd,bhsd->bhts', q, k) / jnp.sqrt(jnp.float32(Dh))
        attn = jax.nn.softmax(scores, axis=-1)
        y = jnp.einsum('bhts,bhsd->bhtd', attn, v)
        y = y.transpose(0, 2, 1, 3).reshape(B, T, D)
        attn_out = y @ out_w.T + out_b
        x = x + gate_msa * attn_out
        h = _ln(x) * (1.0 + scale_mlp) + shift_mlp
        mlp_out = jax.nn.gelu(h @ mlp_w1.T + mlp_b1, approximate=False) @ mlp_w2.T + mlp_b2
        x = x + gate_mlp * mlp_out
        vg = x @ tg_fc_w.T + tg_fc_b
        v_, g_ = jnp.split(vg, 2, axis=-1)
        x = x + jax.nn.gelu(v_, approximate=False) * jnp.tanh(g_) @ tg_out_w.T + tg_out_b
        return x

    def _L3_cond_ref(x, ada_emb, ln_g, ln_b, W1, b1, W2, b2):
        import jax, jax.numpy as jnp
        import numpy as np
        FEAT = 256
        ADA = 256
        INTER = 256
        RANK = 8
        EPS = 1e-05

        def _layernorm(a, g, b):
            mu = jnp.mean(a, axis=-1, keepdims=True)
            var = jnp.mean(jnp.square(a - mu), axis=-1, keepdims=True)
            return (a - mu) * jax.lax.rsqrt(var + EPS) * g + b
        B, T, D = x.shape
        h = jax.nn.gelu(_layernorm(ada_emb, ln_g, ln_b) @ W1 + b1, approximate=False)
        w = h @ W2 + b2
        a1, bb1, a2, bb2 = jnp.split(w, 4, axis=-1)
        a1 = a1.reshape(B, D, RANK)
        bb1 = bb1.reshape(B, D, RANK)
        a2 = a2.reshape(B, D, RANK)
        bb2 = bb2.reshape(B, D, RANK)
        y = jnp.einsum('btd,bdr->btr', x, a1)
        y = jnp.einsum('btr,bdr->btd', y, bb1)
        y = jax.nn.gelu(y, approximate=False)
        y = jnp.einsum('btd,bdr->btr', y, a2)
        y = jnp.einsum('btr,bdr->btd', y, bb2)
        return y + x
    x = _L0_cond_ref(x, cond_1024[:, None, :], L0_cond_W_mod, L0_cond_b_mod, L0_cond_W_qkv, L0_cond_W_out, L0_cond_b_out, L0_cond_W1, L0_cond_b1, L0_cond_W2, L0_cond_b2)
    x = _L1_cond_ref(x, cond_1024, fside_BxSx3_0, L1_cond_norm1_w, L1_cond_qkv_w, L1_cond_q_norm_w, L1_cond_k_norm_w, L1_cond_proj_w, L1_cond_proj_b, L1_cond_norm2_w, L1_cond_w1, L1_cond_w3, L1_cond_w2, L1_cond_ada_w, L1_cond_ada_b)
    x = _L2_cond_ref(x, cond_1024, L2_cond_in_proj_w, L2_cond_in_proj_b, L2_cond_out_w, L2_cond_out_b, L2_cond_mlp_w1, L2_cond_mlp_b1, L2_cond_mlp_w2, L2_cond_mlp_b2, L2_cond_film_w, L2_cond_film_b, L2_cond_tg_fc_w, L2_cond_tg_fc_b, L2_cond_tg_out_w, L2_cond_tg_out_b)
    x = _L3_cond_ref(x, cond_1024, L3_cond_ln_g, L3_cond_ln_b, L3_cond_W1, L3_cond_b1, L3_cond_W2, L3_cond_b2)
    return x

_drawn_inputs = setup_inputs


def setup_inputs(seed=0):
    import zlib

    import numpy as np

    out = dict(_drawn_inputs(seed))
    spreads = {'L1_cond_norm1_w': (1.0, 0.6),
     'L1_cond_q_norm_w': (1.0, 0.6),
     'L1_cond_k_norm_w': (1.0, 0.6),
     'L1_cond_proj_b': (0.0, 0.1),
     'L1_cond_norm2_w': (1.0, 0.6),
     'L1_cond_ada_b': (0.0, 0.688),
     'L3_cond_ln_g': (1.0, 0.2),
     'L3_cond_ln_b': (0.0, 0.276),
     'L3_cond_b1': (0.0, 0.1),
     'L3_cond_b2': (0.0, 0.1)}
    factors = {'fside_BxSx3_0': 8.0,
     'L0_cond_b_mod': 8.0,
     'L0_cond_W_qkv': 5.769,
     'L0_cond_W_out': 5.766,
     'L0_cond_b_out': 8.0,
     'L0_cond_b1': 24.599,
     'L0_cond_b2': 8.0,
     'L1_cond_qkv_w': 3.876,
     'L1_cond_proj_w': 3.883,
     'L1_cond_w1': 4.546,
     'L1_cond_w3': 4.487,
     'L1_cond_w2': 4.479,
     'L2_cond_in_proj_w': 8.0,
     'L2_cond_in_proj_b': 8.0,
     'L2_cond_out_w': 8.0,
     'L2_cond_out_b': 64.0,
     'L2_cond_mlp_b1': 64.0,
     'L2_cond_mlp_b2': 64.0,
     'L2_cond_film_b': 8.0,
     'L2_cond_tg_fc_b': 51.238,
     'L2_cond_tg_out_b': 24.544,
     'L2_cond_mlp_w1': 8.0,
     'L2_cond_mlp_w2': 8.0}
    for name, (base, spread) in spreads.items():
        noise = np.random.default_rng([zlib.crc32(name.encode()), seed]).standard_normal(out[name].shape)
        drawn = base * np.exp(spread * noise) if base else spread * noise
        out[name] = jnp.asarray(drawn.astype(out[name].dtype))
    for name, factor in factors.items():
        out[name] = (out[name] * factor).astype(out[name].dtype)
    return out
```

```python
import numpy as np
import concourse.bass as bass
from concourse import mybir
from contextlib import ExitStack

F32 = mybir.dt.float32
F32R = mybir.dt.float32r
ACT = mybir.ActivationFunctionType
ALU = mybir.AluOpType
AXX = mybir.AxisListType.X

P = 128
B, T, D = 64, 64, 256
N = B * T
DH = D // P
CH = 512
NCH = N // CH
CB = CH // T
TL = CH // P
NT = N // P
H = 16
PAIRS = H // 2
DH0 = 64
DH1 = 16
MLP = 1024
SWI = 682
SWIP = 768
RANK = 8
GB = P // RANK
CREDIT = 2

SH_A, SC_A, G_A, SH_M, SC_M, G_M = range(6)


class Count:

    def __init__(self, handle):
        self.h, self.base = handle, CREDIT

    def at(self, n):
        return n + self.base

    def passed(self, n):
        self.base += n


def cond_stack_kernel(nc, io):
    ctx = ExitStack()
    with ctx:
        def sb(name, shape, dt=F32, scope=ctx):
            return scope.enter_context(nc.sbuf_tensor(name, shape, dt))

        def pb(name, shape, dt=F32):
            return ctx.enter_context(nc.psum_tensor(name, shape, dt))

        counts = []

        def count(name):
            c = Count(ctx.enter_context(nc.semaphore(name)))
            counts.append(c)
            return c

        X = sb("X", [P, DH, N])
        MOD = [sb(f"MOD{l}", [P, 6, DH, B]) for l in range(3)]
        ident = sb("ident", [P, P])
        mean_w = sb("mean_w", [P, P], F32R)
        hmask = sb("hmask", [P, 8])
        rope_c1 = sb("rope_c1", [P, NT, 12])
        rope_s1 = sb("rope_s1", [P, NT, 12])
        bias_cols = sb("bias_cols", [P, 34])
        BC = {"b_out0": 0, "b2_0": 2, "b_out1": 4, "b_out2": 6, "b2_2": 8, "b_tgo": 10, "b1_0": 12, "b1_2": 20, "zero": 28}
        tgb = sb("tgb", [P, 8])
        spare = sb("spare", [P, 2])


        BK = [pb(f"bank{i}", [P, 512]) for i in range(4)]
        S2 = pb("S2", [P, 2, 512])
        O2 = pb("O2", [P, 2, 512])

        f_xh, f_xl, f_mean, f_d, f_dd, f_sqh, f_sql, f_var, f_v, f_ln, f_rs = [
            count(n) for n in ("f_xh", "f_xl", "f_mean", "f_d", "f_dd", "f_sqh", "f_sql", "f_var", "f_v", "f_ln", "f_rs")]
        f_n1, f_n2, f_n3, f_n, f_m, f_h, f_hh, f_hl, h_done = [
            count(n) for n in ("f_n1", "f_n2", "f_n3", "f_n", "f_m", "f_h", "f_hh", "f_hl", "h_done")]
        out_ready, out_taken, x_added = count("out_ready"), count("out_taken"), count("x_added")
        w_in, w_hi, w_lo = count("w_in"), count("w_hi"), count("w_lo")
        d_in = count("d_in")
        w_st = [count("w_st0"), count("w_st1")]
        out_st = [count("out_st0"), count("out_st1")]
        q_ps, k_ps, v_ps = count("q_ps"), count("k_ps"), count("v_ps")
        q_sb, ka_sb, kd_sb, va_sb, vd_sb = [count(n) for n in ("q_sb", "ka_sb", "kd_sb", "va_sb", "vd_sb")]
        pj_free = [count("pj_free0"), count("pj_free1")]
        s_ready, s_max, s_sub, p_exp, p_sum, p_rec = [count(n) for n in ("s_ready", "s_max", "s_sub", "p_exp", "p_sum", "p_rec")]
        pt_ps, pt_sb, o_ps, o_sb, ot_ps, ot_hi, ot_lo = [
            count(n) for n in ("pt_ps", "pt_sb", "o_ps", "o_sb", "ot_ps", "ot_hi", "ot_lo")]
        a_ps, g_act, g_hi, g_lo, g_used, g_mul, g_act2 = [
            count(n) for n in ("a_ps", "g_act", "g_hi", "g_lo", "g_used", "g_mul", "g_act2")]
        t4_ps, sq_sb, ss_sum, ss_eps, ss_ln, ss_exp, ss_n1, ss_n2, ss_r = [
            count(n) for n in ("t4_ps", "sq_sb", "ss_sum", "ss_eps", "ss_ln", "ss_exp", "ss_n1", "ss_n2", "ss_r")]
        qk_n, qk_w, ra, rb, rc, tr_free0, tr_free1 = [
            count(n) for n in ("qk_n", "qk_w", "ra", "rb", "rc", "tr_free0", "tr_free1")]
        tr_free = [tr_free0, tr_free1]
        step_v, step_a, step_p = count("step_v"), count("step_a"), count("step_p")
        out_dma = count("out_dma")
        spare_done = count("spare_done")

        with nc.Block() as block:
            @block.sync
            def _(sp):
                for c in counts:
                    sp.sem_inc(c.h, CREDIT)

        def seq(eng, cnt):
            n = [0]

            def step(ins):
                ins.then_inc(cnt.h, 1)
                n[0] += 1
                eng.wait_ge(cnt.h, cnt.at(n[0]))
            step.n = n
            return step

        with ExitStack() as sc:
            ones_f = sb("ones_f", [P, P], scope=sc)
            cT = sb("cT", [P, DH, B], scope=sc)
            cS = sb("cS", [P, DH, B], scope=sc)
            wm = sb("wm", [P, 3, DH, 6 * D], scope=sc)
            bm = sb("bm", [P, 3, 12], scope=sc)
            n12 = sb("n12", [P, 2, DH], scope=sc)
            ang = sb("ang", [P, NT, 3, 2], scope=sc)
            pos = sb("pos", [P, NT, 3], scope=sc)
            an2 = sb("an2", [P, NT, 6], scope=sc)
            an3 = sb("an3", [P, NT, 6], scope=sc)
            ada = sb("ada", [B, D], scope=sc)
            ada2 = sb("ada2", [B, D], scope=sc)
            gB = sb("gB", [B, 2, D], scope=sc)
            st = sb("st", [B, 8], scope=sc)
            aT = sb("aT", [P, DH, B], scope=sc)
            hT = sb("hT", [P, DH, B], scope=sc)
            w1 = sb("w1", [P, DH, D], scope=sc)
            b1 = sb("b1", [P, DH], scope=sc)
            w2 = sb("w2", [P, 2, DH, 2 * D * RANK], scope=sc)
            b2c = sb("b2c", [P, 2, DH, RANK], scope=sc)
            b2r = sb("b2r", [B, 2, D * RANK], scope=sc)
            As = sb("As", [P, 2, DH, B, RANK], scope=sc)
            Bs = sb("Bs", [B, 2, D * RANK], scope=sc)

            with nc.Block() as block:
                small = [(cT[:], io["condT"].rearrange("(k p) b -> p k b", p=P)), (bm[:], io["b_mods"]), (n12[:], io["norm_w"]),
                         (ident[:], io["ident"]), (hmask[:], io["hmask"]), (pos[:], io["pos"]),
                         (ada[:], io["cond"]), (bias_cols[:], io["bias_cols"]), (tgb[:], io["tg_b"]),
                         (gB[:], io["ln_gb"].rearrange("(o a) d -> o a d", o=1).to_broadcast([B, 2, D])),
                         (b1[:], io["l3_b1"]), (b2c[:], io["l3_b2c"]),
                         (b2r[:], io["l3_b2r"].rearrange("(o a) n -> o a n", o=1).to_broadcast([B, 2, D * RANK])),
                         (w1[:], io["l3_w1"].rearrange("(k p) n -> p k n", p=P))]
                n_small = len(small)

                @block.sync
                def _(sp):
                    for dst, src in small:
                        sp.dma_start(dst, src).then_inc(d_in.h, 16)
                    for l in range(3):
                        for k in range(DH):
                            sp.dma_start(wm[:, l, k], io["w_mods"][l, k * P:(k + 1) * P, :]).then_inc(w_in.h, 16)
                    for q in range(2):
                        for k in range(DH):
                            sp.dma_start(w2[:, q, k], io["l3_w2"][k * P:(k + 1) * P, q * 4096:(q + 1) * 4096]).then_inc(w_hi.h, 16)
                    for k in range(DH):
                        for h in range(2):
                            sp.dma_start(X[:, k, h * 2048:(h + 1) * 2048],
                                         io["xT"][k * P:(k + 1) * P, h * 2048:(h + 1) * 2048]).then_inc(w_lo.h, 16)
                    sp.wait_ge(g_act.h, g_act.at(4))
                    for a in range(2):
                        sp.dma_start(io["scrA"][a], As[:, a].rearrange("p h b r -> p h (b r)")).then_inc(out_dma.h, 16)
                    sp.wait_ge(g_hi.h, g_hi.at(8))
                    for a in range(2):
                        sp.dma_start(io["scrB"][a], Bs[:, a, :]).then_inc(out_dma.h, 16)
                    sp.wait_ge(out_dma.h, out_dma.at(64))
                    sp.wait_ge(w_lo.h, w_lo.at(64))

                bk = [BK[0], BK[1], BK[2], BK[3]]

                @block.tensor
                def _(pe):
                    pe.wait_ge(d_in.h, d_in.at(16 * n_small))
                    for l in range(3):
                        pe.wait_ge(w_in.h, w_in.at(96))
                        if l == 0:
                            pe.wait_ge(q_sb.h, q_sb.at(1))
                        for h in range(2):
                            u = l * 2 + h
                            if u >= 2:
                                pe.wait_ge(k_ps.h, k_ps.at(u - 1))
                            for m in range(6 * h, 6 * h + 6):
                                for k in range(DH):
                                    last = nc.tensor.matmul(bk[u % 2][:, (m % 6) * B:(m % 6) * B + B],
                                                            wm[:, l, k, m * P:(m + 1) * P], (cT if l == 1 else cS)[:, k, :],
                                                            start=(k == 0), stop=(k == DH - 1))
                            last.then_inc(q_ps.h, 1)
                    pe.wait_ge(s_sub.h, s_sub.at(1))
                    for k in range(DH):
                        last = nc.tensor.transpose(BK[2][:, k * B:(k + 1) * B], ada2[:, k * P:(k + 1) * P], ident[0:B, 0:B])
                    last.then_inc(t4_ps.h, 1)
                    pe.wait_ge(pt_sb.h, pt_sb.at(1))
                    for m in range(DH):
                        for k in range(DH):
                            last = nc.tensor.matmul(BK[3][:, m * B:(m + 1) * B], w1[:, k, m * P:(m + 1) * P], aT[:, k, :],
                                                    start=(k == 0), stop=(k == DH - 1))
                    last.then_inc(o_ps.h, 1)
                    pe.wait_ge(o_sb.h, o_sb.at(1))
                    pe.wait_ge(k_ps.h, k_ps.at(6))
                    for q in range(2):
                        pe.wait_ge(w_hi.h, w_hi.at(64))
                        for h in range(DH):
                            u = q * 2 + h
                            if u >= 2:
                                pe.wait_ge(g_act.h, g_act.at(u - 1))
                            for r in range(RANK):
                                for k in range(DH):
                                    last = nc.tensor.matmul(BK[u % 2][:, r * B:(r + 1) * B],
                                                            w2[:, q, k, r * D + h * P:r * D + h * P + P], hT[:, k, :],
                                                            start=(k == 0), stop=(k == DH - 1))
                            last.then_inc(a_ps.h, 1)
                    for q in range(2):
                        for n in range(4):
                            u = q * 4 + n
                            if u >= 2:
                                pe.wait_ge(g_hi.h, g_hi.at(u - 1))
                            for k in range(DH):
                                last = nc.tensor.matmul(S2[0:B, u % 2, :], hT[:, k, :],
                                                        w2[:, q, k, 2048 + n * 512:2048 + (n + 1) * 512],
                                                        start=(k == 0), stop=(k == DH - 1))
                            last.then_inc(s_ready.h, 1)

                @block.scalar
                def _(act):
                    act.wait_ge(d_in.h, d_in.at(16 * n_small))
                    nc.scalar.activation(cS[:], cT[:], ACT.Silu).then_inc(q_sb.h, 1)
                    act.wait_ge(s_max.h, s_max.at(1))
                    nc.scalar.activation(st[:, 3:4], st[:, 2:3], ACT.Sqrt).then_inc(p_exp.h, 1)
                    act.wait_ge(qk_n.h, qk_n.at(1))
                    for i, sign in enumerate((-1.0, 1.0)):
                        nc.scalar.activation(rope_s1[:].rearrange("p t (a i) -> p t a i", i=2)[:, :, :, i], an2[:], ACT.Sin,
                                             scale=sign).then_inc(step_a.h, 1)
                    for i in range(2):
                        nc.scalar.activation(rope_c1[:].rearrange("p t (a i) -> p t a i", i=2)[:, :, :, i], an3[:], ACT.Sin,
                                             ).then_inc(step_a.h, 1)
                    act.wait_ge(t4_ps.h, t4_ps.at(1))
                    nc.scalar.activation(aT[:].rearrange("p k b -> p (k b)"), BK[2][:, 0:DH * B], ACT.Copy).then_inc(pt_sb.h, 1)
                    act.wait_ge(o_ps.h, o_ps.at(1))
                    for m in range(DH):
                        ins = nc.scalar.activation(hT[:, m, :], BK[3][:, m * B:(m + 1) * B], ACT.Gelu, bias=b1[:, m:m + 1])
                    ins.then_inc(o_sb.h, 1)

                @block.vector
                def _(dve):
                    step = seq(dve, step_v)
                    step(nc.vector.memset(ones_f[:], 1.0 / D))
                    nc.vector.tensor_copy(mean_w[:], ones_f[:]).then_inc(ka_sb.h, 1)
                    dve.wait_ge(d_in.h, d_in.at(16 * n_small))
                    step(nc.vector.tensor_reduce(st[:, 0:1], ada[:], AXX, ALU.add))
                    step(nc.vector.tensor_scalar(st[:, 0:1], st[:, 0:1], 1.0 / D, None, ALU.mult))
                    step(nc.vector.tensor_scalar(ada2[:], ada[:], st[:, 0:1], None, ALU.subtract))
                    step(nc.vector.tensor_tensor(ada[:], ada2[:], ada2[:], ALU.mult))
                    step(nc.vector.tensor_reduce(st[:, 1:2], ada[:], AXX, ALU.add))
                    nc.vector.tensor_scalar(st[:, 2:3], st[:, 1:2], 1.0 / D, 1e-5, ALU.mult, ALU.add).then_inc(s_max.h, 1)
                    for f, w in enumerate(io["freqs"]):
                        step(nc.vector.tensor_scalar(ang[:, :, :, f], pos[:], w, None, ALU.mult))
                    an = ang[:].rearrange("p t a f -> p t (a f)")
                    step(nc.vector.tensor_scalar(an2[:], an, float(np.float32(1 / (2 * np.pi))), 12582912.0, ALU.mult, ALU.add))
                    step(nc.vector.tensor_scalar(an2[:], an2[:], 12582912.0, None, ALU.subtract))
                    for part in io["two_pi"]:
                        step(nc.vector.scalar_tensor_tensor(out=an.rearrange("p t a -> p (t a)"), in0=an2[:].rearrange("p t a -> p (t a)"),
                                                            scalar=-part, in1=an.rearrange("p t a -> p (t a)"), op0=ALU.mult, op1=ALU.add))
                    lim = 3.1415925
                    step(nc.vector.tensor_scalar(an2[:], an, lim, -lim, ALU.min, ALU.max))
                    step(nc.vector.tensor_scalar(an3[:], an2[:], -1.0, None, ALU.mult))
                    step(nc.vector.tensor_tensor(an3[:], an3[:], an2[:], ALU.max))
                    nc.vector.tensor_scalar(an3[:], an3[:], -1.0, float(np.float32(np.pi / 2)), ALU.mult, ALU.add).then_inc(qk_n.h, 1)
                    for l in range(3):
                        for h in range(2):
                            u = l * 2 + h
                            dve.wait_ge(q_ps.h, q_ps.at(u + 1))
                            nc.vector.tensor_tensor(
                                MOD[l][:, 3 * h:3 * h + 3].rearrange("p a k b -> p (a k) b"),
                                bk[u % 2][:, 0:6 * B].rearrange("p (m b) -> p m b", b=B),
                                bm[:, l, 6 * h:6 * h + 6].unsqueeze(2).to_broadcast([P, 6, B]), ALU.add).then_inc(k_ps.h, 1)
                            dve.wait_ge(k_ps.h, k_ps.at(u + 1))
                            i = SC_A if h == 0 else SC_M
                            if l == 1:
                                for k in range(DH):
                                    step(nc.vector.tensor_scalar(MOD[l][:, i, k], MOD[l][:, i, k], 1.0, n12[:, h, k:k + 1], ALU.add, ALU.mult))
                            else:
                                step(nc.vector.tensor_scalar(MOD[l][:, i], MOD[l][:, i], 1.0, None, ALU.add))
                    dve.wait_ge(p_exp.h, p_exp.at(1))
                    step(nc.vector.reciprocal(st[:, 4:5], st[:, 3:4]))
                    step(nc.vector.scalar_tensor_tensor(out=ada[:], in0=ada2[:], scalar=st[:, 4:5], in1=gB[:, 0], op0=ALU.mult, op1=ALU.mult))
                    nc.vector.tensor_tensor(ada2[:], ada[:], gB[:, 1], ALU.add).then_inc(s_sub.h, 1)
                    for q in range(2):
                        for h in range(DH):
                            u = q * 2 + h
                            dve.wait_ge(a_ps.h, a_ps.at(u + 1))
                            nc.vector.tensor_tensor(
                                As[:, q, h].rearrange("p b r -> p r b"), BK[u % 2][:].rearrange("p (r b) -> p r b", b=B),
                                b2c[:, q, h].unsqueeze(2).to_broadcast([P, RANK, B]), ALU.add).then_inc(g_act.h, 1)
                    for q in range(2):
                        for n in range(4):
                            u = q * 4 + n
                            dve.wait_ge(s_ready.h, s_ready.at(u + 1))
                            nc.vector.tensor_tensor(Bs[:, q, n * 512:(n + 1) * 512], S2[0:B, u % 2, :],
                                                    b2r[:, q, n * 512:(n + 1) * 512], ALU.add).then_inc(g_hi.h, 1)
                    step_v.pending = step.n[0]

            d_in.passed(16 * n_small); w_in.passed(96); w_hi.passed(64); w_lo.passed(64)
            q_ps.passed(6); t4_ps.passed(1); o_ps.passed(1); a_ps.passed(4); s_ready.passed(8)
            q_sb.passed(1); p_exp.passed(1); step_a.passed(4); pt_sb.passed(1); o_sb.passed(1)
            step_v.passed(step_v.pending); ka_sb.passed(1); s_max.passed(1); qk_n.passed(1); k_ps.passed(6)
            s_sub.passed(1); g_act.passed(4); g_hi.passed(8); out_dma.passed(64)

        def tok(c):
            return bass.ds(c * CH, CH)

        def load_split(sp_list, scope):
            big = max(src.shape[1] for src, _, _ in sp_list)
            stage = [sb(f"stage{i}_{nc.next_id()}", [P, big], scope=scope) for i in range(2)]
            n = len(sp_list)

            def sync(sp):
                for i, (src, _, _) in enumerate(sp_list):
                    if i >= 2:
                        sp.wait_ge(w_lo.h, w_lo.at(i - 1))
                    sp.dma_start(stage[i % 2][:, 0:src.shape[1]], src).then_inc(w_st[i % 2].h, 16)

            def scalar(act):
                for i, (src, hi, _) in enumerate(sp_list):
                    act.wait_ge(w_st[i % 2].h, w_st[i % 2].at(16 * (i // 2 + 1)))
                    nc.scalar.activation(hi, stage[i % 2][:, 0:src.shape[1]], ACT.Copy).then_inc(w_hi.h, 1)

            def vector(dve):
                for i, (src, hi, lo) in enumerate(sp_list):
                    dve.wait_ge(w_hi.h, w_hi.at(i + 1))
                    nc.vector.tensor_tensor(lo, stage[i % 2][:, 0:src.shape[1]], hi.bitcast(F32), ALU.subtract).then_inc(w_lo.h, 1)

            def passed():
                w_st[0].passed(16 * ((n + 1) // 2)); w_st[1].passed(16 * (n // 2)); w_hi.passed(n); w_lo.passed(n)
            return sync, scalar, vector, n, passed

        class Front:

            def __init__(self, scope, l, i_sh, i_sc, centred, eps, mean_bank, var_bank, free_mean, free_var, h_free, keep_h=True):
                tag = f"{nc.next_id()}"
                self.l, self.i_sh, self.i_sc, self.centred, self.eps = l, i_sh, i_sc, centred, eps
                self.mean_bank, self.var_bank, self.free_mean, self.free_var, self.h_free = mean_bank, var_bank, free_mean, free_var, h_free
                self.FA = sb("FA" + tag, [P, DH, CH], F32R, scope)
                self.FB = sb("FB" + tag, [P, DH, CH], F32R, scope)
                self.Dv = sb("Dv" + tag, [P, DH, CH], F32, scope)
                self.Tm = sb("Tm" + tag, [P, DH, CH], F32, scope)
                self.V1, self.V2, self.V3 = [sb(f"V{i}" + tag, [P, CH], F32, scope) for i in range(3)]
                self.H32 = [sb(f"H32_{i}" + tag, [P, DH, CH], F32, scope) for i in range(2 if keep_h else 1)]
                self.HH = [sb(f"HH_{i}" + tag, [P, DH, CH], F32R, scope) for i in range(2)]
                self.HL = [sb(f"HL_{i}" + tag, [P, DH, CH], F32R, scope) for i in range(2)]

            def h32(self, p):
                return self.H32[p % len(self.H32)]

            def _by_batch(self, i):
                return MOD[self.l][:, i]

            def act_xh(self, act, c):
                if self.centred:
                    act.wait_ge(f_var.h, f_var.at(c))
                    nc.scalar.activation(self.FA[:], X[:, :, tok(c)], ACT.Copy).then_inc(f_xh.h, 1)

            def act_sq(self, act, c):
                act.wait_ge(f_dd.h, f_dd.at(c + 1))
                if self.centred:
                    act.wait_ge(f_mean.h, f_mean.at(c + 1))
                else:
                    act.wait_ge(f_var.h, f_var.at(c))
                nc.scalar.activation(self.FA[:], self.Tm[:], ACT.Copy).then_inc(f_sqh.h, 1)

            def act_rstd(self, act, c):
                act.wait_ge(f_v.h, f_v.at(c + 1))
                nc.scalar.activation(self.V2[:], self.V1[:], ACT.Ln).then_inc(f_ln.h, 1)
                act.wait_ge(f_ln.h, f_ln.at(c + 1))
                nc.scalar.activation(self.V2[:], self.V2[:], ACT.Exp, scale=-0.5).then_inc(f_rs.h, 1)

            def act_hh(self, act, c, p):
                act.wait_ge(f_h.h, f_h.at(c + 1))
                nc.scalar.activation(self.HH[p][:], self.h32(p)[:], ACT.Copy).then_inc(f_hh.h, 1)

            def pool_xl(self, pool, c):
                if self.centred:
                    pool.wait_ge(f_xh.h, f_xh.at(c + 1))
                    nc.gpsimd.tensor_tensor(self.FB[:], X[:, :, tok(c)], self.FA[:].bitcast(F32), ALU.subtract).then_inc(f_xl.h, 1)

            def pool_sq(self, pool, c):
                pool.wait_ge(f_h.h, f_h.at(c))
                if self.centred:
                    pool.wait_ge(f_d.h, f_d.at(c + 1))
                    nc.gpsimd.tensor_tensor(self.Tm[:], self.Dv[:], self.Dv[:], ALU.mult).then_inc(f_dd.h, 1)
                else:
                    nc.gpsimd.tensor_tensor(self.Tm[:], X[:, :, tok(c)], X[:, :, tok(c)], ALU.mult).then_inc(f_dd.h, 1)
                pool.wait_ge(f_dd.h, f_dd.at(c + 1))
                pool.wait_ge(f_sqh.h, f_sqh.at(c + 1))
                nc.gpsimd.tensor_tensor(self.FB[:], self.Tm[:], self.FA[:].bitcast(F32), ALU.subtract).then_inc(f_sql.h, 1)

            def pool_scale(self, pool, c):
                pool.wait_ge(f_n.h, f_n.at(c + 1))
                pool.wait_ge(f_sql.h, f_sql.at(c + 1))
                for k in range(DH):
                    m = MOD[self.l][:, self.i_sc, k, bass.ds(c * CB, CB)].unsqueeze(2).to_broadcast([P, CB, T])
                    nc.gpsimd.tensor_tensor(self.Tm[:, k].rearrange("p (b t) -> p b t", t=T),
                                            self.Dv[:, k].rearrange("p (b t) -> p b t", t=T), m, ALU.mult).then_inc(f_m.h, 1)

            def _sum(self, bank):
                ops = [(part, k) for part in (self.FB, self.FA) for k in range(DH)]
                for i, (part, k) in enumerate(ops):
                    last = nc.tensor.matmul(bank, mean_w[:], part[:, k], start=(i == 0), stop=(i == len(ops) - 1))
                return last

            def pe_mean(self, pe, c):
                if self.centred:
                    pe.wait_ge(f_xl.h, f_xl.at(c + 1))
                    self.free_mean(pe, c)
                    self._sum(self.mean_bank).then_inc(f_mean.h, 1)

            def pe_var(self, pe, c):
                pe.wait_ge(f_sql.h, f_sql.at(c + 1))
                self.free_var(pe, c)
                self._sum(self.var_bank).then_inc(f_var.h, 1)

            def dve_d(self, dve, c):
                if self.centred:
                    dve.wait_ge(f_mean.h, f_mean.at(c + 1))
                    dve.wait_ge(f_m.h, f_m.at(2 * c))
                    nc.vector.tensor_tensor(self.Dv[:], X[:, :, tok(c)], self.mean_bank.unsqueeze(1).to_broadcast([P, DH, CH]),
                                            ALU.subtract).then_inc(f_d.h, 1)

            def dve_v(self, dve, c):
                dve.wait_ge(f_var.h, f_var.at(c + 1))
                nc.vector.tensor_scalar(self.V1[:], self.var_bank, self.eps, None, ALU.add).then_inc(f_v.h, 1)

            def dve_norm(self, dve, c):
                dve.wait_ge(f_rs.h, f_rs.at(c + 1))
                nc.vector.scalar_tensor_tensor(out=self.V3[:], in0=self.V2[:], scalar=-0.5, in1=self.V2[:], op0=ALU.mult, op1=ALU.mult).then_inc(f_n1.h, 1)
                dve.wait_ge(f_n1.h, f_n1.at(c + 1))
                nc.vector.tensor_tensor(self.V3[:], self.V3[:], self.V1[:], ALU.mult).then_inc(f_n2.h, 1)
                dve.wait_ge(f_n2.h, f_n2.at(c + 1))
                nc.vector.scalar_tensor_tensor(out=self.V3[:], in0=self.V3[:], scalar=1.5, in1=self.V2[:], op0=ALU.add, op1=ALU.mult).then_inc(f_n3.h, 1)
                dve.wait_ge(f_n3.h, f_n3.at(c + 1))
                r = self.V3[:].unsqueeze(1).to_broadcast([P, DH, CH])
                if self.centred:
                    nc.vector.tensor_tensor(self.Dv[:], self.Dv[:], r, ALU.mult).then_inc(f_n.h, 1)
                else:
                    dve.wait_ge(f_m.h, f_m.at(2 * c))
                    nc.vector.tensor_tensor(self.Dv[:], X[:, :, tok(c)], r, ALU.mult).then_inc(f_n.h, 1)

            def dve_h(self, dve, c, p):
                dve.wait_ge(f_m.h, f_m.at(2 * c + 2))
                self.h_free(dve, c)
                h = self.h32(p)
                for k in range(DH):
                    m = MOD[self.l][:, self.i_sh, k, bass.ds(c * CB, CB)].unsqueeze(2).to_broadcast([P, CB, T])
                    last = nc.vector.tensor_tensor(h[:, k].rearrange("p (b t) -> p b t", t=T),
                                                   self.Tm[:, k].rearrange("p (b t) -> p b t", t=T), m, ALU.add)
                last.then_inc(f_h.h, 1)

            def dve_hl(self, dve, c, p):
                dve.wait_ge(f_hh.h, f_hh.at(c + 1))
                nc.vector.tensor_tensor(self.HL[p][:], self.h32(p)[:], self.HH[p][:].bitcast(F32), ALU.subtract).then_inc(f_hl.h, 1)

            def passed(self):
                if self.centred:
                    for c in (f_xh, f_xl, f_mean, f_d):
                        c.passed(NCH)
                for c in (f_dd, f_sqh, f_sql, f_var, f_v, f_ln, f_rs, f_n1, f_n2, f_n3, f_n, f_h, f_hh, f_hl):
                    c.passed(NCH)
                f_m.passed(2 * NCH)

        def chunks(eng, body):
            with eng.Fori(0, NCH // 2 - 1) as j:
                body(2 * j, 0, True)
                body(2 * j + 1, 1, True)
            body(NCH - 2, 0, True)
            body(NCH - 1, 1, False)

        def split3(out, w_hi_ap, w_lo_ap, x_hi, x_lo, first, last):
            nc.tensor.matmul(out, w_lo_ap, x_hi, start=first, stop=False)
            nc.tensor.matmul(out, w_hi_ap, x_lo, start=False, stop=False)
            return nc.tensor.matmul(out, w_hi_ap, x_hi, start=False, stop=last)

        def residual_dve(dve, c, l, i_g, bcol, RT, bank):
            dve.wait_ge(x_added.h, x_added.at(c))
            for m in range(DH):
                nc.vector.scalar_tensor_tensor(
                    out=RT[:, m].rearrange("p (b t) -> p b t", t=T), in0=bank[:, m].rearrange("p (b t) -> p b t", t=T),
                    scalar=bias_cols[:, bcol + m:bcol + m + 1],
                    in1=MOD[l][:, i_g, m, bass.ds(c * CB, CB)].unsqueeze(2).to_broadcast([P, CB, T]),
                    op0=ALU.add, op1=ALU.mult).then_inc(out_taken.h, 1)

        def residual_pool(pool, c, RT):
            pool.wait_ge(out_taken.h, out_taken.at(2 * c + 2))
            nc.gpsimd.tensor_tensor(spare[:, 0:1], RT[:, 0, 0:1], RT[:, 1, 0:1], ALU.add).then_inc(spare_done.h, 1)
            pool.wait_ge(spare_done.h, spare_done.at(1))
            nc.gpsimd.tensor_tensor(X[:, :, tok(c)], X[:, :, tok(c)], RT[:], ALU.add).then_inc(x_added.h, 1)

        def attention0():
            with ExitStack() as sc:
                WQK = [sb(f"WQK0_{i}", [P, DH, 2 * H * DH0], F32R, sc) for i in range(2)]
                WO = [sb(f"WO0_{i}", [P, PAIRS, D], F32R, sc) for i in range(2)]
                WV = sb("WV0", [P, DH, 2, PAIRS, DH0], scope=sc)
                TRA, TRB, S, O = BK[2], BK[3], S2[:, 0, :], S2[:, 1, :]
                fr = Front(sc, 0, SH_A, SC_A, True, 1e-5, TRB[:], TRB[:],
                           lambda pe, c: None, lambda pe, c: None,
                           lambda e, c: None if isinstance(c, int) and c < 2 else e.wait_ge(k_ps.h, k_ps.at(8 * c - 8)))
                Q = [sb(f"Q0_{i}", [P, CH], scope=sc) for i in range(2)]
                KB = [sb(f"KB0_{i}", [P, CB, 2, T], scope=sc) for i in range(2)]
                VB = [sb(f"VB0_{i}", [P, CB, 2, 2, DH0], scope=sc) for i in range(2)]
                SP = [sb(f"SP0_{i}", [P, TL, 2, T], scope=sc) for i in range(2)]
                PT = [sb(f"PT0_{i}", [P, TL, P], scope=sc) for i in range(2)]
                OT = sb("Ot0", [P, TL * 2, DH0], scope=sc)
                OH = [sb(f"OH0_{i}", [P, CH], F32R, sc) for i in range(1)]
                OL = [sb(f"OL0_{i}", [P, CH], F32R, sc) for i in range(1)]
                mx, sm, rs = [sb(f"{n}0", [P, 2, TL * 2], scope=sc) for n in ("mx", "sm", "rs")]
                RT = fr.Tm if False else sb("RT0", [P, DH, CH], scope=sc)
                wq = io["l0_wqk"].rearrange("(k p) n -> k p n", p=P)
                wo = io["l0_wo"].rearrange("(g p) n -> p g n", p=P)
                pieces = [(wq[k][:, n * 512:(n + 1) * 512], WQK[0][:, k, n * 512:(n + 1) * 512], WQK[1][:, k, n * 512:(n + 1) * 512])
                          for n in range(4) for k in range(DH)]
                pieces += [(io["l0_wo"][g * P:(g + 1) * P, :], WO[0][:, g, :], WO[1][:, g, :]) for g in range(PAIRS)]
                l_sync, l_act, l_dve, n_w, l_passed = load_split(pieces, sc)

                def pe_proj(pe, G, jj, c, p, first):
                    if jj == 0:
                        pe.wait_ge(f_hl.h, f_hl.at(c + 1))
                    gr = c * 4 + jj // 2
                    if not first:
                        if jj % 2:
                            pe.wait_ge(va_sb.h, va_sb.at(2 * gr + 1)); pe.wait_ge(vd_sb.h, vd_sb.at(2 * gr + 1))
                        else:
                            pe.wait_ge(q_sb.h, q_sb.at(G))
                    for i, bank in ((0, BK[0]), (1, BK[1])):
                        if i == 1 and not first:
                            if jj % 2:
                                pe.wait_ge(va_sb.h, va_sb.at(2 * gr + 2)); pe.wait_ge(vd_sb.h, vd_sb.at(2 * gr + 2))
                            else:
                                pe.wait_ge(ka_sb.h, ka_sb.at(G)); pe.wait_ge(kd_sb.h, kd_sb.at(G))
                        o = i * H * DH0 + jj * P
                        for k in range(DH):
                            last = split3(bank[:], WQK[0][:, k, o:o + P], WQK[1][:, k, o:o + P], fr.HH[p][:, k], fr.HL[p][:, k],
                                          k == 0, k == DH - 1)
                        last.then_inc((q_ps, k_ps)[i].h, 1)
                    if jj % 2 == 0:
                        for hf in range(2):
                            if hf == 0:
                                pe.wait_ge(q_sb.h, q_sb.at(G + 1))
                            else:
                                pe.wait_ge(ka_sb.h, ka_sb.at(G + 1)); pe.wait_ge(kd_sb.h, kd_sb.at(G + 1))
                            for b in range(CB // 2):
                                for k in range(DH):
                                    for h2 in range(2):
                                        bb = hf * CB // 2 + b
                                        last = nc.tensor.matmul(BK[hf][h2 * T:(h2 + 1) * T, b * P:(b + 1) * P],
                                                                fr.h32(p)[:, k, bb * T:(bb + 1) * T], WV[:, k, h2, jj:jj + 2, :],
                                                                start=(k == 0), stop=(k == DH - 1), skip_group_check=True)
                            last.then_inc(v_ps.h, 1)

                def act_proj(act, G, jj, c):
                    act.wait_ge(q_ps.h, q_ps.at(G + 1))
                    if jj is not None and not (isinstance(G, int) and G < 2):
                        act.wait_ge(s_ready.h, s_ready.at(G - 1))
                    nc.scalar.activation(Q[jj % 2][:], BK[0][:], ACT.Copy).then_inc(q_sb.h, 1)
                    act.wait_ge(k_ps.h, k_ps.at(G + 1))
                    nc.scalar.activation(KB[jj % 2][0:T, :, 0, :], BK[1][0:T, :].rearrange("p (b t) -> p b t", t=T), ACT.Copy).then_inc(ka_sb.h, 1)
                    if jj % 2 == 0:
                        gr = c * 4 + jj // 2
                        for hf in range(2):
                            act.wait_ge(v_ps.h, v_ps.at(2 * gr + hf + 1))
                            if not (isinstance(gr, int) and gr < 2):
                                act.wait_ge(o_ps.h, o_ps.at(2 * gr - 2))
                            nc.scalar.activation(VB[(jj // 2) % 2][0:T, 4 * hf:4 * hf + 4, :, 0, :],
                                                 BK[hf][0:T, :].rearrange("p (b r d) -> p b r d", b=4, r=2), ACT.Copy).then_inc(va_sb.h, 1)

                def dve_proj(dve, G, jj, c):
                    dve.wait_ge(k_ps.h, k_ps.at(G + 1))
                    if not (isinstance(G, int) and G < 2):
                        dve.wait_ge(s_ready.h, s_ready.at(G - 1))
                    nc.vector.tensor_copy(KB[jj % 2][T:P, :, 1, :], BK[1][T:P, :].rearrange("p (b t) -> p b t", t=T)).then_inc(kd_sb.h, 1)
                    if jj % 2 == 0:
                        gr = c * 4 + jj // 2
                        for hf in range(2):
                            dve.wait_ge(v_ps.h, v_ps.at(2 * gr + hf + 1))
                            if not (isinstance(gr, int) and gr < 2):
                                dve.wait_ge(o_ps.h, o_ps.at(2 * gr - 2))
                            nc.vector.tensor_copy(VB[(jj // 2) % 2][T:P, 4 * hf:4 * hf + 4, :, 1, :],
                                                  BK[hf][T:P, :].rearrange("p (b r d) -> p b r d", b=4, r=2)).then_inc(vd_sb.h, 1)

                with nc.Block() as block:
                    @block.sync
                    def _(sp):
                        sp.dma_start(WV[:], io["l0_wv"].rearrange("(k p) (a r d) -> p k a r d", p=P, a=2, r=PAIRS)).then_inc(d_in.h, 16)
                        l_sync(sp)
                        sp.wait_ge(d_in.h, d_in.at(16))

                    @block.tensor
                    def _(pe):
                        fr.pe_mean(pe, 0)
                        pe.wait_ge(f_d.h, f_d.at(1))
                        fr.pe_var(pe, 0)
                        pe.wait_ge(w_lo.h, w_lo.at(n_w))
                        pe.wait_ge(d_in.h, d_in.at(16))
                        pe.wait_ge(f_v.h, f_v.at(1))
                        pe_proj(pe, 0, 0, 0, 0, True)

                        def t_o(pe, g):
                            pe.wait_ge(o_sb.h, o_sb.at(g + 1))
                            pe.wait_ge(ot_lo.h, ot_lo.at(g))
                            for t in range(TL):
                                last = nc.tensor.transpose(TRB[:, t * P:(t + 1) * P], OT[:, 2 * t:2 * t + 2, :].rearrange("p a d -> p (a d)"), ident[:])
                            last.then_inc(ot_ps.h, 1)

                        def out(pe, g, jj, c):
                            pe.wait_ge(ot_hi.h, ot_hi.at(g + 1)); pe.wait_ge(ot_lo.h, ot_lo.at(g + 1))
                            if jj == 0:
                                pe.wait_ge(out_taken.h, out_taken.at(2 * c))
                            for m in range(DH):
                                last = split3(O2[:, m, :], WO[0][:, jj, m * P:(m + 1) * P], WO[1][:, jj, m * P:(m + 1) * P],
                                              OH[0][:], OL[0][:], jj == 0, jj == PAIRS - 1)
                            last.then_inc(out_ready.h, 1)

                        def body(c, p, more):
                            for j in range(PAIRS):
                                g = c * PAIRS + j
                                pe.wait_ge(q_sb.h, q_sb.at(g + 1)); pe.wait_ge(ka_sb.h, ka_sb.at(g + 1)); pe.wait_ge(kd_sb.h, kd_sb.at(g + 1))
                                pe.wait_ge(s_sub.h, s_sub.at(g))
                                for t in range(TL):
                                    for b in range(2):
                                        bb = 2 * t + b
                                        last = nc.tensor.matmul(S[b * T:(b + 1) * T, t * P:(t + 1) * P], Q[j % 2][:, bb * T:(bb + 1) * T],
                                                                KB[j % 2][:, bb].rearrange("p a t -> p (a t)"), start=True, stop=True)
                                last.then_inc(s_ready.h, 1)
                                if j > 0:
                                    if j == 2 and more:
                                        pe.wait_ge(f_d.h, f_d.at(c + 2))
                                    if j == 5 and more:
                                        pe.wait_ge(f_v.h, f_v.at(c + 2))
                                    t_o(pe, g - 1)
                                if j < PAIRS - 1:
                                    pe_proj(pe, g + 1, j + 1, c, p, False)
                                elif more:
                                    pe_proj(pe, g + 1, 0, c + 1, 1 - p, False)
                                pe.wait_ge(p_exp.h, p_exp.at(g + 1))
                                pe.wait_ge(pt_sb.h, pt_sb.at(g))
                                for t in range(TL):
                                    last = nc.tensor.transpose(TRA[:, t * P:(t + 1) * P], SP[j % 2][:, t].rearrange("p a t -> p (a t)"), ident[:])
                                last.then_inc(pt_ps.h, 1)
                                if j > 0:
                                    out(pe, g - 1, j - 1, c)
                                if j == 1 and more:
                                    fr.pe_mean(pe, c + 1)
                                if j == 4 and more:
                                    fr.pe_var(pe, c + 1)
                                pe.wait_ge(pt_sb.h, pt_sb.at(g + 1))
                                gr = c * 4 + j // 2
                                pe.wait_ge(va_sb.h, va_sb.at(2 * gr + 2)); pe.wait_ge(vd_sb.h, vd_sb.at(2 * gr + 2))
                                pe.wait_ge(o_sb.h, o_sb.at(g))
                                for t in range(TL):
                                    for b in range(2):
                                        last = nc.tensor.matmul(O[b * T:(b + 1) * T, t * P:(t + 1) * P], PT[j % 2][:, t, b * T:(b + 1) * T],
                                                                VB[(j // 2) % 2][:, 2 * t + b, j % 2].rearrange("p a d -> p (a d)"), start=True, stop=True)
                                last.then_inc(o_ps.h, 1)
                            t_o(pe, c * PAIRS + PAIRS - 1)
                            out(pe, c * PAIRS + PAIRS - 1, PAIRS - 1, c)
                        chunks(pe, body)

                    @block.scalar
                    def _(act):
                        fr.act_xh(act, 0)
                        fr.act_sq(act, 0)
                        fr.act_rstd(act, 0)
                        fr.act_hh(act, 0, 0)
                        l_act(act)
                        z_done = step_p
                        act.wait_ge(z_done.h, z_done.at(4))
                        act_proj(act, 0, 0, 0)

                        def oh(g, jj):
                            act.wait_ge(ot_ps.h, ot_ps.at(g + 1))
                            act.wait_ge(out_ready.h, out_ready.at(g))
                            nc.scalar.activation(OH[0][:], TRB[:], ACT.Copy).then_inc(ot_hi.h, 1)

                        def body(c, p, more):
                            for j in range(PAIRS):
                                g = c * PAIRS + j
                                if j > 0:
                                    oh(g - 1, j - 1)
                                if j < PAIRS - 1:
                                    act_proj(act, g + 1, j + 1, c)
                                elif more:
                                    act_proj(act, g + 1, 0, c + 1)
                                act.wait_ge(s_sub.h, s_sub.at(g + 1))
                                nc.scalar.activation(SP[j % 2][:], SP[j % 2][:], ACT.Exp, scale=DH0 ** -0.5).then_inc(p_exp.h, 1)
                                act.wait_ge(pt_ps.h, pt_ps.at(g + 1))
                                if not (isinstance(g, int) and g < 2) and j >= 1:
                                    act.wait_ge(o_ps.h, o_ps.at(g - 1))
                                elif j == 0:
                                    act.wait_ge(o_ps.h, o_ps.at(g))
                                nc.scalar.activation(PT[j % 2][:].rearrange("p t q -> p (t q)"), TRA[:], ACT.Copy).then_inc(pt_sb.h, 1)
                                if more:
                                    if j == 0:
                                        fr.act_xh(act, c + 1)
                                    if j == 3:
                                        fr.act_sq(act, c + 1)
                                    if j == 5:
                                        fr.act_rstd(act, c + 1)
                                    if j == 6:
                                        fr.act_hh(act, c + 1, 1 - p)
                            oh(c * PAIRS + PAIRS - 1, PAIRS - 1)
                        chunks(act, body)

                    @block.vector
                    def _(dve):
                        fr.dve_d(dve, 0)
                        fr.dve_v(dve, 0)
                        fr.dve_norm(dve, 0)
                        fr.dve_h(dve, 0, 0)
                        fr.dve_hl(dve, 0, 0)
                        l_dve(dve)
                        dve.wait_ge(step_p.h, step_p.at(4))
                        dve_proj(dve, 0, 0, 0)

                        def ol(g):
                            dve.wait_ge(ot_hi.h, ot_hi.at(g + 1))
                            nc.vector.tensor_tensor(OL[0][:], TRB[:], OH[0][:].bitcast(F32), ALU.subtract).then_inc(ot_lo.h, 1)

                        def body(c, p, more):
                            for j in range(PAIRS):
                                g = c * PAIRS + j
                                dve.wait_ge(s_ready.h, s_ready.at(g + 1))
                                sv = S.rearrange("p (a t) -> p a t", t=T)
                                nc.vector.tensor_reduce(mx[:, j % 2], sv, AXX, ALU.max).then_inc(s_max.h, 1)
                                dve.wait_ge(s_max.h, s_max.at(g + 1))
                                if j == 0:
                                    dve.wait_ge(pt_ps.h, pt_ps.at(g))
                                else:
                                    dve.wait_ge(pt_ps.h, pt_ps.at(g - 1))
                                spv = SP[j % 2][:].rearrange("p t a k -> p (t a) k")
                                nc.vector.tensor_tensor(spv, sv, mx[:, j % 2].unsqueeze(2).to_broadcast([P, TL * 2, T]), ALU.subtract).then_inc(s_sub.h, 1)
                                if j > 0:
                                    ol(g - 1)
                                if j < PAIRS - 1:
                                    dve_proj(dve, g + 1, j + 1, c)
                                elif more:
                                    dve_proj(dve, g + 1, 0, c + 1)
                                dve.wait_ge(p_exp.h, p_exp.at(g + 1))
                                nc.vector.tensor_reduce(sm[:, j % 2], spv, AXX, ALU.add).then_inc(p_sum.h, 1)
                                dve.wait_ge(p_sum.h, p_sum.at(g + 1))
                                nc.vector.reciprocal(rs[:, j % 2], sm[:, j % 2]).then_inc(p_rec.h, 1)
                                if more:
                                    if j == 1:
                                        fr.dve_d(dve, c + 1)
                                    if j == 4:
                                        fr.dve_v(dve, c + 1)
                                    if j == 5:
                                        fr.dve_norm(dve, c + 1)
                                    if j == 6:
                                        fr.dve_h(dve, c + 1, 1 - p)
                                        fr.dve_hl(dve, c + 1, 1 - p)
                                dve.wait_ge(o_ps.h, o_ps.at(g + 1))
                                dve.wait_ge(p_rec.h, p_rec.at(g + 1))
                                dve.wait_ge(ot_ps.h, ot_ps.at(g))
                                nc.vector.tensor_tensor(OT[:], O.rearrange("p (a d) -> p a d", d=DH0),
                                                        rs[:, j % 2].unsqueeze(2).to_broadcast([P, TL * 2, DH0]), ALU.mult).then_inc(o_sb.h, 1)
                            ol(c * PAIRS + PAIRS - 1)
                            dve.wait_ge(out_ready.h, out_ready.at((c + 1) * PAIRS))
                            residual_dve(dve, c, 0, G_A, BC["b_out0"], RT, O2)
                        chunks(dve, body)

                    @block.gpsimd
                    def _(pool):
                        for i in range(2):
                            nc.gpsimd.memset(KB[i][:], 0.0).then_inc(step_p.h, 1)
                            nc.gpsimd.memset(VB[i][:], 0.0).then_inc(step_p.h, 1)
                        fr.pool_xl(pool, 0)
                        fr.pool_sq(pool, 0)
                        fr.pool_scale(pool, 0)

                        def body(c, p, more):
                            if more:
                                fr.pool_xl(pool, c + 1)
                                fr.pool_sq(pool, c + 1)
                                fr.pool_scale(pool, c + 1)
                            residual_pool(pool, c, RT)
                        chunks(pool, body)
                fr.passed(); l_passed(); d_in.passed(16); step_p.passed(4)
                n = NCH * PAIRS
                for c in (q_ps, k_ps, q_sb, ka_sb, kd_sb, s_ready, s_max, s_sub, p_exp, p_sum, p_rec, pt_ps, pt_sb, o_ps, o_sb,
                          ot_ps, ot_hi, ot_lo, out_ready, v_ps, va_sb, vd_sb):
                    c.passed(n)
                out_taken.passed(2 * NCH); x_added.passed(NCH)

        def feed_forward(tag, l, kind, n_m, ins1, in2, centred, eps, bcol_in, bcol_out):
            with ExitStack() as sc:
                n_in = len(ins1)
                W1 = [[sb(f"W1{tag}_{a}{i}", [P, DH, n_m * P], F32R, sc) for i in range(2)] for a in range(n_in)]
                W2 = [sb(f"W2{tag}_{i}", [P, n_m, D], F32R, sc) for i in range(2)]
                gate = kind == "gate"
                h_free = lambda e, c: None if isinstance(c, int) and c < 2 else e.wait_ge(a_ps.h, a_ps.at(n_m * (c - 1)))
                MB, VBK = S2[:, 0, :], S2[:, 1, :]
                fr = Front(sc, l, SH_M, SC_M, centred, eps, MB, VBK,
                           lambda pe, c: pe.wait_ge(f_d.h, f_d.at(c)), lambda pe, c: pe.wait_ge(f_v.h, f_v.at(c)), h_free, keep_h=False)
                Gf = [sb(f"Gf{tag}{i}", [P, CH], scope=sc) for i in range(2)]
                Gt = [sb(f"Gt{tag}{i}", [P, CH], scope=sc) for i in range(2)]
                Gh = [sb(f"Gh{tag}{i}", [P, CH], F32R, sc) for i in range(2)]
                Gl = [sb(f"Gl{tag}{i}", [P, CH], F32R, sc) for i in range(2)]
                RT = sb(f"RT{tag}", [P, DH, CH], scope=sc)
                pieces = []
                step_w = 512 if (n_m * P) % 512 == 0 else 384
                for n in range(0, n_m * P, step_w):
                    for a in range(n_in):
                        for k in range(DH):
                            pieces.append((ins1[a][k * P:(k + 1) * P, n:n + step_w], W1[a][0][:, k, n:n + step_w], W1[a][1][:, k, n:n + step_w]))
                pieces += [(in2[m * P:(m + 1) * P, :], W2[0][:, m, :], W2[1][:, m, :]) for m in range(n_m)]
                l_sync, l_act, l_dve, n_w, l_passed = load_split(pieces, sc)

                def bias(a, m):
                    if kind == "gate":
                        return tgb[:, a * n_m + m:a * n_m + m + 1]
                    return bias_cols[:, bcol_in + m:bcol_in + m + 1]

                def front_act(act, s, c, p):
                    if gate:
                        if s == 0:
                            if not (isinstance(c, int) and c < 2):
                                h_free(act, c)
                            nc.scalar.activation(fr.HH[p][:], X[:, :, tok(c)], ACT.Copy).then_inc(f_hh.h, 1)
                        return
                    if s == 0: fr.act_xh(act, c)
                    if s == 1: fr.act_sq(act, c)
                    if s == 2: fr.act_rstd(act, c)
                    if s == 3: fr.act_hh(act, c, p)

                def front_dve(dve, s, c, p):
                    if gate:
                        if s == 0:
                            dve.wait_ge(f_hh.h, f_hh.at(c + 1))
                            nc.vector.tensor_tensor(fr.HL[p][:], X[:, :, tok(c)], fr.HH[p][:].bitcast(F32), ALU.subtract).then_inc(f_hl.h, 1)
                        return
                    if s == 0: fr.dve_d(dve, c)
                    if s == 1: fr.dve_v(dve, c)
                    if s == 2: fr.dve_norm(dve, c)
                    if s == 3:
                        fr.dve_h(dve, c, p)
                        fr.dve_hl(dve, c, p)

                def front_pe(pe, s, c):
                    if not gate:
                        if s == 0: fr.pe_mean(pe, c)
                        if s == 1: fr.pe_var(pe, c)

                def front_pool(pool, c):
                    if not gate:
                        fr.pool_xl(pool, c)
                        fr.pool_sq(pool, c)
                        fr.pool_scale(pool, c)

                slots = {0: 0, 1: 1, 2: 2, 3: 3} if n_m >= 4 and n_m < 6 else {0: 0, 2: 1, 3: 2, 4: 3}
                dual = n_in == 2

                with nc.Block() as block:
                    @block.sync
                    def _(sp):
                        l_sync(sp)

                    @block.tensor
                    def _(pe):
                        def up(G, m, c, p, first):
                            if m == 0:
                                pe.wait_ge(f_hl.h, f_hl.at(c + 1))
                            if not first:
                                pe.wait_ge(g_act.h, g_act.at((2 if gate else 1) * (G - 1)))
                                if kind == "swiglu":
                                    pe.wait_ge(g_mul.h, g_mul.at(G - 1))
                            for a in range(n_in):
                                for k in range(DH):
                                    last = split3(BK[2 * a + m % 2][:], W1[a][0][:, k, m * P:(m + 1) * P], W1[a][1][:, k, m * P:(m + 1) * P],
                                                  fr.HH[p][:, k], fr.HL[p][:, k], k == 0, k == DH - 1)
                            last.then_inc(a_ps.h, 1)

                        front_pe(pe, 0, 0)
                        front_pe(pe, 1, 0)
                        pe.wait_ge(w_lo.h, w_lo.at(n_w))
                        up(0, 0, 0, 0, True)

                        def body(c, p, more):
                            for m in range(n_m):
                                g = c * n_m + m
                                if m < n_m - 1:
                                    up(g + 1, m + 1, c, p, False)
                                elif more:
                                    up(g + 1, 0, c + 1, 1 - p, False)
                                pe.wait_ge(g_lo.h, g_lo.at(g + 1))
                                if m == 0:
                                    pe.wait_ge(out_taken.h, out_taken.at(2 * c))
                                for mo in range(DH):
                                    last = split3(O2[:, mo, :], W2[0][:, m, mo * P:(mo + 1) * P], W2[1][:, m, mo * P:(mo + 1) * P],
                                                  Gh[m % 2][:], Gl[m % 2][:], m == 0, m == n_m - 1)
                                last.then_inc(g_used.h, 1)
                                if more and m in slots:
                                    front_pe(pe, slots[m], c + 1)
                        chunks(pe, body)

                    @block.scalar
                    def _(act):
                        for s in range(4):
                            front_act(act, s, 0, 0)
                        l_act(act)

                        def body(c, p, more):
                            for m in range(n_m):
                                g = c * n_m + m
                                act.wait_ge(a_ps.h, a_ps.at(g + 1))
                                if m == 0:
                                    act.wait_ge(g_lo.h, g_lo.at(g))
                                else:
                                    act.wait_ge(g_lo.h, g_lo.at(g - 1))
                                src = BK[m % 2][:]
                                if kind == "swiglu":
                                    nc.scalar.activation(Gf[m % 2][:], src, ACT.Silu).then_inc(g_act.h, 1)
                                else:
                                    nc.scalar.activation(Gf[m % 2][:], src, ACT.Gelu, bias=bias(0, m)).then_inc(g_act.h, 1)
                                if gate:
                                    nc.scalar.activation(Gt[m % 2][:], BK[2 + m % 2][:], ACT.Tanh, bias=bias(1, m)).then_inc(g_act.h, 1)
                                if more and m in slots:
                                    front_act(act, slots[m], c + 1, 1 - p)
                        chunks(act, body)

                    @block.vector
                    def _(dve):
                        for s in range(4):
                            front_dve(dve, s, 0, 0)
                        l_dve(dve)

                        def body(c, p, more):
                            for m in range(n_m):
                                g = c * n_m + m
                                gf = Gf[m % 2][:]
                                if gate:
                                    dve.wait_ge(g_act.h, g_act.at(2 * g + 2))
                                    nc.vector.tensor_tensor(gf, gf, Gt[m % 2][:], ALU.mult).then_inc(g_mul.h, 1)
                                    dve.wait_ge(g_mul.h, g_mul.at(g + 1))
                                else:
                                    dve.wait_ge(g_act.h, g_act.at(g + 1))
                                if kind == "swiglu":
                                    nc.vector.tensor_tensor(gf, gf, BK[2 + m % 2][:], ALU.mult).then_inc(g_mul.h, 1)
                                    dve.wait_ge(g_mul.h, g_mul.at(g + 1))
                                if m == 0:
                                    dve.wait_ge(g_used.h, g_used.at(g))
                                else:
                                    dve.wait_ge(g_used.h, g_used.at(g - 1))
                                nc.vector.tensor_copy(Gh[m % 2][:], gf).then_inc(g_hi.h, 1)
                                dve.wait_ge(g_hi.h, g_hi.at(g + 1))
                                nc.vector.tensor_tensor(Gl[m % 2][:], gf, Gh[m % 2][:].bitcast(F32), ALU.subtract).then_inc(g_lo.h, 1)
                                if more and m in slots:
                                    front_dve(dve, slots[m], c + 1, 1 - p)
                            dve.wait_ge(g_used.h, g_used.at((c + 1) * n_m))
                            if gate:
                                for mo in range(DH):
                                    nc.vector.scalar_tensor_tensor(out=X[:, mo, tok(c)], in0=O2[:, mo, :], scalar=bias_cols[:, bcol_out + mo:bcol_out + mo + 1],
                                                                   in1=X[:, mo, tok(c)], op0=ALU.add, op1=ALU.add).then_inc(out_taken.h, 1)
                            else:
                                residual_dve(dve, c, l, G_M, bcol_out, RT, O2)
                        chunks(dve, body)

                    @block.gpsimd
                    def _(pool):
                        front_pool(pool, 0)

                        def body(c, p, more):
                            if more:
                                front_pool(pool, c + 1)
                            residual_pool(pool, c, RT)
                        if not gate:
                            chunks(pool, body)
                if gate:
                    f_hh.passed(NCH); f_hl.passed(NCH)
                else:
                    fr.passed(); x_added.passed(NCH)
                l_passed()
                n = NCH * n_m
                for c in (a_ps, g_hi, g_lo, g_used):
                    c.passed(n)
                g_act.passed(2 * n if gate else n)
                if kind != "gelu":
                    g_mul.passed(n)
                out_taken.passed(2 * NCH)

        def attention12(l):
            with ExitStack() as sc:
                tag = f"a{l}"
                WQK = [sb(f"WQK{tag}_{i}", [P, DH, 2 * D], F32R, sc) for i in range(2)]
                WO = [sb(f"WO{tag}_{i}", [P, DH, D], F32R, sc) for i in range(2)]
                WV = sb("WV" + tag, [P, DH, 2, P], scope=sc)
                SB_ = S2
                fr = Front(sc, l, SH_A, SC_A, l == 2, 1e-6, O2[:, 1, :], O2[:, 1, :],
                           lambda pe, c: pe.wait_ge(f_v.h, f_v.at(c)), (lambda pe, c: pe.wait_ge(f_d.h, f_d.at(c + 1))) if l == 2 else (lambda pe, c: pe.wait_ge(f_v.h, f_v.at(c))),
                           lambda e, c: None if isinstance(c, int) and c < 2 else e.wait_ge(v_ps.h, v_ps.at(TL * (c - 1))))
                SQ = sb("SQ" + tag, [P, 2 * H, DH1], scope=sc)
                SS = sb("SS" + tag, [P, 4, 2 * H], scope=sc)
                WN = sb("WN" + tag, [P, 2 * H, DH1], scope=sc)
                VBI = sb("VBI" + tag, [P, PAIRS, DH1], scope=sc)
                RC = sb("RC" + tag, [P, 2, DH1], scope=sc)
                QN = [sb(f"QN{tag}{i}", [P, 2 * H, DH1], scope=sc) for i in range(2)]
                RA = sb("RA" + tag, [P, 2 * H, DH1], scope=sc)
                RB = sb("RB" + tag, [P, 2 * H, DH1], scope=sc)
                QT = sb("QT" + tag, [P, 2, P], scope=sc)
                KB = sb("KB" + tag, [P, 2, 2, 8, T], scope=sc)
                VB = [sb(f"VB{tag}{i}", [P, 2, PAIRS, 2, DH1 + 1], scope=sc) for i in range(TL)]
                SP = [sb(f"SP{tag}{i}", [P, H, T], scope=sc) for i in range(2)]
                PT = sb("PT" + tag, [P, PAIRS, P], scope=sc)
                mx = sb("mx" + tag, [P, 2, H], scope=sc)
                rs = sb("rs" + tag, [P, H], scope=sc)
                OT = sb("OT" + tag, [P, H, DH1], scope=sc)
                OH = sb("OH" + tag, [P, DH, CH], F32R, sc)
                OL = sb("OL" + tag, [P, DH, CH], F32R, sc)
                RT = sb("RT" + tag, [P, DH, CH], scope=sc)
                ones1 = sb("ones1" + tag, [P, 2, PAIRS], scope=sc)
                w = io[f"l{l}_wqk"]
                pieces = [(w[k * P:(k + 1) * P, :], WQK[0][:, k], WQK[1][:, k]) for k in range(DH)]
                pieces += [(io[f"l{l}_wo"][k * P:(k + 1) * P, :], WO[0][:, k], WO[1][:, k]) for k in range(DH)]
                l_sync, l_act, l_dve, n_w, l_passed = load_split(pieces, sc)
                QKB, VBK, TR, O = BK[0], BK[1], (BK[2], BK[3]), O2[:, 0, 0:PAIRS * 2 * (DH1 + 1)]

                order = [("t4", 0)]
                for t in range(1, TL):
                    order += [("t4", t), ("pa", t - 1), ("pb", t - 1), ("to", t - 1)]
                order += [("pa", TL - 1), ("pb", TL - 1), ("to", TL - 1)]
                n_tr = len(order)

                def tr(kind, t):
                    return TR[order.index((kind, t)) % 2]

                def tr_wait(pe, kind, t, c):
                    i = order.index((kind, t))
                    k0, t0 = order[(i - 2) % n_tr]
                    tt = c * TL + t0 - (TL if i < 2 else 0)
                    if k0 == "t4":
                        pe.wait_ge(kd_sb.h, kd_sb.at(2 * tt + 2))
                    elif k0 == "pa":
                        pe.wait_ge(pt_sb.h, pt_sb.at(2 * tt + 1))
                    elif k0 == "pb":
                        pe.wait_ge(pt_sb.h, pt_sb.at(2 * tt + 2))
                    else:
                        pe.wait_ge(ot_lo.h, ot_lo.at(tt + 1))

                n_d = 32 if l == 1 else 80

                def pe_proj(pe, tt, t, c, p, first):
                    if t == 0:
                        pe.wait_ge(f_hl.h, f_hl.at(c + 1))
                    if not first:
                        pe.wait_ge(qk_n.h, qk_n.at(tt))
                    for i, (xp, wp) in enumerate(((0, 1), (1, 0), (0, 0))):
                        for k in range(DH):
                            last = nc.tensor.matmul(QKB[:], (fr.HH, fr.HL)[xp][p][:, k, t * P:(t + 1) * P], WQK[wp][:, k],
                                                    start=(i == 0 and k == 0), stop=(i == 2 and k == DH - 1))
                    last.then_inc(q_ps.h, 1)
                    if not first:
                        pe.wait_ge(va_sb.h, va_sb.at(tt)); pe.wait_ge(vd_sb.h, vd_sb.at(tt))
                    for b in range(2):
                        for k in range(DH):
                            for h2 in range(2):
                                last = nc.tensor.matmul(VBK[h2 * T:(h2 + 1) * T, b * P:(b + 1) * P],
                                                        fr.h32(p)[:, k, t * P + b * T:t * P + (b + 1) * T], WV[:, k, h2],
                                                        start=(k == 0), stop=(k == DH - 1), skip_group_check=True)
                    last.then_inc(v_ps.h, 1)

                def v_src(half):
                    return VBK[half * T:(half + 1) * T, 0:2 * P].rearrange("p (b r d) -> p b r d", b=2, r=PAIRS)

                def act_proj(act, tt, t):
                    act.wait_ge(v_ps.h, v_ps.at(tt + 1))
                    if l == 1:
                        if not (isinstance(tt, int) and tt < 2):
                            act.wait_ge(o_ps.h, o_ps.at(tt - 3))
                        nc.scalar.activation(VB[t][0:T, :, :, 0, 0:DH1], v_src(0), ACT.Copy).then_inc(va_sb.h, 1)
                        act.wait_ge(q_ps.h, q_ps.at(tt + 1))
                        act.wait_ge(ss_sum.h, ss_sum.at(tt))
                        nc.scalar.activation(SQ[:].rearrange("p h d -> p (h d)"), QKB[:], ACT.Square).then_inc(sq_sb.h, 1)
                        act.wait_ge(ss_eps.h, ss_eps.at(tt + 1))
                        nc.scalar.activation(SS[:, 1], SS[:, 0], ACT.Ln).then_inc(ss_ln.h, 1)
                        act.wait_ge(ss_ln.h, ss_ln.at(tt + 1))
                        nc.scalar.activation(SS[:, 1], SS[:, 1], ACT.Exp, scale=-0.5).then_inc(ss_exp.h, 1)

                def dve_proj(dve, tt, t):
                    dve.wait_ge(v_ps.h, v_ps.at(tt + 1))
                    if not (isinstance(tt, int) and tt < 2):
                        dve.wait_ge(o_ps.h, o_ps.at(tt - 3))
                    if l == 2:
                        for half in range(2):
                            nc.vector.tensor_tensor(VB[t][half * T:(half + 1) * T, :, :, half, 0:DH1], v_src(half),
                                                    VBI[half * T:(half + 1) * T].unsqueeze(1).to_broadcast([T, 2, PAIRS, DH1]),
                                                    ALU.add).then_inc((va_sb, vd_sb)[half].h, 1)
                    else:
                        nc.vector.tensor_copy(VB[t][T:P, :, :, 1, 0:DH1], v_src(1)).then_inc(vd_sb.h, 1)
                    qk = QKB[:].rearrange("p (h d) -> p h d", d=DH1)
                    if l == 1:
                        dve.wait_ge(sq_sb.h, sq_sb.at(tt + 1))
                        nc.vector.tensor_reduce(SS[:, 0], SQ[:], AXX, ALU.add).then_inc(ss_sum.h, 1)
                        dve.wait_ge(ss_sum.h, ss_sum.at(tt + 1))
                        nc.vector.tensor_scalar(SS[:, 0], SS[:, 0], 1.0 / DH1, 1e-6, ALU.mult, ALU.add).then_inc(ss_eps.h, 1)
                        dve.wait_ge(ss_exp.h, ss_exp.at(tt + 1))
                        nc.vector.scalar_tensor_tensor(out=SS[:, 2], in0=SS[:, 1], scalar=-0.5, in1=SS[:, 1], op0=ALU.mult, op1=ALU.mult).then_inc(ss_n1.h, 1)
                        dve.wait_ge(ss_n1.h, ss_n1.at(tt + 1))
                        nc.vector.tensor_tensor(SS[:, 2], SS[:, 2], SS[:, 0], ALU.mult).then_inc(ss_n2.h, 1)
                        dve.wait_ge(ss_n2.h, ss_n2.at(tt + 1))
                        nc.vector.scalar_tensor_tensor(out=SS[:, 3], in0=SS[:, 2], scalar=1.5, in1=SS[:, 1], op0=ALU.add, op1=ALU.mult).then_inc(ss_r.h, 1)
                        dve.wait_ge(ss_r.h, ss_r.at(tt + 1))
                    else:
                        dve.wait_ge(q_ps.h, q_ps.at(tt + 1))
                    if not (isinstance(tt, int) and tt < 2):
                        dve.wait_ge(t4_ps.h, t4_ps.at(tt - 1))
                    if l == 1:
                        nc.vector.tensor_tensor(QN[t % 2][:], qk, SS[:, 3].unsqueeze(2).to_broadcast([P, 2 * H, DH1]), ALU.mult).then_inc(qk_n.h, 1)
                    else:
                        nc.vector.tensor_tensor(QN[t % 2][:], qk, WN[:], ALU.add).then_inc(qk_n.h, 1)

                def pool_rope(pool, tt, t):
                    pool.wait_ge(qk_n.h, qk_n.at(tt + 1))
                    q = QN[t % 2]
                    if l == 1:
                        nc.gpsimd.tensor_tensor(q[:], q[:], WN[:], ALU.mult).then_inc(qk_w.h, 1)
                        pool.wait_ge(qk_w.h, qk_w.at(tt + 1))
                        n = 12
                        cs = rope_c1[:, bass.ds(tt, 1), :].to_broadcast([P, 2 * H, n])
                        sn = rope_s1[:, bass.ds(tt, 1), :].rearrange("p o (a i) -> p o a i", i=2)
                        qv = q[:, :, 0:n].rearrange("p h (a i) -> p h a i", i=2)
                        bv = RB[:, :, 0:n].rearrange("p h (a i) -> p h a i", i=2)
                        halves = [(bv[:, :, :, i], qv[:, :, :, 1 - i], sn[:, :, :, i].to_broadcast([P, 2 * H, n // 2])) for i in range(2)]
                    else:
                        n = DH1
                        cs = RC[:, 0:1, :].to_broadcast([P, 2 * H, n])
                        halves = [(RB[:, :, 8 * i:8 * i + 8], q[:, :, 8 - 8 * i:16 - 8 * i], RC[:, 1:2, 8 * i:8 * i + 8].to_broadcast([P, 2 * H, 8]))
                                  for i in range(2)]
                    pool.wait_ge(rc.h, rc.at(tt))
                    nc.gpsimd.tensor_tensor(RA[:, :, 0:n], q[:, :, 0:n], cs, ALU.mult).then_inc(ra.h, 1)
                    for o, a, s_ in halves:
                        nc.gpsimd.tensor_tensor(o, a, s_, ALU.mult).then_inc(rb.h, 1)
                    pool.wait_ge(ra.h, ra.at(tt + 1))
                    pool.wait_ge(rb.h, rb.at(2 * tt + 2))
                    nc.gpsimd.tensor_tensor(q[:, :, 0:n], RA[:, :, 0:n], RB[:, :, 0:n], ALU.add).then_inc(rc.h, 1)

                with nc.Block() as block:
                    @block.sync
                    def _(sp):
                        sp.dma_start(WV[:], io[f"l{l}_wv"].rearrange("(k p) (a n) -> p k a n", p=P, a=2)).then_inc(d_in.h, 16)
                        sp.dma_start(WN[:], io[f"l{l}_qkrow"].rearrange("(o h) d -> o h d", o=1).to_broadcast([P, 2 * H, DH1])).then_inc(d_in.h, 16)
                        if l == 2:
                            for half in range(2):
                                sp.dma_start(VBI[half * T:(half + 1) * T], io["l2_vrow"][half:half + 1].to_broadcast([T, PAIRS, DH1])).then_inc(d_in.h, 16)
                            sp.dma_start(RC[:], io["rope2"]).then_inc(d_in.h, 16)
                        l_sync(sp)
                        sp.wait_ge(d_in.h, d_in.at(n_d))

                    @block.tensor
                    def _(pe):
                        fr.pe_mean(pe, 0)
                        fr.pe_var(pe, 0)
                        pe.wait_ge(w_lo.h, w_lo.at(n_w))
                        pe.wait_ge(d_in.h, d_in.at(n_d))
                        pe_proj(pe, 0, 0, 0, 0, True)

                        def weights_t(pe, tt, t, c):
                            pe.wait_ge(p_exp.h, p_exp.at(tt + 1))
                            for i, kd in enumerate(("pa", "pb")):
                                tr_wait(pe, kd, t, c)
                                for r in range(4):
                                    last = nc.tensor.transpose(tr(kd, t)[:, r * P:(r + 1) * P],
                                                               SP[t % 2][:, 8 * i + 2 * r:8 * i + 2 * r + 2].rearrange("p h k -> p (h k)"), ident[:])
                                last.then_inc(pt_ps.h, 1)
                            pe.wait_ge(va_sb.h, va_sb.at(tt + 1)); pe.wait_ge(vd_sb.h, vd_sb.at(tt + 1))
                            pe.wait_ge(o_sb.h, o_sb.at(tt))
                            w_ = 2 * (DH1 + 1)
                            for r in range(PAIRS):
                                if r % 4 == 0:
                                    pe.wait_ge(pt_sb.h, pt_sb.at(2 * tt + 1 + r // 4))
                                for b in range(2):
                                    last = nc.tensor.matmul(O[b * T:(b + 1) * T, r * w_:(r + 1) * w_], PT[:, r, b * T:(b + 1) * T],
                                                            VB[t][:, b, r].rearrange("p a d -> p (a d)"), start=True, stop=True)
                            last.then_inc(o_ps.h, 1)

                        def out_t(pe, tt, t, c):
                            pe.wait_ge(o_sb.h, o_sb.at(tt + 1))
                            tr_wait(pe, "to", t, c)
                            for g in range(DH):
                                last = nc.tensor.transpose(tr("to", t)[:, g * P:(g + 1) * P], OT[:, 8 * g:8 * g + 8].rearrange("p h d -> p (h d)"), ident[:])
                            last.then_inc(ot_ps.h, 1)

                        def body(c, p, more):
                            for t in range(TL):
                                tt = c * TL + t
                                pe.wait_ge(rc.h, rc.at(tt + 1))
                                tr_wait(pe, "t4", t, c)
                                for g in range(4):
                                    last = nc.tensor.transpose(tr("t4", t)[:, g * P:(g + 1) * P], QN[t % 2][:, 8 * g:8 * g + 8].rearrange("p h d -> p (h d)"), ident[:])
                                last.then_inc(t4_ps.h, 1)
                                if t < TL - 1:
                                    pe_proj(pe, tt + 1, t + 1, c, p, False)
                                elif more:
                                    pe_proj(pe, tt + 1, 0, c + 1, 1 - p, False)
                                if t > 0:
                                    weights_t(pe, tt - 1, t - 1, c)
                                pe.wait_ge(q_sb.h, q_sb.at(tt + 1))
                                pe.wait_ge(kd_sb.h, kd_sb.at(2 * tt + 2))
                                pe.wait_ge(s_sub.h, s_sub.at(tt))
                                if t == 0:
                                    pe.wait_ge(out_taken.h, out_taken.at(2 * c))
                                for g in range(2):
                                    for b in range(2):
                                        last = nc.tensor.matmul(SB_[b * T:(b + 1) * T, g, :], QT[:, g, b * T:(b + 1) * T],
                                                                KB[:, g, b].rearrange("p h k -> p (h k)"), start=True, stop=True)
                                last.then_inc(s_ready.h, 1)
                                if t > 0:
                                    out_t(pe, tt - 1, t - 1, c)
                                if more:
                                    if t == 0:
                                        fr.pe_mean(pe, c + 1)
                                    if t == 1:
                                        fr.pe_var(pe, c + 1)
                            tt = c * TL + TL - 1
                            weights_t(pe, tt, TL - 1, c)
                            out_t(pe, tt, TL - 1, c)
                            pe.wait_ge(ot_hi.h, ot_hi.at(tt + 1))
                            pe.wait_ge(ot_lo.h, ot_lo.at(tt + 1))
                            pe.wait_ge(s_sub.h, s_sub.at(tt + 1))
                            for m in range(DH):
                                for k in range(DH):
                                    last = split3(SB_[:, m, :], WO[0][:, k, m * P:(m + 1) * P], WO[1][:, k, m * P:(m + 1) * P],
                                                  OH[:, k], OL[:, k], k == 0, k == DH - 1)
                            last.then_inc(out_ready.h, 1)
                        chunks(pe, body)

                    @block.scalar
                    def _(act):
                        fr.act_xh(act, 0)
                        fr.act_sq(act, 0)
                        fr.act_rstd(act, 0)
                        fr.act_hh(act, 0, 0)
                        l_act(act)
                        act.wait_ge(step_p.h, step_p.at(2 * TL))
                        act_proj(act, 0, 0)

                        def pt(tt, t, c):
                            for i, kd in enumerate(("pa", "pb")):
                                act.wait_ge(pt_ps.h, pt_ps.at(2 * tt + 1 + i))
                                act.wait_ge(o_ps.h, o_ps.at(tt))
                                nc.scalar.activation(PT[:, 4 * i:4 * i + 4].rearrange("p r q -> p (r q)"), tr(kd, t)[:], ACT.Copy).then_inc(pt_sb.h, 1)

                        def oh(tt, t, c):
                            act.wait_ge(ot_ps.h, ot_ps.at(tt + 1))
                            if t == 0:
                                act.wait_ge(out_ready.h, out_ready.at(c))
                            nc.scalar.activation(OH[:, :, t * P:(t + 1) * P], tr("to", t)[:, 0:2 * P].rearrange("p (g q) -> p g q", g=2),
                                                 ACT.Copy).then_inc(ot_hi.h, 1)

                        def body(c, p, more):
                            for t in range(TL):
                                tt = c * TL + t
                                act.wait_ge(t4_ps.h, t4_ps.at(tt + 1))
                                act.wait_ge(s_ready.h, s_ready.at(tt))
                                nc.scalar.activation(QT[:], tr("t4", t)[:, 0:2 * P].rearrange("p (g q) -> p g q", g=2), ACT.Copy).then_inc(q_sb.h, 1)
                                if t < TL - 1 or more:
                                    act_proj(act, tt + 1, (t + 1) % TL)
                                if t > 0:
                                    pt(tt - 1, t - 1, c)
                                act.wait_ge(s_sub.h, s_sub.at(tt + 1))
                                nc.scalar.activation(SP[t % 2][:], SP[t % 2][:], ACT.Exp, scale=DH1 ** -0.5).then_inc(p_exp.h, 1)
                                if t > 0:
                                    oh(tt - 1, t - 1, c)
                                if more:
                                    if t == 0:
                                        fr.act_xh(act, c + 1)
                                    if t == 1:
                                        fr.act_sq(act, c + 1)
                                        fr.act_rstd(act, c + 1)
                                    if t == 2:
                                        fr.act_hh(act, c + 1, 1 - p)
                            pt(c * TL + TL - 1, TL - 1, c)
                            oh(c * TL + TL - 1, TL - 1, c)
                        chunks(act, body)

                    @block.vector
                    def _(dve):
                        fr.dve_d(dve, 0)
                        fr.dve_v(dve, 0)
                        fr.dve_norm(dve, 0)
                        fr.dve_h(dve, 0, 0)
                        fr.dve_hl(dve, 0, 0)
                        l_dve(dve)
                        dve.wait_ge(step_p.h, step_p.at(2 * TL))
                        dve.wait_ge(d_in.h, d_in.at(n_d))
                        dve_proj(dve, 0, 0)

                        def o_out(tt):
                            dve.wait_ge(o_ps.h, o_ps.at(tt + 1))
                            ov = O.rearrange("p (h d) -> p h d", d=DH1 + 1)
                            nc.vector.reciprocal(rs[:], ov[:, :, DH1]).then_inc(p_rec.h, 1)
                            dve.wait_ge(p_rec.h, p_rec.at(tt + 1))
                            dve.wait_ge(ot_ps.h, ot_ps.at(tt))
                            nc.vector.tensor_tensor(OT[:], ov[:, :, 0:DH1], rs[:].unsqueeze(2).to_broadcast([P, H, DH1]), ALU.mult).then_inc(o_sb.h, 1)

                        def ol(tt, t):
                            dve.wait_ge(ot_hi.h, ot_hi.at(tt + 1))
                            nc.vector.tensor_tensor(OL[:, :, t * P:(t + 1) * P], tr("to", t)[:, 0:2 * P].rearrange("p (g q) -> p g q", g=2),
                                                    OH[:, :, t * P:(t + 1) * P].bitcast(F32), ALU.subtract).then_inc(ot_lo.h, 1)

                        def body(c, p, more):
                            for t in range(TL):
                                tt = c * TL + t
                                dve.wait_ge(q_sb.h, q_sb.at(tt + 1))
                                dve.wait_ge(s_ready.h, s_ready.at(tt))
                                for g in range(2):
                                    src = tr("t4", t)[:, (2 + g) * P:(3 + g) * P].rearrange("p (b k) -> p b k", b=2)
                                    nc.vector.tensor_tensor(KB[:, g], src.unsqueeze(2).to_broadcast([P, 2, 8, T]),
                                                            hmask[:].unsqueeze(1).unsqueeze(3).to_broadcast([P, 2, 8, T]), ALU.mult).then_inc(kd_sb.h, 1)
                                if t < TL - 1 or more:
                                    dve_proj(dve, tt + 1, (t + 1) % TL)
                                if t > 0:
                                    o_out(tt - 1)
                                dve.wait_ge(s_ready.h, s_ready.at(tt + 1))
                                sv = SB_[:].rearrange("p g (h k) -> p (g h) k", k=T)
                                nc.vector.tensor_reduce(mx[:, t % 2], sv, AXX, ALU.max).then_inc(s_max.h, 1)
                                dve.wait_ge(s_max.h, s_max.at(tt + 1))
                                if t == 0:
                                    dve.wait_ge(pt_ps.h, pt_ps.at(2 * tt))
                                else:
                                    dve.wait_ge(pt_ps.h, pt_ps.at(2 * tt - 2))
                                nc.vector.tensor_tensor(SP[t % 2][:], sv, mx[:, t % 2].unsqueeze(2).to_broadcast([P, H, T]), ALU.subtract).then_inc(s_sub.h, 1)
                                if t > 0:
                                    ol(tt - 1, t - 1)
                                if more:
                                    if t == 0:
                                        fr.dve_d(dve, c + 1)
                                    if t == 1:
                                        fr.dve_v(dve, c + 1)
                                    if t == 2:
                                        fr.dve_norm(dve, c + 1)
                                        fr.dve_h(dve, c + 1, 1 - p)
                                        fr.dve_hl(dve, c + 1, 1 - p)
                            o_out(c * TL + TL - 1)
                            ol(c * TL + TL - 1, TL - 1)
                            dve.wait_ge(out_ready.h, out_ready.at(c + 1))
                            residual_dve(dve, c, l, G_A, BC[f"b_out{l}"], RT, S2)
                        chunks(dve, body)

                    @block.gpsimd
                    def _(pool):
                        for i in range(TL):
                            nc.gpsimd.memset(VB[i][:], 0.0).then_inc(step_a.h, 1)
                        pool.wait_ge(step_a.h, step_a.at(TL))
                        for i in range(TL):
                            for half in range(2):
                                nc.gpsimd.memset(VB[i][half * T:(half + 1) * T, :, :, half, DH1], 1.0).then_inc(step_p.h, 1)
                                pool.wait_ge(step_p.h, step_p.at(2 * i + half + 1))
                        fr.pool_xl(pool, 0)
                        fr.pool_sq(pool, 0)
                        fr.pool_scale(pool, 0)
                        pool.wait_ge(d_in.h, d_in.at(n_d))
                        pool_rope(pool, 0, 0)

                        def body(c, p, more):
                            for t in range(TL):
                                tt = c * TL + t
                                if t < TL - 1 or more:
                                    pool_rope(pool, tt + 1, (t + 1) % TL)
                                if more:
                                    if t == 0:
                                        fr.pool_xl(pool, c + 1)
                                    if t == 1:
                                        fr.pool_sq(pool, c + 1)
                                    if t == 2:
                                        fr.pool_scale(pool, c + 1)
                            residual_pool(pool, c, RT)
                        chunks(pool, body)
                fr.passed(); l_passed(); d_in.passed(n_d); step_p.passed(2 * TL); step_a.passed(TL)
                for c in (q_ps, v_ps, t4_ps, q_sb, va_sb, vd_sb, qk_n, rc, ra, s_ready, s_max, s_sub, p_exp, p_rec, o_ps, o_sb, ot_ps, ot_hi, ot_lo):
                    c.passed(NT)
                for c in (kd_sb, pt_ps, pt_sb, rb):
                    c.passed(2 * NT)
                if l == 1:
                    for c in (qk_w, sq_sb, ss_sum, ss_eps, ss_ln, ss_exp, ss_n1, ss_n2, ss_r):
                        c.passed(NT)
                out_ready.passed(NCH); out_taken.passed(2 * NCH); x_added.passed(NCH)

        def low_rank():
            with ExitStack() as sc:
                A3 = sb("A3", [P, 2, DH, B * RANK], scope=sc)
                B3 = sb("B3", [P, 2, B * RANK // P, D], scope=sc)
                bmask = sb("bmask", [P, GB], scope=sc)
                Y = [[sb(f"Y{s}{i}", [P, CH], scope=sc) for i in range(2)] for s in range(2)]
                G3 = [sb(f"G3_{i}", [P, DH, CH], scope=sc) for i in range(2)]
                XO = [sb(f"XO_{i}", [P, DH, CH], scope=sc) for i in range(2)]
                YB = [[BK[0], BK[1]], [BK[2], BK[3]]]
                outT = io["out"].rearrange("(k p) n -> p k n", p=P)

                def mask(c):
                    return bmask[:, CB * (c % 2):CB * (c % 2) + CB].unsqueeze(2).to_broadcast([P, CB, T])

                with nc.Block() as block:
                    @block.sync
                    def _(sp):
                        for a in range(2):
                            sp.dma_start(A3[:, a], io["scrA"][a]).then_inc(d_in.h, 16)
                            sp.dma_start(B3[:, a], io["scrB"][a].rearrange("(g b) (r d) -> (b r) g d", b=GB, r=RANK)
                                         if False else io["scrB"][a].rearrange("b (r d) -> (b r) d", r=RANK).rearrange("(g q) d -> q g d", q=P)
                                         ).then_inc(d_in.h, 16)
                        sp.dma_start(bmask[:], io["bmask"]).then_inc(d_in.h, 16)
                        for c in range(NCH):
                            sp.wait_ge(x_added.h, x_added.at(2 * c + 2))
                            sp.dma_start(outT[:, :, c * CH:(c + 1) * CH], XO[c % 2][:]).then_inc(out_st[c % 2].h, 16)
                        sp.wait_ge(out_st[0].h, out_st[0].at(8 * NCH))
                        sp.wait_ge(out_st[1].h, out_st[1].at(8 * NCH))

                    @block.tensor
                    def _(pe):
                        pe.wait_ge(d_in.h, d_in.at(80))
                        for c in range(NCH):
                            g = c // 2
                            for s in range(2):
                                u = 2 * c + s
                                if c >= 1:
                                    pe.wait_ge(g_hi.h, g_hi.at(u - 1))
                                if s == 1:
                                    pe.wait_ge(g_act.h, g_act.at(2 * c + 2))
                                for k in range(DH):
                                    last = nc.tensor.matmul(YB[s][c % 2][:], A3[:, s, k, g * P:(g + 1) * P],
                                                            X[:, k, c * CH:(c + 1) * CH] if s == 0 else G3[c % 2][:, k],
                                                            start=(k == 0), stop=(k == DH - 1))
                                last.then_inc(a_ps.h, 1)
                                pe.wait_ge(g_hi.h, g_hi.at(u + 1))
                                if c >= 1:
                                    if s == 0:
                                        pe.wait_ge(g_act.h, g_act.at(2 * c))
                                    else:
                                        pe.wait_ge(x_added.h, x_added.at(2 * c))
                                for m in range(DH):
                                    last = nc.tensor.matmul((S2, O2)[s][:, m, :], B3[:, s, g, m * P:(m + 1) * P], Y[s][c % 2][:], start=True, stop=True)
                                    last.then_inc((s_ready, o_ps)[s].h, 1)

                    @block.scalar
                    def _(act):
                        for c in range(NCH):
                            if c >= 2:
                                act.wait_ge(a_ps.h, a_ps.at(2 * c - 2))
                            for m in range(DH):
                                act.wait_ge(s_ready.h, s_ready.at(2 * c + m + 1))
                                nc.scalar.activation(G3[c % 2][:, m], S2[:, m, :], ACT.Gelu).then_inc(g_act.h, 1)

                    @block.vector
                    def _(dve):
                        dve.wait_ge(d_in.h, d_in.at(80))
                        for c in range(NCH):
                            for s in range(2):
                                u = 2 * c + s
                                dve.wait_ge(a_ps.h, a_ps.at(u + 1))
                                if c >= 2:
                                    dve.wait_ge((s_ready, o_ps)[s].h, (s_ready, o_ps)[s].at(2 * c - 2))
                                nc.vector.tensor_tensor(Y[s][c % 2][:].rearrange("p (b t) -> p b t", t=T),
                                                        YB[s][c % 2][:].rearrange("p (b t) -> p b t", t=T), mask(c), ALU.mult).then_inc(g_hi.h, 1)
                            if c >= 2:
                                dve.wait_ge(out_st[c % 2].h, out_st[c % 2].at(16 * (c // 2)))
                            for m in range(DH):
                                dve.wait_ge(o_ps.h, o_ps.at(2 * c + m + 1))
                                nc.vector.tensor_tensor(XO[c % 2][:, m], O2[:, m, :], X[:, m, c * CH:(c + 1) * CH], ALU.add).then_inc(x_added.h, 1)

        attention0()
        feed_forward("b0", 0, "gelu", MLP // P, [io["l0_w1"]], io["l0_w2"], True, 1e-5, BC["b1_0"], BC["b2_0"])
        attention12(1)
        feed_forward("b1", 1, "swiglu", SWIP // P, [io["l1_w1"], io["l1_w3"]], io["l1_w2"], False, 1e-6, None, BC["zero"])
        attention12(2)
        feed_forward("b2", 2, "gelu", MLP // P, [io["l2_w1"]], io["l2_w2"], True, 1e-6, BC["b1_2"], BC["b2_2"])
        feed_forward("c2", 2, "gate", 4, [io["l2_tv"], io["l2_tg"]], io["l2_to"], False, 0.0, None, BC["b_tgo"])
        low_rank()


def kernel(**a):
    import concourse.bacc as bacc
    from concourse.bass_utils import run_bass_kernel_spmd

    a = {k: np.asarray(v) for k, v in a.items()}
    f = np.float32

    def cols(v):
        return v.reshape(-1, P).T

    def heads_apart(w, dh):
        return w.reshape(w.shape[0], PAIRS, 2, dh).transpose(0, 2, 1, 3).reshape(w.shape[0], -1)

    in1 = a["L1_cond_qkv_w"].T
    in2 = a["L2_cond_in_proj_w"].T
    b_in2 = a["L2_cond_in_proj_b"]

    def padded(w, axis):
        pad = [(0, 0), (0, 0)]
        pad[axis] = (0, SWIP - SWI)
        return np.pad(w, pad)

    inv = (f(1.0) / (f(10000.0) ** (np.arange(0, DH1, 2, dtype=f) / f(DH1)))).astype(f)
    ang = (np.arange(T, dtype=f)[:, None] * inv[None, :]).astype(f).astype(np.float64)
    cos, sin = np.cos(ang).astype(f), np.sin(ang).astype(f)
    rope2 = np.stack([np.concatenate([cos, cos], 1), np.concatenate([-sin, sin], 1)], 1)
    rope2 = np.concatenate([rope2, rope2], 0)
    two_pi = [6.28125, 0.0019350051879882812, 3.0199157663446e-07]
    freqs = [1.0, float(f(1.0) / (f(10000.0) ** f(0.5)))]
    w2 = a["L3_cond_W2"].reshape(D, 4, D, RANK).transpose(0, 1, 3, 2).reshape(D, -1)
    b2 = a["L3_cond_b2"].reshape(4, D, RANK)
    arrays = {
        "xT": a["x"].reshape(N, D).T,
        "condT": a["cond_1024"].T, "cond": a["cond_1024"],
        "pos": a["fside_BxSx3_0"].reshape(NT, P, 3).transpose(1, 0, 2),
        "w_mods": np.stack([a["L0_cond_W_mod"], a["L1_cond_ada_w"].T, a["L2_cond_film_w"].T]),
        "b_mods": np.stack([cols(a["L0_cond_b_mod"]), cols(a["L1_cond_ada_b"]), cols(a["L2_cond_film_b"])], 1),
        "norm_w": np.stack([cols(a["L1_cond_norm1_w"]), cols(a["L1_cond_norm2_w"])], 1),
        "ident": np.eye(P, dtype=f),
        "hmask": np.repeat(np.eye(8, dtype=f), DH1, 0),
        "bmask": np.repeat(np.eye(GB, dtype=f), RANK, 0),
        "rope2": rope2,
        "bias_cols": np.concatenate([cols(a[n]) for n in (
            "L0_cond_b_out", "L0_cond_b2", "L1_cond_proj_b", "L2_cond_out_b", "L2_cond_mlp_b2", "L2_cond_tg_out_b",
            "L0_cond_b1", "L2_cond_mlp_b1")] + [np.zeros((P, 6), f)], 1),
        "tg_b": cols(a["L2_cond_tg_fc_b"]),
        "ln_gb": np.stack([a["L3_cond_ln_g"], a["L3_cond_ln_b"]]),
        "l3_b1": cols(a["L3_cond_b1"]), "l3_w1": a["L3_cond_W1"], "l3_w2": w2,
        "l3_b2c": b2[[0, 2]].reshape(2, DH, P, RANK).transpose(2, 0, 1, 3),
        "l3_b2r": b2[[1, 3]].transpose(0, 2, 1).reshape(2, -1),
        "l0_wqk": a["L0_cond_W_qkv"][:, 0:2 * H * DH0], "l0_wv": heads_apart(a["L0_cond_W_qkv"][:, 2 * H * DH0:], DH0),
        "l0_wo": a["L0_cond_W_out"], "l0_w1": a["L0_cond_W1"], "l0_w2": a["L0_cond_W2"],
        "l1_wqk": in1[:, 0:2 * D], "l1_wv": heads_apart(in1[:, 2 * D:], DH1), "l1_wo": a["L1_cond_proj_w"].T,
        "l1_qkrow": np.concatenate([np.tile(a["L1_cond_q_norm_w"], (H, 1)), np.tile(a["L1_cond_k_norm_w"], (H, 1))], 0),
        "l1_w1": padded(a["L1_cond_w1"].T, 1), "l1_w3": padded(a["L1_cond_w3"].T, 1), "l1_w2": padded(a["L1_cond_w2"].T, 0),
        "l2_wqk": in2[:, 0:2 * D], "l2_wv": heads_apart(in2[:, 2 * D:], DH1), "l2_wo": a["L2_cond_out_w"].T,
        "l2_qkrow": b_in2[0:2 * D].reshape(2 * H, DH1),
        "l2_vrow": b_in2[2 * D:].reshape(PAIRS, 2, DH1).transpose(1, 0, 2),
        "l2_w1": a["L2_cond_mlp_w1"].T, "l2_w2": a["L2_cond_mlp_w2"].T,
        "l2_tv": a["L2_cond_tg_fc_w"].T[:, 0:2 * D], "l2_tg": a["L2_cond_tg_fc_w"].T[:, 2 * D:], "l2_to": a["L2_cond_tg_out_w"].T,
    }
    arrays = {k: np.ascontiguousarray(v) for k, v in arrays.items()}
    nc = bacc.Bacc("TRN2", target_bir_lowering=False, num_devices=1)
    io = {k: nc.dram_tensor(k + "_dram", v.shape, F32, kind="ExternalInput").ap() for k, v in arrays.items()}
    io["out"] = nc.dram_tensor("out_dram", (D, N), F32, kind="ExternalOutput").ap()
    io["scrA"] = nc.dram_tensor("scrA_dram", (2, P, DH, B * RANK), F32, kind="Internal").ap()
    io["scrB"] = nc.dram_tensor("scrB_dram", (2, B, D * RANK), F32, kind="Internal").ap()
    io["two_pi"], io["freqs"] = two_pi, freqs
    cond_stack_kernel(nc, io)
    r = run_bass_kernel_spmd(nc, [{k + "_dram": v for k, v in arrays.items()}], core_ids=[0])
    return r.results[0]["out_dram"].T.reshape(B, T, D)
```

```python
import numpy as np
import concourse.bass as bass
from concourse import mybir
from contextlib import ExitStack

F32 = mybir.dt.float32
F32R = mybir.dt.float32r
ACT = mybir.ActivationFunctionType
ALU = mybir.AluOpType
AXX = mybir.AxisListType.X

LN_EXP = "natural_log_exp_and_others"

P = 128
B, T, D = 64, 64, 256
N = B * T
DH = D // P
CH = 512
NCH = N // CH
CB = CH // T
TL = CH // P
NT = N // P
H = 16
PAIRS = H // 2
DH0 = 64
DH1 = 16
MLP = 1024
SWI = 682
SWIP = 768
RANK = 8
GB = P // RANK
CREDIT = 2

SH_A, SC_A, G_A, SH_M, SC_M, G_M = range(6)


class Count:

    def __init__(self, handle):
        self.h, self.base = handle, CREDIT

    def at(self, n):
        return n + self.base

    def passed(self, n):
        self.base += n


def cond_stack_kernel(nc, io):
    ctx = ExitStack()
    with ctx:
        def sb(name, shape, dt=F32, scope=ctx):
            return scope.enter_context(nc.sbuf_tensor(name, shape, dt))

        def pb(name, shape, dt=F32):
            return ctx.enter_context(nc.psum_tensor(name, shape, dt))

        counts = []

        def count(name):
            c = Count(ctx.enter_context(nc.semaphore(name)))
            counts.append(c)
            return c

        X = sb("X", [P, DH, N])
        MOD = [sb(f"MOD{l}", [P, 6, DH, B]) for l in range(3)]
        ident = sb("ident", [P, P])
        mean_f = sb("mean_f", [P, P])
        mean_w = sb("mean_w", [P, P], F32R)
        hmask = sb("hmask", [P, 8])
        rope_c1 = sb("rope_c1", [P, NT, 12])
        rope_s1 = sb("rope_s1", [P, NT, 12])
        bias_cols = sb("bias_cols", [P, 34])
        BC = {"b_out0": 0, "b2_0": 2, "b_out1": 4, "b_out2": 6, "b2_2": 8, "b_tgo": 10, "b1_0": 12, "b1_2": 20, "zero": 28}
        tgb = sb("tgb", [P, 8])
        spare = sb("spare", [P, 2])


        BK = [pb(f"bank{i}", [P, 512]) for i in range(4)]
        S2 = pb("S2", [P, 2, 512])
        O2 = pb("O2", [P, 2, 512])

        f_xs, f_xh, f_xl, f_mean, f_d, f_dd, f_ss, f_sqh, f_sql, f_var, f_v, f_ln, f_rs = [
            count(n) for n in ("f_xs", "f_xh", "f_xl", "f_mean", "f_d", "f_dd", "f_ss", "f_sqh", "f_sql", "f_var", "f_v", "f_ln", "f_rs")]
        f_n1, f_n2, f_n3, f_n, f_m, f_h, f_hh, f_hl = [
            count(n) for n in ("f_n1", "f_n2", "f_n3", "f_n", "f_m", "f_h", "f_hh", "f_hl")]
        out_ready, out_taken, x_added = count("out_ready"), count("out_taken"), count("x_added")
        w_in, w_hi, w_lo = count("w_in"), count("w_hi"), count("w_lo")
        d_in = count("d_in")
        w_st = [count("w_st0"), count("w_st1")]
        out_st = [count("out_st0"), count("out_st1")]
        q_ps, k_ps, v_ps = count("q_ps"), count("k_ps"), count("v_ps")
        q_sb, ka_sb, kd_sb, va_sb, vd_sb = [count(n) for n in ("q_sb", "ka_sb", "kd_sb", "va_sb", "vd_sb")]
        pj_free = [count("pj_free0"), count("pj_free1")]
        s_ready, s_max, s_sub, p_exp, p_sum, p_rec = [count(n) for n in ("s_ready", "s_max", "s_sub", "p_exp", "p_sum", "p_rec")]
        pt_ps, pt_sb, o_ps, o_sb, ot_ps, ot_hi, ot_lo = [
            count(n) for n in ("pt_ps", "pt_sb", "o_ps", "o_sb", "ot_ps", "ot_hi", "ot_lo")]
        a_ps, g_act, g_hi, g_lo, g_used, g_mul, g_act2 = [
            count(n) for n in ("a_ps", "g_act", "g_hi", "g_lo", "g_used", "g_mul", "g_act2")]
        t4_ps, sq_sb, ss_sum, ss_eps, ss_ln, ss_exp, ss_n1, ss_n2, ss_r = [
            count(n) for n in ("t4_ps", "sq_sb", "ss_sum", "ss_eps", "ss_ln", "ss_exp", "ss_n1", "ss_n2", "ss_r")]
        qk_n, qk_w, ra, rb, rc, tr_free0, tr_free1 = [
            count(n) for n in ("qk_n", "qk_w", "ra", "rb", "rc", "tr_free0", "tr_free1")]
        tr_free = [tr_free0, tr_free1]
        step_v, step_a, step_p = count("step_v"), count("step_a"), count("step_p")
        out_dma = count("out_dma")
        spare_done = count("spare_done")

        with nc.Block() as block:
            @block.sync
            def _(sp):
                for c in counts:
                    sp.sem_inc(c.h, CREDIT)

        def seq(eng, cnt):
            n = [0]

            def step(ins):
                ins.then_inc(cnt.h, 1)
                n[0] += 1
                eng.wait_ge(cnt.h, cnt.at(n[0]))
            step.n = n
            return step

        with ExitStack() as sc:
            cT = sb("cT", [P, DH, B], scope=sc)
            cS = sb("cS", [P, DH, B], scope=sc)
            wm = sb("wm", [P, 3, DH, 6 * D], scope=sc)
            bm = sb("bm", [P, 3, 12], scope=sc)
            n12 = sb("n12", [P, 2, DH], scope=sc)
            ang = sb("ang", [P, NT, 3, 2], scope=sc)
            pos = sb("pos", [P, NT, 3], scope=sc)
            an2 = sb("an2", [P, NT, 6], scope=sc)
            an3 = sb("an3", [P, NT, 6], scope=sc)
            ada = sb("ada", [B, D], scope=sc)
            ada2 = sb("ada2", [B, D], scope=sc)
            gB = sb("gB", [B, 2, D], scope=sc)
            st = sb("st", [B, 8], scope=sc)
            aT = sb("aT", [P, DH, B], scope=sc)
            hT = sb("hT", [P, DH, B], scope=sc)
            w1 = sb("w1", [P, DH, D], scope=sc)
            b1 = sb("b1", [P, DH], scope=sc)
            w2 = sb("w2", [P, 2, DH, 2 * D * RANK], scope=sc)
            b2c = sb("b2c", [P, 2, DH, RANK], scope=sc)
            b2r = sb("b2r", [B, 2, D * RANK], scope=sc)
            As = sb("As", [P, 2, DH, B, RANK], scope=sc)
            Bs = sb("Bs", [B, 2, D * RANK], scope=sc)

            with nc.Block() as block:
                small = [(cT[:], io["condT"].rearrange("(k p) b -> p k b", p=P)), (bm[:], io["b_mods"]), (n12[:], io["norm_w"]),
                         (ident[:], io["ident"]), (hmask[:], io["hmask"]), (pos[:], io["pos"]),
                         (ada[:], io["cond"]), (bias_cols[:], io["bias_cols"]), (tgb[:], io["tg_b"]),
                         (gB[:], io["ln_gb"].rearrange("(o a) d -> o a d", o=1).to_broadcast([B, 2, D])),
                         (b1[:], io["l3_b1"]), (b2c[:], io["l3_b2c"]),
                         (b2r[:], io["l3_b2r"].rearrange("(o a) n -> o a n", o=1).to_broadcast([B, 2, D * RANK])),
                         (w1[:], io["l3_w1"].rearrange("(k p) n -> p k n", p=P))]
                n_small = len(small)

                @block.sync
                def _(sp):
                    for dst, src in small:
                        sp.dma_start(dst, src).then_inc(d_in.h, 16)
                    for l in range(3):
                        for k in range(DH):
                            sp.dma_start(wm[:, l, k], io["w_mods"][l, k * P:(k + 1) * P, :]).then_inc(w_in.h, 16)
                    for q in range(2):
                        for k in range(DH):
                            sp.dma_start(w2[:, q, k], io["l3_w2"][k * P:(k + 1) * P, q * 4096:(q + 1) * 4096]).then_inc(w_hi.h, 16)
                    for k in range(DH):
                        for h in range(2):
                            sp.dma_start(X[:, k, h * 2048:(h + 1) * 2048],
                                         io["xT"][k * P:(k + 1) * P, h * 2048:(h + 1) * 2048]).then_inc(w_lo.h, 16)
                    sp.wait_ge(g_act.h, g_act.at(4))
                    for a in range(2):
                        sp.dma_start(io["scrA"][a], As[:, a].rearrange("p h b r -> p h (b r)")).then_inc(out_dma.h, 16)
                    sp.wait_ge(g_hi.h, g_hi.at(8))
                    for a in range(2):
                        sp.dma_start(io["scrB"][a], Bs[:, a, :]).then_inc(out_dma.h, 16)
                    sp.wait_ge(out_dma.h, out_dma.at(64))
                    sp.wait_ge(w_lo.h, w_lo.at(64))

                bk = [BK[0], BK[1], BK[2], BK[3]]

                @block.tensor
                def _(pe):
                    pe.wait_ge(d_in.h, d_in.at(16 * n_small))
                    for l in range(3):
                        pe.wait_ge(w_in.h, w_in.at(96))
                        if l == 0:
                            pe.wait_ge(q_sb.h, q_sb.at(1))
                        for h in range(2):
                            u = l * 2 + h
                            if u >= 2:
                                pe.wait_ge(k_ps.h, k_ps.at(u - 1))
                            for m in range(6 * h, 6 * h + 6):
                                for k in range(DH):
                                    last = nc.tensor.matmul(bk[u % 2][:, (m % 6) * B:(m % 6) * B + B],
                                                            wm[:, l, k, m * P:(m + 1) * P], (cT if l == 1 else cS)[:, k, :],
                                                            start=(k == 0), stop=(k == DH - 1))
                            last.then_inc(q_ps.h, 1)
                    pe.wait_ge(s_sub.h, s_sub.at(1))
                    for k in range(DH):
                        last = nc.tensor.transpose(BK[2][:, k * B:(k + 1) * B], ada2[:, k * P:(k + 1) * P], ident[0:B, 0:B])
                    last.then_inc(t4_ps.h, 1)
                    pe.wait_ge(pt_sb.h, pt_sb.at(1))
                    for m in range(DH):
                        for k in range(DH):
                            last = nc.tensor.matmul(BK[3][:, m * B:(m + 1) * B], w1[:, k, m * P:(m + 1) * P], aT[:, k, :],
                                                    start=(k == 0), stop=(k == DH - 1))
                    last.then_inc(o_ps.h, 1)
                    pe.wait_ge(o_sb.h, o_sb.at(1))
                    pe.wait_ge(k_ps.h, k_ps.at(6))
                    for q in range(2):
                        pe.wait_ge(w_hi.h, w_hi.at(64))
                        for h in range(DH):
                            u = q * 2 + h
                            if u >= 2:
                                pe.wait_ge(g_act.h, g_act.at(u - 1))
                            for r in range(RANK):
                                for k in range(DH):
                                    last = nc.tensor.matmul(BK[u % 2][:, r * B:(r + 1) * B],
                                                            w2[:, q, k, r * D + h * P:r * D + h * P + P], hT[:, k, :],
                                                            start=(k == 0), stop=(k == DH - 1))
                            last.then_inc(a_ps.h, 1)
                    for q in range(2):
                        for n in range(4):
                            u = q * 4 + n
                            if u >= 2:
                                pe.wait_ge(g_hi.h, g_hi.at(u - 1))
                            for k in range(DH):
                                last = nc.tensor.matmul(S2[0:B, u % 2, :], hT[:, k, :],
                                                        w2[:, q, k, 2048 + n * 512:2048 + (n + 1) * 512],
                                                        start=(k == 0), stop=(k == DH - 1))
                            last.then_inc(s_ready.h, 1)

                @block.scalar
                def _(act):
                    act.wait_ge(d_in.h, d_in.at(16 * n_small))
                    nc.scalar.activation(cS[:], cT[:], ACT.Silu).then_inc(q_sb.h, 1)
                    act.wait_ge(s_max.h, s_max.at(1))
                    nc.scalar.activation(st[:, 3:4], st[:, 2:3], ACT.Sqrt).then_inc(p_exp.h, 1)
                    act.wait_ge(qk_n.h, qk_n.at(1))
                    for i, sign in enumerate((-1.0, 1.0)):
                        nc.scalar.activation(rope_s1[:].rearrange("p t (a i) -> p t a i", i=2)[:, :, :, i], an2[:], ACT.Sin,
                                             scale=sign).then_inc(step_a.h, 1)
                    for i in range(2):
                        nc.scalar.activation(rope_c1[:].rearrange("p t (a i) -> p t a i", i=2)[:, :, :, i], an3[:], ACT.Sin,
                                             ).then_inc(step_a.h, 1)
                    act.wait_ge(t4_ps.h, t4_ps.at(1))
                    nc.scalar.activation(aT[:].rearrange("p k b -> p (k b)"), BK[2][:, 0:DH * B], ACT.Copy).then_inc(pt_sb.h, 1)
                    act.wait_ge(o_ps.h, o_ps.at(1))
                    for m in range(DH):
                        ins = nc.scalar.activation(hT[:, m, :], BK[3][:, m * B:(m + 1) * B], ACT.Gelu, bias=b1[:, m:m + 1])
                    ins.then_inc(o_sb.h, 1)

                @block.vector
                def _(dve):
                    step = seq(dve, step_v)
                    step(nc.vector.memset(mean_f[:], 1.0 / D))
                    nc.vector.tensor_copy(mean_w[:], mean_f[:]).then_inc(ka_sb.h, 1)
                    dve.wait_ge(d_in.h, d_in.at(16 * n_small))
                    step(nc.vector.tensor_reduce(st[:, 0:1], ada[:], AXX, ALU.add))
                    step(nc.vector.tensor_scalar(st[:, 0:1], st[:, 0:1], 1.0 / D, None, ALU.mult))
                    step(nc.vector.tensor_scalar(ada2[:], ada[:], st[:, 0:1], None, ALU.subtract))
                    step(nc.vector.tensor_tensor(ada[:], ada2[:], ada2[:], ALU.mult))
                    step(nc.vector.tensor_reduce(st[:, 1:2], ada[:], AXX, ALU.add))
                    nc.vector.tensor_scalar(st[:, 2:3], st[:, 1:2], 1.0 / D, 1e-5, ALU.mult, ALU.add).then_inc(s_max.h, 1)
                    for f, w in enumerate(io["freqs"]):
                        step(nc.vector.tensor_scalar(ang[:, :, :, f], pos[:], w, None, ALU.mult))
                    an = ang[:].rearrange("p t a f -> p t (a f)")
                    step(nc.vector.tensor_scalar(an2[:], an, float(np.float32(1 / (2 * np.pi))), 12582912.0, ALU.mult, ALU.add))
                    step(nc.vector.tensor_scalar(an2[:], an2[:], 12582912.0, None, ALU.subtract))
                    for part in io["two_pi"]:
                        step(nc.vector.scalar_tensor_tensor(out=an.rearrange("p t a -> p (t a)"), in0=an2[:].rearrange("p t a -> p (t a)"),
                                                            scalar=-part, in1=an.rearrange("p t a -> p (t a)"), op0=ALU.mult, op1=ALU.add))
                    lim = 3.1415925
                    step(nc.vector.tensor_scalar(an2[:], an, lim, -lim, ALU.min, ALU.max))
                    step(nc.vector.tensor_scalar(an3[:], an2[:], -1.0, None, ALU.mult))
                    step(nc.vector.tensor_tensor(an3[:], an3[:], an2[:], ALU.max))
                    nc.vector.tensor_scalar(an3[:], an3[:], -1.0, float(np.float32(np.pi / 2)), ALU.mult, ALU.add).then_inc(qk_n.h, 1)
                    for l in range(3):
                        for h in range(2):
                            u = l * 2 + h
                            dve.wait_ge(q_ps.h, q_ps.at(u + 1))
                            nc.vector.tensor_tensor(
                                MOD[l][:, 3 * h:3 * h + 3].rearrange("p a k b -> p (a k) b"),
                                bk[u % 2][:, 0:6 * B].rearrange("p (m b) -> p m b", b=B),
                                bm[:, l, 6 * h:6 * h + 6].unsqueeze(2).to_broadcast([P, 6, B]), ALU.add).then_inc(k_ps.h, 1)
                            dve.wait_ge(k_ps.h, k_ps.at(u + 1))
                            i = SC_A if h == 0 else SC_M
                            if l == 1:
                                for k in range(DH):
                                    step(nc.vector.tensor_scalar(MOD[l][:, i, k], MOD[l][:, i, k], 1.0, n12[:, h, k:k + 1], ALU.add, ALU.mult))
                            else:
                                step(nc.vector.tensor_scalar(MOD[l][:, i], MOD[l][:, i], 1.0, None, ALU.add))
                    dve.wait_ge(p_exp.h, p_exp.at(1))
                    step(nc.vector.reciprocal(st[:, 4:5], st[:, 3:4]))
                    step(nc.vector.scalar_tensor_tensor(out=ada[:], in0=ada2[:], scalar=st[:, 4:5], in1=gB[:, 0], op0=ALU.mult, op1=ALU.mult))
                    nc.vector.tensor_tensor(ada2[:], ada[:], gB[:, 1], ALU.add).then_inc(s_sub.h, 1)
                    for q in range(2):
                        for h in range(DH):
                            u = q * 2 + h
                            dve.wait_ge(a_ps.h, a_ps.at(u + 1))
                            nc.vector.tensor_tensor(
                                As[:, q, h].rearrange("p b r -> p r b"), BK[u % 2][:].rearrange("p (r b) -> p r b", b=B),
                                b2c[:, q, h].unsqueeze(2).to_broadcast([P, RANK, B]), ALU.add).then_inc(g_act.h, 1)
                    for q in range(2):
                        for n in range(4):
                            u = q * 4 + n
                            dve.wait_ge(s_ready.h, s_ready.at(u + 1))
                            nc.vector.tensor_tensor(Bs[:, q, n * 512:(n + 1) * 512], S2[0:B, u % 2, :],
                                                    b2r[:, q, n * 512:(n + 1) * 512], ALU.add).then_inc(g_hi.h, 1)
                    step_v.pending = step.n[0]

            d_in.passed(16 * n_small); w_in.passed(96); w_hi.passed(64); w_lo.passed(64)
            q_ps.passed(6); t4_ps.passed(1); o_ps.passed(1); a_ps.passed(4); s_ready.passed(8)
            q_sb.passed(1); p_exp.passed(1); step_a.passed(4); pt_sb.passed(1); o_sb.passed(1)
            step_v.passed(step_v.pending); ka_sb.passed(1); s_max.passed(1); qk_n.passed(1); k_ps.passed(6)
            s_sub.passed(1); g_act.passed(4); g_hi.passed(8); out_dma.passed(64)

        def tok(c):
            return bass.ds(c * CH, CH)

        def load_split(sp_list, scope):
            big = max(src.shape[1] for src, _, _ in sp_list)
            stage = [sb(f"stage{i}_{nc.next_id()}", [P, big], scope=scope) for i in range(2)]
            n = len(sp_list)

            def sync(sp):
                for i, (src, _, _) in enumerate(sp_list):
                    if i >= 2:
                        sp.wait_ge(w_lo.h, w_lo.at(i - 1))
                    sp.dma_start(stage[i % 2][:, 0:src.shape[1]], src).then_inc(w_st[i % 2].h, 16)

            def scalar(act):
                for i, (src, hi, _) in enumerate(sp_list):
                    act.wait_ge(w_st[i % 2].h, w_st[i % 2].at(16 * (i // 2 + 1)))
                    nc.scalar.activation(hi, stage[i % 2][:, 0:src.shape[1]], ACT.Copy).then_inc(w_hi.h, 1)

            def vector(dve):
                for i, (src, hi, lo) in enumerate(sp_list):
                    dve.wait_ge(w_hi.h, w_hi.at(i + 1))
                    nc.vector.tensor_tensor(lo, stage[i % 2][:, 0:src.shape[1]], hi.bitcast(F32), ALU.subtract).then_inc(w_lo.h, 1)

            def passed():
                w_st[0].passed(16 * ((n + 1) // 2)); w_st[1].passed(16 * (n // 2)); w_hi.passed(n); w_lo.passed(n)
            return sync, scalar, vector, n, passed

        class Front:

            def __init__(self, scope, l, i_sh, i_sc, centred, eps, mean_bank, var_bank, free_mean, free_var, h_free, keep_h=True, preload=False, whole_mean=False):
                tag = f"{nc.next_id()}"
                self.preload, self.whole_mean = preload, whole_mean
                self.l, self.i_sh, self.i_sc, self.centred, self.eps = l, i_sh, i_sc, centred, eps
                self.mean_bank, self.var_bank, self.free_mean, self.free_var, self.h_free = mean_bank, var_bank, free_mean, free_var, h_free
                self.XS = sb("XS" + tag, [P, CH], F32, scope)
                self.FA = sb("FA" + tag, [P, CH], F32R, scope)
                self.FB = sb("FB" + tag, [P, CH], F32R, scope)
                self.Dv = sb("Dv" + tag, [P, DH, CH], F32, scope)
                self.Tm = sb("Tm" + tag, [P, DH, CH], F32, scope)
                self.V1, self.V2, self.V3 = [sb(f"V{i}" + tag, [P, CH], F32, scope) for i in range(3)]
                self.H32 = [sb(f"H32_{i}" + tag, [P, DH, CH], F32, scope) for i in range(2 if keep_h else 1)]
                self.HH = [sb(f"HH_{i}" + tag, [P, DH, CH], F32R, scope) for i in range(2)]
                self.HL = [sb(f"HL_{i}" + tag, [P, DH, CH], F32R, scope) for i in range(2)]

            def h32(self, p):
                return self.H32[p % len(self.H32)]

            def _by_batch(self, i):
                return MOD[self.l][:, i]

            def act_xh(self, act, c):
                act.wait_ge(f_xs.h, f_xs.at(c + 1))
                act.wait_ge(f_var.h, f_var.at(c))
                nc.scalar.activation(self.FA[:], self.XS[:], ACT.Copy).then_inc(f_xh.h, 1)

            def act_square(self, act, c):
                act.wait_ge(f_h.h, f_h.at(c))
                if self.centred:
                    act.wait_ge(f_d.h, f_d.at(c + 1))
                nc.scalar.activation(self.Tm[:], self.Dv[:] if self.centred else X[:, :, tok(c)], ACT.Square).then_inc(f_dd.h, 1)

            def act_sqh(self, act, c):
                act.wait_ge(f_ss.h, f_ss.at(c + 1))
                act.wait_ge(f_var.h, f_var.at(c))
                nc.scalar.activation(self.FA[:], self.XS[:], ACT.Copy).then_inc(f_sqh.h, 1)

            def act_rstd(self, act, c):
                if self.preload:
                    nc.scalar.preload_act_table_set(LN_EXP)
                act.wait_ge(f_v.h, f_v.at(c + 1))
                nc.scalar.activation(self.V2[:], self.V1[:], ACT.Ln).then_inc(f_ln.h, 1)
                act.wait_ge(f_ln.h, f_ln.at(c + 1))
                nc.scalar.activation(self.V2[:], self.V2[:], ACT.Exp, scale=-0.5).then_inc(f_rs.h, 1)

            def act_hh(self, act, c, p):
                act.wait_ge(f_h.h, f_h.at(c + 1))
                nc.scalar.activation(self.HH[p][:], self.h32(p)[:], ACT.Copy).then_inc(f_hh.h, 1)

            def pool_xs(self, pool, c):
                pool.wait_ge(f_sql.h, f_sql.at(c))
                nc.gpsimd.tensor_tensor(self.XS[:], X[:, 0, tok(c)], X[:, 1, tok(c)], ALU.add).then_inc(f_xs.h, 1)

            def pool_xl(self, pool, c):
                pool.wait_ge(f_xh.h, f_xh.at(c + 1))
                nc.gpsimd.tensor_tensor(self.FB[:], self.XS[:], self.FA[:].bitcast(F32), ALU.subtract).then_inc(f_xl.h, 1)

            def pool_ss(self, pool, c):
                pool.wait_ge(f_dd.h, f_dd.at(c + 1))
                if not self.centred or self.whole_mean:
                    pool.wait_ge(f_sql.h, f_sql.at(c))
                nc.gpsimd.tensor_tensor(self.XS[:], self.Tm[:, 0], self.Tm[:, 1], ALU.add).then_inc(f_ss.h, 1)

            def pool_sql(self, pool, c):
                pool.wait_ge(f_sqh.h, f_sqh.at(c + 1))
                nc.gpsimd.tensor_tensor(self.FB[:], self.XS[:], self.FA[:].bitcast(F32), ALU.subtract).then_inc(f_sql.h, 1)

            def pool_h(self, pool, c, p):
                pool.wait_ge(f_n.h, f_n.at(c + 1))
                for k in range(DH):
                    m = MOD[self.l][:, self.i_sc, k, bass.ds(c * CB, CB)].unsqueeze(2).to_broadcast([P, CB, T])
                    nc.gpsimd.tensor_tensor(self.Tm[:, k].rearrange("p (b t) -> p b t", t=T),
                                            self.Dv[:, k].rearrange("p (b t) -> p b t", t=T), m, ALU.mult).then_inc(f_m.h, 1)
                pool.wait_ge(f_m.h, f_m.at(2 * c + 2))
                self.h_free(pool, c)
                if len(self.H32) == 1:
                    pool.wait_ge(f_hl.h, f_hl.at(c))
                h = self.h32(p)
                for k in range(DH):
                    m = MOD[self.l][:, self.i_sh, k, bass.ds(c * CB, CB)].unsqueeze(2).to_broadcast([P, CB, T])
                    last = nc.gpsimd.tensor_tensor(h[:, k].rearrange("p (b t) -> p b t", t=T),
                                                   self.Tm[:, k].rearrange("p (b t) -> p b t", t=T), m, ALU.add)
                last.then_inc(f_h.h, 1)

            def _sum(self, bank):
                nc.tensor.matmul(bank, mean_w[:], self.FB[:], start=True, stop=False)
                return nc.tensor.matmul(bank, mean_w[:], self.FA[:], start=False, stop=True)

            def pe_mean(self, pe, c):
                if self.centred and self.whole_mean:
                    self.free_mean(pe, c)
                    for k in range(DH):
                        last = nc.tensor.matmul(self.mean_bank, mean_f[:], X[:, k, tok(c)], start=(k == 0), stop=(k == DH - 1))
                    last.then_inc(f_mean.h, 1)
                elif self.centred:
                    pe.wait_ge(f_xl.h, f_xl.at(c + 1))
                    self.free_mean(pe, c)
                    self._sum(self.mean_bank).then_inc(f_mean.h, 1)

            def pe_var(self, pe, c):
                pe.wait_ge(f_sql.h, f_sql.at(c + 1))
                self.free_var(pe, c)
                self._sum(self.var_bank).then_inc(f_var.h, 1)

            def dve_d(self, dve, c):
                if self.centred:
                    dve.wait_ge(f_mean.h, f_mean.at(c + 1))
                    dve.wait_ge(f_h.h, f_h.at(c))
                    nc.vector.tensor_tensor(self.Dv[:], X[:, :, tok(c)], self.mean_bank.unsqueeze(1).to_broadcast([P, DH, CH]),
                                            ALU.subtract).then_inc(f_d.h, 1)

            def dve_v(self, dve, c):
                dve.wait_ge(f_var.h, f_var.at(c + 1))
                nc.vector.tensor_scalar(self.V1[:], self.var_bank, self.eps, None, ALU.add).then_inc(f_v.h, 1)

            def dve_norm(self, dve, c):
                dve.wait_ge(f_rs.h, f_rs.at(c + 1))
                nc.vector.scalar_tensor_tensor(out=self.V3[:], in0=self.V2[:], scalar=-0.5, in1=self.V2[:], op0=ALU.mult, op1=ALU.mult).then_inc(f_n1.h, 1)
                dve.wait_ge(f_n1.h, f_n1.at(c + 1))
                nc.vector.tensor_tensor(self.V3[:], self.V3[:], self.V1[:], ALU.mult).then_inc(f_n2.h, 1)
                dve.wait_ge(f_n2.h, f_n2.at(c + 1))
                nc.vector.scalar_tensor_tensor(out=self.V3[:], in0=self.V3[:], scalar=1.5, in1=self.V2[:], op0=ALU.add, op1=ALU.mult).then_inc(f_n3.h, 1)
                dve.wait_ge(f_n3.h, f_n3.at(c + 1))
                r = self.V3[:].unsqueeze(1).to_broadcast([P, DH, CH])
                if self.centred:
                    nc.vector.tensor_tensor(self.Dv[:], self.Dv[:], r, ALU.mult).then_inc(f_n.h, 1)
                else:
                    dve.wait_ge(f_h.h, f_h.at(c))
                    nc.vector.tensor_tensor(self.Dv[:], X[:, :, tok(c)], r, ALU.mult).then_inc(f_n.h, 1)

            def dve_hl(self, dve, c, p):
                dve.wait_ge(f_hh.h, f_hh.at(c + 1))
                nc.vector.tensor_tensor(self.HL[p][:], self.h32(p)[:], self.HH[p][:].bitcast(F32), ALU.subtract).then_inc(f_hl.h, 1)

            def act_all(self, act, c, p, early=False):
                if self.centred and not self.whole_mean:
                    self.act_xh(act, c)
                self.act_square(act, c)
                self.act_sqh(act, c)
                if not early:
                    self.act_rstd(act, c)
                    self.act_hh(act, c, p)

            def pool_all(self, pool, c, early=False):
                if self.centred and not self.whole_mean:
                    self.pool_xs(pool, c)
                    self.pool_xl(pool, c)
                self.pool_ss(pool, c)
                self.pool_sql(pool, c)
                if not early:
                    self.pool_h(pool, c, 0)

            def dve_all(self, dve, c, p, early=False):
                self.dve_d(dve, c)
                if not early:
                    self.dve_v(dve, c)
                    self.dve_norm(dve, c)
                    self.dve_hl(dve, c, p)

            def passed(self):
                if self.centred:
                    for c in (f_mean, f_d):
                        c.passed(NCH)
                if self.centred and not self.whole_mean:
                    for c in (f_xs, f_xh, f_xl):
                        c.passed(NCH)
                f_m.passed(2 * NCH)
                for c in (f_dd, f_ss, f_sqh, f_sql, f_var, f_v, f_ln, f_rs, f_n1, f_n2, f_n3, f_n, f_h, f_hh, f_hl):
                    c.passed(NCH)

        def chunks(eng, body):
            with eng.Fori(0, NCH // 2 - 1) as j:
                body(2 * j, 0, 2)
                body(2 * j + 1, 1, 2)
            body(NCH - 2, 0, 1)
            body(NCH - 1, 1, 0)

        def split3(out, w_hi_ap, w_lo_ap, x_hi, x_lo, first, last):
            nc.tensor.matmul(out, w_lo_ap, x_hi, start=first, stop=False)
            nc.tensor.matmul(out, w_hi_ap, x_lo, start=False, stop=False)
            return nc.tensor.matmul(out, w_hi_ap, x_hi, start=False, stop=last)

        def residual_dve(dve, c, l, i_g, bcol, RT, bank):
            dve.wait_ge(x_added.h, x_added.at(c))
            for m in range(DH):
                residual_half(c, l, m, i_g, bcol, RT, bank)

        def residual_half(c, l, m, i_g, bcol, RT, bank):
            nc.vector.scalar_tensor_tensor(
                out=RT[:, m].rearrange("p (b t) -> p b t", t=T), in0=bank[:, m].rearrange("p (b t) -> p b t", t=T),
                scalar=bias_cols[:, bcol + m:bcol + m + 1],
                in1=MOD[l][:, i_g, m, bass.ds(c * CB, CB)].unsqueeze(2).to_broadcast([P, CB, T]),
                op0=ALU.add, op1=ALU.mult).then_inc(out_taken.h, 1)

        def residual_pool(pool, c, RT):
            pool.wait_ge(out_taken.h, out_taken.at(2 * c + 2))
            nc.gpsimd.tensor_tensor(spare[:, 0:1], RT[:, 0, 0:1], RT[:, 1, 0:1], ALU.add).then_inc(spare_done.h, 1)
            pool.wait_ge(spare_done.h, spare_done.at(1))
            nc.gpsimd.tensor_tensor(X[:, :, tok(c)], X[:, :, tok(c)], RT[:], ALU.add).then_inc(x_added.h, 1)

        def attention0():
            with ExitStack() as sc:
                WQK = [sb(f"WQK0_{i}", [P, DH, 2 * H * DH0], F32R, sc) for i in range(2)]
                WO = [sb(f"WO0_{i}", [P, PAIRS, D], F32R, sc) for i in range(2)]
                WV = sb("WV0", [P, DH, 2, PAIRS, DH0], scope=sc)
                TRA, TRB, S, O = BK[2], BK[3], S2[:, 0, :], S2[:, 1, :]
                fr = Front(sc, 0, SH_A, SC_A, True, 1e-5, TRB[:], TRB[:],
                           lambda pe, c: None, lambda pe, c: None,
                           lambda e, c: None if isinstance(c, int) and c < 2 else e.wait_ge(k_ps.h, k_ps.at(8 * c - 8)))
                Q = [sb(f"Q0_{i}", [P, CH], scope=sc) for i in range(2)]
                KB = [sb(f"KB0_{i}", [P, CB, 2, T], scope=sc) for i in range(2)]
                VB = [sb(f"VB0_{i}", [P, CB, 2, 2, DH0], scope=sc) for i in range(2)]
                SP = [sb(f"SP0_{i}", [P, TL, 2, T], scope=sc) for i in range(2)]
                PT = [sb(f"PT0_{i}", [P, TL, P], scope=sc) for i in range(2)]
                OT = sb("Ot0", [P, TL * 2, DH0], scope=sc)
                OH, OL = [sb(n, [P, CH], F32R, sc) for n in ("OH0", "OL0")]
                mx, sm, rs = [sb(f"{n}0", [P, 2, TL * 2], scope=sc) for n in ("mx", "sm", "rs")]
                RT = sb("RT0", [P, DH, CH], scope=sc)
                wq = io["l0_wqk"].rearrange("(k p) n -> k p n", p=P)
                pieces = [(wq[k][:, n * 512:(n + 1) * 512], WQK[0][:, k, n * 512:(n + 1) * 512], WQK[1][:, k, n * 512:(n + 1) * 512])
                          for n in range(4) for k in range(DH)]
                pieces += [(io["l0_wo"][g * P:(g + 1) * P, :], WO[0][:, g, :], WO[1][:, g, :]) for g in range(PAIRS)]
                l_sync, l_act, l_dve, n_w, l_passed = load_split(pieces, sc)

                def pe_proj(pe, G, jj, c, p, first):
                    if jj == 0:
                        pe.wait_ge(f_hl.h, f_hl.at(c + 1))
                    gr = c * 4 + jj // 2
                    if not first:
                        if jj % 2:
                            pe.wait_ge(va_sb.h, va_sb.at(2 * gr + 1)); pe.wait_ge(vd_sb.h, vd_sb.at(2 * gr + 1))
                        else:
                            pe.wait_ge(q_sb.h, q_sb.at(G))
                    for i, bank in ((0, BK[0]), (1, BK[1])):
                        if i == 1 and not first:
                            if jj % 2:
                                pe.wait_ge(va_sb.h, va_sb.at(2 * gr + 2)); pe.wait_ge(vd_sb.h, vd_sb.at(2 * gr + 2))
                            else:
                                pe.wait_ge(ka_sb.h, ka_sb.at(G)); pe.wait_ge(kd_sb.h, kd_sb.at(G))
                        o = i * H * DH0 + jj * P
                        for k in range(DH):
                            last = split3(bank[:], WQK[0][:, k, o:o + P], WQK[1][:, k, o:o + P], fr.HH[p][:, k], fr.HL[p][:, k],
                                          k == 0, k == DH - 1)
                        last.then_inc((q_ps, k_ps)[i].h, 1)

                def pe_v(pe, G, jj, c, p):
                    for hf in range(2):
                        if hf == 0:
                            pe.wait_ge(q_sb.h, q_sb.at(G + 1))
                        else:
                            pe.wait_ge(ka_sb.h, ka_sb.at(G + 1)); pe.wait_ge(kd_sb.h, kd_sb.at(G + 1))
                        for b in range(CB // 2):
                            for k in range(DH):
                                for h2 in range(2):
                                    bb = hf * CB // 2 + b
                                    last = nc.tensor.matmul(BK[hf][h2 * T:(h2 + 1) * T, b * P:(b + 1) * P],
                                                            fr.h32(p)[:, k, bb * T:(bb + 1) * T], WV[:, k, h2, jj:jj + 2, :],
                                                            start=(k == 0), stop=(k == DH - 1), skip_group_check=True)
                        last.then_inc(v_ps.h, 1)

                def act_proj(act, G, jj, c):
                    act.wait_ge(q_ps.h, q_ps.at(G + 1))
                    if not (isinstance(G, int) and G < 2):
                        act.wait_ge(s_ready.h, s_ready.at(G - 1))
                    nc.scalar.activation(Q[jj % 2][:], BK[0][:], ACT.Copy).then_inc(q_sb.h, 1)
                    act.wait_ge(k_ps.h, k_ps.at(G + 1))
                    nc.scalar.activation(KB[jj % 2][0:T, :, 0, :], BK[1][0:T, :].rearrange("p (b t) -> p b t", t=T), ACT.Copy).then_inc(ka_sb.h, 1)

                def act_v(act, jj, c):
                    if jj % 2 == 0:
                        gr = c * 4 + jj // 2
                        for hf in range(2):
                            act.wait_ge(v_ps.h, v_ps.at(2 * gr + hf + 1))
                            if not (isinstance(gr, int) and gr < 2):
                                act.wait_ge(o_ps.h, o_ps.at(2 * gr - 2))
                            nc.scalar.activation(VB[(jj // 2) % 2][0:T, 4 * hf:4 * hf + 4, :, 0, :],
                                                 BK[hf][0:T, :].rearrange("p (b r d) -> p b r d", b=4, r=2), ACT.Copy).then_inc(va_sb.h, 1)

                def dve_proj(dve, G, jj, c):
                    dve.wait_ge(k_ps.h, k_ps.at(G + 1))
                    if not (isinstance(G, int) and G < 2):
                        dve.wait_ge(s_ready.h, s_ready.at(G - 1))
                    nc.vector.tensor_copy(KB[jj % 2][T:P, :, 1, :], BK[1][T:P, :].rearrange("p (b t) -> p b t", t=T)).then_inc(kd_sb.h, 1)

                def dve_v(dve, jj, c):
                    if jj % 2 == 0:
                        gr = c * 4 + jj // 2
                        for hf in range(2):
                            dve.wait_ge(v_ps.h, v_ps.at(2 * gr + hf + 1))
                            if not (isinstance(gr, int) and gr < 2):
                                dve.wait_ge(o_ps.h, o_ps.at(2 * gr - 2))
                            nc.vector.tensor_copy(VB[(jj // 2) % 2][T:P, 4 * hf:4 * hf + 4, :, 1, :],
                                                  BK[hf][T:P, :].rearrange("p (b r d) -> p b r d", b=4, r=2)).then_inc(vd_sb.h, 1)

                M_NORM, M_HH, M_HL = 2, 4, 5
                M_XH, M_MEAN, M_D, M_SQ, M_SQH = 3, 4, 5, 5, 6
                M_VAR = 1

                def steps(step, residual):
                    def body(c, p, more):
                        for j in range(2, PAIRS):
                            step(c, j, p, more)
                        for j in range(2):
                            step(c + 1, j, 1 - p, more, tail=True)
                        residual(c)
                    return body

                def nxt(c, j, p):
                    return (c, j + 1, p) if j < PAIRS - 1 else (c + 1, 0, 1 - p)

                with nc.Block() as block:
                    @block.sync
                    def _(sp):
                        sp.dma_start(WV[:], io["l0_wv"].rearrange("(k p) (a r d) -> p k a r d", p=P, a=2, r=PAIRS)).then_inc(d_in.h, 16)
                        l_sync(sp)
                        sp.wait_ge(d_in.h, d_in.at(16))

                    @block.tensor
                    def _(pe):
                        for c in range(2):
                            if c:
                                pe.wait_ge(f_v.h, f_v.at(c))
                            fr.pe_mean(pe, c)
                            pe.wait_ge(f_d.h, f_d.at(c + 1))
                            fr.pe_var(pe, c)
                        pe.wait_ge(w_lo.h, w_lo.at(n_w))
                        pe.wait_ge(d_in.h, d_in.at(16))
                        pe_proj(pe, 0, 0, 0, 0, True)
                        pe_v(pe, 0, 0, 0, 0)

                        def step(c, j, p, more, tail=False, first=False):
                            g = c * PAIRS + j
                            if more or not tail:
                                pe.wait_ge(q_sb.h, q_sb.at(g + 1)); pe.wait_ge(ka_sb.h, ka_sb.at(g + 1)); pe.wait_ge(kd_sb.h, kd_sb.at(g + 1))
                                pe.wait_ge(s_sub.h, s_sub.at(g))
                                for t in range(TL):
                                    for b in range(2):
                                        bb = 2 * t + b
                                        last = nc.tensor.matmul(S[b * T:(b + 1) * T, t * P:(t + 1) * P], Q[j % 2][:, bb * T:(bb + 1) * T],
                                                                KB[j % 2][:, bb].rearrange("p a t -> p (a t)"), start=True, stop=True)
                                last.then_inc(s_ready.h, 1)
                            weights = (more or not tail or j == 0) and not (first and j == 0)
                            if weights:
                                pe.wait_ge(p_exp.h, p_exp.at(g))
                                pe.wait_ge(pt_sb.h, pt_sb.at(g - 1))
                                for t in range(TL):
                                    last = nc.tensor.transpose(TRA[:, t * P:(t + 1) * P], SP[(j + 1) % 2][:, t].rearrange("p a t -> p (a t)"), ident[:])
                                last.then_inc(pt_ps.h, 1)
                            if not first:
                                pe.wait_ge(o_sb.h, o_sb.at(g - 1))
                                pe.wait_ge(ot_lo.h, ot_lo.at(g - 2))
                                if j == M_MEAN + 1 and more == 2:
                                    pe.wait_ge(f_d.h, f_d.at(c + 3))
                                if j == 2:
                                    pe.wait_ge(f_v.h, f_v.at(c + (2 if more else 1)))
                                for t in range(TL):
                                    last = nc.tensor.transpose(TRB[:, t * P:(t + 1) * P], OT[:, 2 * t:2 * t + 2, :].rearrange("p a d -> p (a d)"), ident[:])
                                last.then_inc(ot_ps.h, 1)
                            if (not tail and (more or j < PAIRS - 1)) or (tail and more):
                                cn, jn, pn = nxt(c, j, p)
                                pe_proj(pe, g + 1, jn, cn, pn, False)
                            if weights:
                                jw = (j - 1) % PAIRS
                                gr2 = g + 1 - jw % 2
                                pe.wait_ge(pt_sb.h, pt_sb.at(g))
                                pe.wait_ge(va_sb.h, va_sb.at(gr2)); pe.wait_ge(vd_sb.h, vd_sb.at(gr2))
                                pe.wait_ge(o_sb.h, o_sb.at(g - 1))
                                for t in range(TL):
                                    for b in range(2):
                                        last = nc.tensor.matmul(O[b * T:(b + 1) * T, t * P:(t + 1) * P], PT[jw % 2][:, t, b * T:(b + 1) * T],
                                                                VB[(jw // 2) % 2][:, 2 * t + b, jw % 2].rearrange("p a d -> p (a d)"), start=True, stop=True)
                                last.then_inc(o_ps.h, 1)
                            if not first:
                                jo = (j - 2) % PAIRS
                                pe.wait_ge(ot_hi.h, ot_hi.at(g - 1)); pe.wait_ge(ot_lo.h, ot_lo.at(g - 1))
                                if jo == 0:
                                    pe.wait_ge(out_taken.h, out_taken.at(2 * c))
                                for m in range(DH):
                                    last = split3(O2[:, m, :], WO[0][:, jo, m * P:(m + 1) * P], WO[1][:, jo, m * P:(m + 1) * P],
                                                  OH[:], OL[:], jo == 0, jo == PAIRS - 1)
                                last.then_inc(out_ready.h, 1)
                            if (not tail and (more or j < PAIRS - 1)) or (tail and more):
                                if jn % 2 == 0:
                                    pe_v(pe, g + 1, jn, cn, pn)
                            if more == 2 and not first:
                                if j == M_MEAN:
                                    fr.pe_mean(pe, c + 2)
                                if j == M_VAR:
                                    fr.pe_var(pe, c + 1)
                        for j in range(2):
                            step(0, j, 0, 2, first=True)
                        chunks(pe, steps(step, lambda c: None))

                    @block.scalar
                    def _(act):
                        nc.scalar.preload_act_table_set(LN_EXP)
                        fr.act_all(act, 0, 0)
                        fr.act_all(act, 1, 1, early=True)
                        l_act(act)
                        act.wait_ge(step_p.h, step_p.at(4))
                        act_proj(act, 0, 0, 0)
                        act_v(act, 0, 0)

                        def step(c, j, p, more, tail=False, first=False):
                            g = c * PAIRS + j
                            if (more or not tail or j == 0) and not (first and j == 0):
                                act.wait_ge(pt_ps.h, pt_ps.at(g))
                                act.wait_ge(o_ps.h, o_ps.at(g - 2))
                                nc.scalar.activation(PT[(j + 1) % 2][:].rearrange("p t q -> p (t q)"), TRA[:], ACT.Copy).then_inc(pt_sb.h, 1)
                            if not first:
                                act.wait_ge(ot_ps.h, ot_ps.at(g - 1))
                                act.wait_ge(out_ready.h, out_ready.at(g - 2))
                                nc.scalar.activation(OH[:], TRB[:], ACT.Copy).then_inc(ot_hi.h, 1)
                            if more or not tail:
                                act.wait_ge(s_sub.h, s_sub.at(g + 1))
                                nc.scalar.activation(SP[j % 2][:], SP[j % 2][:], ACT.Exp, scale=DH0 ** -0.5).then_inc(p_exp.h, 1)
                            ahead = (not tail and (more or j < PAIRS - 1)) or (tail and more)
                            if ahead:
                                cn, jn, pn = nxt(c, j, p)
                                act_proj(act, g + 1, jn, cn)
                            if ahead:
                                act_v(act, jn, cn)
                            if more and not tail and not first and j == M_NORM:
                                fr.act_rstd(act, c + 1)
                            if more and not tail and j == M_HH:
                                fr.act_hh(act, c + 1, 1 - p)
                            if more == 2 and not tail and not first:
                                if j == M_XH:
                                    fr.act_xh(act, c + 2)
                                if j == M_SQ:
                                    fr.act_square(act, c + 2)
                                if j == M_SQH:
                                    fr.act_sqh(act, c + 2)
                        for j in range(2):
                            step(0, j, 0, 2, first=True)
                        chunks(act, steps(step, lambda c: None))

                    @block.vector
                    def _(dve):
                        fr.dve_all(dve, 0, 0)
                        fr.dve_all(dve, 1, 1, early=True)
                        fr.dve_v(dve, 1)
                        l_dve(dve)
                        dve.wait_ge(step_p.h, step_p.at(4))
                        dve_proj(dve, 0, 0, 0)
                        dve_v(dve, 0, 0)

                        def step(c, j, p, more, tail=False, first=False):
                            g = c * PAIRS + j
                            if more or not tail:
                                dve.wait_ge(s_ready.h, s_ready.at(g + 1))
                                sv = S.rearrange("p (a t) -> p a t", t=T)
                                nc.vector.tensor_reduce(mx[:, j % 2], sv, AXX, ALU.max).then_inc(s_max.h, 1)
                                dve.wait_ge(s_max.h, s_max.at(g + 1))
                                dve.wait_ge(pt_ps.h, pt_ps.at(g - 1))
                                nc.vector.tensor_tensor(SP[j % 2][:].rearrange("p t a k -> p (t a) k"), sv,
                                                        mx[:, j % 2].unsqueeze(2).to_broadcast([P, TL * 2, T]), ALU.subtract).then_inc(s_sub.h, 1)
                            weights = (more or not tail or j == 0) and not (first and j == 0)
                            if weights:
                                i = (j + 1) % 2
                                dve.wait_ge(p_exp.h, p_exp.at(g))
                                nc.vector.tensor_reduce(sm[:, i], SP[i][:].rearrange("p t a k -> p (t a) k"), AXX, ALU.add).then_inc(p_sum.h, 1)
                                dve.wait_ge(p_sum.h, p_sum.at(g))
                                nc.vector.reciprocal(rs[:, i], sm[:, i]).then_inc(p_rec.h, 1)
                            if not first:
                                dve.wait_ge(ot_hi.h, ot_hi.at(g - 1))
                                nc.vector.tensor_tensor(OL[:], TRB[:], OH[:].bitcast(F32), ALU.subtract).then_inc(ot_lo.h, 1)
                            ahead = (not tail and (more or j < PAIRS - 1)) or (tail and more)
                            if ahead:
                                cn, jn, pn = nxt(c, j, p)
                                dve_proj(dve, g + 1, jn, cn)
                            if weights:
                                dve.wait_ge(o_ps.h, o_ps.at(g))
                                dve.wait_ge(p_rec.h, p_rec.at(g))
                                dve.wait_ge(ot_ps.h, ot_ps.at(g - 1))
                                nc.vector.tensor_tensor(OT[:], O.rearrange("p (a d) -> p a d", d=DH0),
                                                        rs[:, i].unsqueeze(2).to_broadcast([P, TL * 2, DH0]), ALU.mult).then_inc(o_sb.h, 1)
                            if ahead:
                                dve_v(dve, jn, cn)
                            if more and not tail and not first and j == M_NORM:
                                fr.dve_norm(dve, c + 1)
                            if more and not tail and j == M_HL:
                                fr.dve_hl(dve, c + 1, 1 - p)
                            if more == 2 and not first:
                                if not tail and j == M_D - 1:
                                    fr.dve_d(dve, c + 2)
                                if tail and j == M_VAR:
                                    fr.dve_v(dve, c + 1)

                        def residual(c):
                            dve.wait_ge(out_ready.h, out_ready.at((c + 1) * PAIRS))
                            residual_dve(dve, c, 0, G_A, BC["b_out0"], RT, O2)

                        for j in range(2):
                            step(0, j, 0, 2, first=True)
                        chunks(dve, steps(step, residual))

                    @block.gpsimd
                    def _(pool):
                        for i in range(2):
                            nc.gpsimd.memset(KB[i][:], 0.0).then_inc(step_p.h, 1)
                            nc.gpsimd.memset(VB[i][:], 0.0).then_inc(step_p.h, 1)
                        fr.pool_all(pool, 0)
                        fr.pool_all(pool, 1, early=True)

                        def body(c, p, more):
                            if more == 2:
                                fr.pool_xs(pool, c + 2)
                            if more:
                                fr.pool_h(pool, c + 1, 1 - p)
                            if more == 2:
                                fr.pool_xl(pool, c + 2)
                                fr.pool_ss(pool, c + 2)
                                fr.pool_sql(pool, c + 2)
                            residual_pool(pool, c, RT)
                        chunks(pool, body)
                fr.passed(); l_passed(); d_in.passed(16); step_p.passed(4)
                n = NCH * PAIRS
                for c in (q_ps, k_ps, q_sb, ka_sb, kd_sb, s_ready, s_max, s_sub, p_exp, p_sum, p_rec, pt_ps, pt_sb, o_ps, o_sb,
                          ot_ps, ot_hi, ot_lo, out_ready, v_ps, va_sb, vd_sb):
                    c.passed(n)
                out_taken.passed(2 * NCH); x_added.passed(NCH)

        def feed_forward(tag, l, kind, n_m, ins1, in2, centred, eps, bcol_in, bcol_out):
            with ExitStack() as sc:
                n_in = len(ins1)
                W1 = [[sb(f"W1{tag}_{a}{i}", [P, DH, n_m * P], F32R, sc) for i in range(2)] for a in range(n_in)]
                W2 = [sb(f"W2{tag}_{i}", [P, n_m, D], F32R, sc) for i in range(2)]
                gate = kind == "gate"
                h_free = lambda e, c: None if isinstance(c, int) and c < 2 else e.wait_ge(a_ps.h, a_ps.at(n_m * (c - 1)))
                MB, VBK = S2[:, 0, :], S2[:, 1, :]
                fr = Front(sc, l, SH_M, SC_M, centred, eps, MB, VBK,
                           lambda pe, c: pe.wait_ge(f_d.h, f_d.at(c)), lambda pe, c: pe.wait_ge(f_v.h, f_v.at(c)), h_free, keep_h=False, preload=True)
                Gf = [sb(f"Gf{tag}{i}", [P, CH], scope=sc) for i in range(2)]
                Gt = [sb(f"Gt{tag}{i}", [P, CH], scope=sc) for i in range(2)]
                Gh = [sb(f"Gh{tag}{i}", [P, CH], F32R, sc) for i in range(2)]
                Gl = [sb(f"Gl{tag}{i}", [P, CH], F32R, sc) for i in range(2)]
                RT = sb(f"RT{tag}", [P, DH, CH], scope=sc)
                pieces = []
                step_w = 512 if (n_m * P) % 512 == 0 else 384
                for n in range(0, n_m * P, step_w):
                    for a in range(n_in):
                        for k in range(DH):
                            pieces.append((ins1[a][k * P:(k + 1) * P, n:n + step_w], W1[a][0][:, k, n:n + step_w], W1[a][1][:, k, n:n + step_w]))
                pieces += [(in2[m * P:(m + 1) * P, :], W2[0][:, m, :], W2[1][:, m, :]) for m in range(n_m)]
                l_sync, l_act, l_dve, n_w, l_passed = load_split(pieces, sc)

                lead = 2 if kind == "gelu" else 1

                def up_bank(a, m):
                    return BK[m % 4] if kind == "gelu" else BK[2 * a + m % 2]

                def bias(a, m):
                    if kind == "gate":
                        return tgb[:, a * n_m + m:a * n_m + m + 1]
                    return bias_cols[:, bcol_in + m:bcol_in + m + 1]

                def h_x(eng, c, p):
                    if eng is nc.scalar:
                        if not (isinstance(c, int) and c < 2):
                            h_free(eng, c)
                        nc.scalar.activation(fr.HH[p][:], X[:, :, tok(c)], ACT.Copy).then_inc(f_hh.h, 1)
                    else:
                        eng.wait_ge(f_hh.h, f_hh.at(c + 1))
                        nc.vector.tensor_tensor(fr.HL[p][:], X[:, :, tok(c)], fr.HH[p][:].bitcast(F32), ALU.subtract).then_inc(f_hl.h, 1)

                if centred:
                    M_NORM, M_HH, M_HL = 1, 4, 4
                    M_XH, M_MEAN, M_D, M_SQ, M_SQH = 1, 3, 4, 5, 6
                else:
                    M_NORM, M_HH, M_HL = 1, 3, 3
                    M_SQ, M_SQH = 3, 4


                with nc.Block() as block:
                    @block.sync
                    def _(sp):
                        l_sync(sp)

                    @block.tensor
                    def _(pe):
                        def up(G, m, c, p, first):
                            if m == 0:
                                pe.wait_ge(f_hl.h, f_hl.at(c + 1))
                            if not first:
                                if kind == "gelu":
                                    pe.wait_ge(g_act.h, g_act.at(G - 3))
                                else:
                                    pe.wait_ge(g_act.h, g_act.at((2 if gate else 1) * (G - 1)))
                                if kind == "swiglu":
                                    pe.wait_ge(g_mul.h, g_mul.at(G - 1))
                            for a in range(n_in):
                                for k in range(DH):
                                    last = split3(up_bank(a, m)[:], W1[a][0][:, k, m * P:(m + 1) * P], W1[a][1][:, k, m * P:(m + 1) * P],
                                                  fr.HH[p][:, k], fr.HL[p][:, k], k == 0, k == DH - 1)
                            last.then_inc(a_ps.h, 1)

                        if not gate:
                            for c in range(2):
                                fr.pe_mean(pe, c)
                                fr.pe_var(pe, c)
                        pe.wait_ge(w_lo.h, w_lo.at(n_w))
                        up(0, 0, 0, 0, True)
                        if lead == 2:
                            up(1, 1, 0, 0, True)

                        def body(c, p, more):
                            for m in range(n_m):
                                g = c * n_m + m
                                if m < n_m - lead:
                                    up(g + lead, m + lead, c, p, False)
                                elif more:
                                    up(g + lead, m + lead - n_m, c + 1, 1 - p, False)
                                if more == 2 and not gate and m == n_m - 1:
                                    fr.pe_var(pe, c + 2)
                                pe.wait_ge(g_lo.h, g_lo.at(g + 1))
                                if m == 0:
                                    pe.wait_ge(out_taken.h, out_taken.at(2 * c))
                                for mo in range(DH):
                                    last = split3(O2[:, mo, :], W2[0][:, m, mo * P:(mo + 1) * P], W2[1][:, m, mo * P:(mo + 1) * P],
                                                  Gh[m % 2][:], Gl[m % 2][:], m == 0, m == n_m - 1)
                                last.then_inc(g_used.h, 1)
                                if more == 2 and centred and m == M_MEAN:
                                    fr.pe_mean(pe, c + 2)
                        chunks(pe, body)

                    @block.scalar
                    def _(act):
                        if gate:
                            h_x(act, 0, 0)
                        else:
                            fr.act_all(act, 0, 0)
                            fr.act_all(act, 1, 1, early=True)
                        l_act(act)

                        def body(c, p, more):
                            for m in range(n_m):
                                g = c * n_m + m
                                act.wait_ge(a_ps.h, a_ps.at(g + 1))
                                act.wait_ge(g_lo.h, g_lo.at(g - 1))
                                src = up_bank(0, m)[:]
                                if kind == "swiglu":
                                    nc.scalar.activation(Gf[m % 2][:], src, ACT.Silu).then_inc(g_act.h, 1)
                                else:
                                    nc.scalar.activation(Gf[m % 2][:], src, ACT.Gelu, bias=bias(0, m)).then_inc(g_act.h, 1)
                                if gate:
                                    nc.scalar.activation(Gt[m % 2][:], BK[2 + m % 2][:], ACT.Tanh, bias=bias(1, m)).then_inc(g_act.h, 1)
                                if gate:
                                    if more and m == 0:
                                        h_x(act, c + 1, 1 - p)
                                    continue
                                if more and m == 0:
                                    fr.act_rstd(act, c + 1)
                                if more and m == M_HH:
                                    fr.act_hh(act, c + 1, 1 - p)
                                if more == 2:
                                    if centred and m == M_XH:
                                        fr.act_xh(act, c + 2)
                                    if m == M_SQ:
                                        fr.act_square(act, c + 2)
                                    if m == M_SQH:
                                        fr.act_sqh(act, c + 2)
                        chunks(act, body)

                    @block.vector
                    def _(dve):
                        if gate:
                            h_x(dve, 0, 0)
                        else:
                            fr.dve_all(dve, 0, 0)
                            fr.dve_all(dve, 1, 1, early=True)
                            fr.dve_v(dve, 1)
                        l_dve(dve)

                        def split_g(g, m):
                            gf = Gf[m % 2][:]
                            if gate:
                                dve.wait_ge(g_act.h, g_act.at(2 * g + 2))
                                nc.vector.tensor_tensor(gf, gf, Gt[m % 2][:], ALU.mult).then_inc(g_mul.h, 1)
                                dve.wait_ge(g_mul.h, g_mul.at(g + 1))
                            else:
                                dve.wait_ge(g_act.h, g_act.at(g + 1))
                            if kind == "swiglu":
                                nc.vector.tensor_tensor(gf, gf, BK[2 + m % 2][:], ALU.mult).then_inc(g_mul.h, 1)
                                dve.wait_ge(g_mul.h, g_mul.at(g + 1))
                            dve.wait_ge(g_used.h, g_used.at(g - 1))
                            nc.vector.tensor_copy(Gh[m % 2][:], gf).then_inc(g_hi.h, 1)
                            dve.wait_ge(g_hi.h, g_hi.at(g + 1))
                            nc.vector.tensor_tensor(Gl[m % 2][:], gf, Gh[m % 2][:].bitcast(F32), ALU.subtract).then_inc(g_lo.h, 1)

                        split_g(0, 0)

                        def body(c, p, more):
                            for m in range(n_m):
                                g = c * n_m + m
                                if m > 0:
                                    split_g(g, m)
                                if gate:
                                    if more and m == 0:
                                        h_x(dve, c + 1, 1 - p)
                                    continue
                                if more and m == M_NORM:
                                    fr.dve_norm(dve, c + 1)
                                if more and m == M_HL:
                                    fr.dve_hl(dve, c + 1, 1 - p)
                                if more == 2 and centred and m == M_D:
                                    fr.dve_d(dve, c + 2)
                            if more == 2 and not gate:
                                fr.dve_v(dve, c + 2)
                            if more:
                                split_g((c + 1) * n_m, 0)
                            dve.wait_ge(g_used.h, g_used.at((c + 1) * n_m))
                            if gate:
                                for mo in range(DH):
                                    nc.vector.scalar_tensor_tensor(out=X[:, mo, tok(c)], in0=O2[:, mo, :], scalar=bias_cols[:, bcol_out + mo:bcol_out + mo + 1],
                                                                   in1=X[:, mo, tok(c)], op0=ALU.add, op1=ALU.add).then_inc(out_taken.h, 1)
                            else:
                                residual_dve(dve, c, l, G_M, bcol_out, RT, O2)
                        chunks(dve, body)

                    @block.gpsimd
                    def _(pool):
                        if not gate:
                            fr.pool_all(pool, 0)
                            fr.pool_all(pool, 1, early=True)

                        def body(c, p, more):
                            if more == 2 and centred:
                                fr.pool_xs(pool, c + 2)
                            if more:
                                fr.pool_h(pool, c + 1, 1 - p)
                            if more == 2:
                                if centred:
                                    fr.pool_xl(pool, c + 2)
                                fr.pool_ss(pool, c + 2)
                                fr.pool_sql(pool, c + 2)
                            residual_pool(pool, c, RT)
                        if not gate:
                            chunks(pool, body)
                if gate:
                    f_hh.passed(NCH); f_hl.passed(NCH)
                else:
                    fr.passed(); x_added.passed(NCH)
                l_passed()
                n = NCH * n_m
                for c in (a_ps, g_hi, g_lo, g_used):
                    c.passed(n)
                g_act.passed(2 * n if gate else n)
                if kind != "gelu":
                    g_mul.passed(n)
                out_taken.passed(2 * NCH)

        def attention12(l):
            with ExitStack() as sc:
                tag = f"a{l}"
                WQK = [sb(f"WQK{tag}_{i}", [P, DH, 2 * D], F32R, sc) for i in range(2)]
                WO = [sb(f"WO{tag}_{i}", [P, DH, D], F32R, sc) for i in range(2)]
                WV = sb("WV" + tag, [P, DH, 2, P], scope=sc)
                SB_ = S2
                fr = Front(sc, l, SH_A, SC_A, l == 2, 1e-6, O2[:, 1, :], O2[:, 1, :],
                           lambda pe, c: pe.wait_ge(f_v.h, f_v.at(c)), (lambda pe, c: pe.wait_ge(f_d.h, f_d.at(c + 1))) if l == 2 else (lambda pe, c: pe.wait_ge(f_v.h, f_v.at(c))),
                           lambda e, c: None if isinstance(c, int) and c < 2 else e.wait_ge(v_ps.h, v_ps.at(TL * (c - 1))), whole_mean=True)
                SQ = sb("SQ" + tag, [P, 2 * H, DH1], scope=sc)
                SS = sb("SS" + tag, [P, 4, 2 * H], scope=sc)
                WN = sb("WN" + tag, [P, 2 * H, DH1], scope=sc)
                VBI = sb("VBI" + tag, [P, PAIRS, DH1], scope=sc)
                RC = sb("RC" + tag, [P, 2, DH1], scope=sc)
                QN = [sb(f"QN{tag}{i}", [P, 2 * H, DH1], scope=sc) for i in range(2)]
                RA = sb("RA" + tag, [P, 2 * H, DH1], scope=sc)
                RB = sb("RB" + tag, [P, 2 * H, DH1], scope=sc)
                QT = [sb(f"QT{tag}{i}", [P, 2, P], scope=sc) for i in range(2)]
                KB = [sb(f"KB{tag}{i}", [P, 2, 2, 8, T], scope=sc) for i in range(2)]
                VB = [sb(f"VB{tag}{i}", [P, 2, PAIRS, 2, DH1 + 1], scope=sc) for i in range(TL)]
                SP = [sb(f"SP{tag}{i}", [P, H, T], scope=sc) for i in range(2)]
                PT = sb("PT" + tag, [P, PAIRS, P], scope=sc)
                mx = sb("mx" + tag, [P, 2, H], scope=sc)
                rs = sb("rs" + tag, [P, H], scope=sc)
                OT = sb("OT" + tag, [P, H, DH1], scope=sc)
                OH = sb("OH" + tag, [P, DH, CH], F32R, sc)
                OL = sb("OL" + tag, [P, DH, CH], F32R, sc)
                RT = sb("RT" + tag, [P, DH, CH], scope=sc)
                w = io[f"l{l}_wqk"]
                pieces = [(w[k * P:(k + 1) * P, :], WQK[0][:, k], WQK[1][:, k]) for k in range(DH)]
                pieces += [(io[f"l{l}_wo"][k * P:(k + 1) * P, :], WO[0][:, k], WO[1][:, k]) for k in range(DH)]
                l_sync, l_act, l_dve, n_w, l_passed = load_split(pieces, sc)
                QKB, VBK, TR, O = BK[0], BK[1], (BK[2], BK[3]), O2[:, 0, 0:PAIRS * 2 * (DH1 + 1)]

                TR_PA, TR_PB, TR_T4, TR_TO = TR[0], TR[1], TR[0], TR[1]

                n_d = 32 if l == 1 else 80

                def pe_proj(pe, tt, t, c, p, first):
                    if t == 0:
                        pe.wait_ge(f_hl.h, f_hl.at(c + 1))
                    if not first:
                        pe.wait_ge(qk_n.h, qk_n.at(tt))
                    for i, (xp, wp) in enumerate(((0, 1), (1, 0), (0, 0))):
                        for k in range(DH):
                            last = nc.tensor.matmul(QKB[:], (fr.HH, fr.HL)[xp][p][:, k, t * P:(t + 1) * P], WQK[wp][:, k],
                                                    start=(i == 0 and k == 0), stop=(i == 2 and k == DH - 1))
                    last.then_inc(q_ps.h, 1)

                def pe_v(pe, tt, t, c, p, first):
                    if not first:
                        pe.wait_ge(va_sb.h, va_sb.at(tt)); pe.wait_ge(vd_sb.h, vd_sb.at(tt))
                    for b in range(2):
                        for k in range(DH):
                            for h2 in range(2):
                                last = nc.tensor.matmul(VBK[h2 * T:(h2 + 1) * T, b * P:(b + 1) * P],
                                                        fr.h32(p)[:, k, t * P + b * T:t * P + (b + 1) * T], WV[:, k, h2],
                                                        start=(k == 0), stop=(k == DH - 1), skip_group_check=True)
                    last.then_inc(v_ps.h, 1)

                def v_src(half):
                    return VBK[half * T:(half + 1) * T, 0:2 * P].rearrange("p (b r d) -> p b r d", b=2, r=PAIRS)

                def act_square(act, tt):
                    if l == 1:
                        act.wait_ge(q_ps.h, q_ps.at(tt + 1))
                        act.wait_ge(ss_sum.h, ss_sum.at(tt))
                        nc.scalar.activation(SQ[:].rearrange("p h d -> p (h d)"), QKB[:], ACT.Square).then_inc(sq_sb.h, 1)

                def act_root(act, tt):
                    if l == 1:
                        act.wait_ge(ss_eps.h, ss_eps.at(tt + 1))
                        nc.scalar.activation(SS[:, 1], SS[:, 0], ACT.Ln).then_inc(ss_ln.h, 1)
                        act.wait_ge(ss_ln.h, ss_ln.at(tt + 1))
                        nc.scalar.activation(SS[:, 1], SS[:, 1], ACT.Exp, scale=-0.5).then_inc(ss_exp.h, 1)

                def act_v(act, tt, t):
                    act.wait_ge(v_ps.h, v_ps.at(tt + 1))
                    if l == 1:
                        if not (isinstance(tt, int) and tt < 2):
                            act.wait_ge(o_ps.h, o_ps.at(tt - 3))
                        nc.scalar.activation(VB[t][0:T, :, :, 0, 0:DH1], v_src(0), ACT.Copy).then_inc(va_sb.h, 1)

                def dve_v(dve, tt, t):
                    dve.wait_ge(v_ps.h, v_ps.at(tt + 1))
                    if not (isinstance(tt, int) and tt < 2):
                        dve.wait_ge(o_ps.h, o_ps.at(tt - 3))
                    if l == 2:
                        for half in range(2):
                            nc.vector.tensor_tensor(VB[t][half * T:(half + 1) * T, :, :, half, 0:DH1], v_src(half),
                                                    VBI[half * T:(half + 1) * T].unsqueeze(1).to_broadcast([T, 2, PAIRS, DH1]),
                                                    ALU.add).then_inc((va_sb, vd_sb)[half].h, 1)
                    else:
                        nc.vector.tensor_copy(VB[t][T:P, :, :, 1, 0:DH1], v_src(1)).then_inc(vd_sb.h, 1)

                def dve_sum(dve, tt):
                    if l == 1:
                        dve.wait_ge(sq_sb.h, sq_sb.at(tt + 1))
                        nc.vector.tensor_reduce(SS[:, 0], SQ[:], AXX, ALU.add).then_inc(ss_sum.h, 1)
                        dve.wait_ge(ss_sum.h, ss_sum.at(tt + 1))
                        nc.vector.tensor_scalar(SS[:, 0], SS[:, 0], 1.0 / DH1, 1e-6, ALU.mult, ALU.add).then_inc(ss_eps.h, 1)

                def dve_qk(dve, tt, t):
                    qk = QKB[:].rearrange("p (h d) -> p h d", d=DH1)
                    if l == 1:
                        dve.wait_ge(ss_exp.h, ss_exp.at(tt + 1))
                        nc.vector.scalar_tensor_tensor(out=SS[:, 2], in0=SS[:, 1], scalar=-0.5, in1=SS[:, 1], op0=ALU.mult, op1=ALU.mult).then_inc(ss_n1.h, 1)
                        dve.wait_ge(ss_n1.h, ss_n1.at(tt + 1))
                        nc.vector.tensor_tensor(SS[:, 2], SS[:, 2], SS[:, 0], ALU.mult).then_inc(ss_n2.h, 1)
                        dve.wait_ge(ss_n2.h, ss_n2.at(tt + 1))
                        nc.vector.scalar_tensor_tensor(out=SS[:, 3], in0=SS[:, 2], scalar=1.5, in1=SS[:, 1], op0=ALU.add, op1=ALU.mult).then_inc(ss_r.h, 1)
                        dve.wait_ge(ss_r.h, ss_r.at(tt + 1))
                    else:
                        dve.wait_ge(q_ps.h, q_ps.at(tt + 1))
                    if not (isinstance(tt, int) and tt < 2):
                        dve.wait_ge(t4_ps.h, t4_ps.at(tt - 1))
                    if l == 1:
                        nc.vector.tensor_tensor(QN[t % 2][:], qk, SS[:, 3].unsqueeze(2).to_broadcast([P, 2 * H, DH1]), ALU.mult).then_inc(qk_n.h, 1)
                    else:
                        nc.vector.tensor_tensor(QN[t % 2][:], qk, WN[:], ALU.add).then_inc(qk_n.h, 1)

                def pool_rope(pool, tt, t):
                    pool.wait_ge(qk_n.h, qk_n.at(tt + 1))
                    q = QN[t % 2]
                    if l == 1:
                        nc.gpsimd.tensor_tensor(q[:], q[:], WN[:], ALU.mult).then_inc(qk_w.h, 1)
                        pool.wait_ge(qk_w.h, qk_w.at(tt + 1))
                        n = 12
                        cs = rope_c1[:, bass.ds(tt, 1), :].to_broadcast([P, 2 * H, n])
                        sn = rope_s1[:, bass.ds(tt, 1), :].rearrange("p o (a i) -> p o a i", i=2)
                        qv = q[:, :, 0:n].rearrange("p h (a i) -> p h a i", i=2)
                        bv = RB[:, :, 0:n].rearrange("p h (a i) -> p h a i", i=2)
                        halves = [(bv[:, :, :, i], qv[:, :, :, 1 - i], sn[:, :, :, i].to_broadcast([P, 2 * H, n // 2])) for i in range(2)]
                    else:
                        n = DH1
                        cs = RC[:, 0:1, :].to_broadcast([P, 2 * H, n])
                        halves = [(RB[:, :, 8 * i:8 * i + 8], q[:, :, 8 - 8 * i:16 - 8 * i], RC[:, 1:2, 8 * i:8 * i + 8].to_broadcast([P, 2 * H, 8]))
                                  for i in range(2)]
                    pool.wait_ge(rc.h, rc.at(tt))
                    nc.gpsimd.tensor_tensor(RA[:, :, 0:n], q[:, :, 0:n], cs, ALU.mult).then_inc(ra.h, 1)
                    for o, a, s_ in halves:
                        nc.gpsimd.tensor_tensor(o, a, s_, ALU.mult).then_inc(rb.h, 1)
                    pool.wait_ge(ra.h, ra.at(tt + 1))
                    pool.wait_ge(rb.h, rb.at(2 * tt + 2))
                    nc.gpsimd.tensor_tensor(q[:, :, 0:n], RA[:, :, 0:n], RB[:, :, 0:n], ALU.add).then_inc(rc.h, 1)

                def ahead(t, more, tail, n):
                    return more >= 1 if tail else t + n < TL or more >= 1

                def steps(step, end):
                    def body(c, p, more):
                        for t in range(1, TL):
                            step(c, t, p, more)
                        step(c + 1, 0, 1 - p, more, tail=True)
                        end(c, more)
                    return body

                with nc.Block() as block:
                    @block.sync
                    def _(sp):
                        sp.dma_start(WV[:], io[f"l{l}_wv"].rearrange("(k p) (a n) -> p k a n", p=P, a=2)).then_inc(d_in.h, 16)
                        sp.dma_start(WN[:], io[f"l{l}_qkrow"].rearrange("(o h) d -> o h d", o=1).to_broadcast([P, 2 * H, DH1])).then_inc(d_in.h, 16)
                        if l == 2:
                            for half in range(2):
                                sp.dma_start(VBI[half * T:(half + 1) * T], io["l2_vrow"][half:half + 1].to_broadcast([T, PAIRS, DH1])).then_inc(d_in.h, 16)
                            sp.dma_start(RC[:], io["rope2"]).then_inc(d_in.h, 16)
                        l_sync(sp)
                        sp.wait_ge(d_in.h, d_in.at(n_d))

                    @block.tensor
                    def _(pe):
                        for c in range(2):
                            fr.pe_mean(pe, c)
                            fr.pe_var(pe, c)
                        pe.wait_ge(w_lo.h, w_lo.at(n_w))
                        pe.wait_ge(d_in.h, d_in.at(n_d))

                        def qk_t(pe, tt, t):
                            pe.wait_ge(rc.h, rc.at(tt + 1))
                            if not (isinstance(tt, int) and tt < 2):
                                pe.wait_ge(pt_sb.h, pt_sb.at(2 * tt - 3))
                            for g in range(4):
                                last = nc.tensor.transpose(TR_T4[:, g * P:(g + 1) * P], QN[t % 2][:, 8 * g:8 * g + 8].rearrange("p h d -> p (h d)"), ident[:])
                            last.then_inc(t4_ps.h, 1)

                        def weights_t(pe, tt, t, followed):
                            pe.wait_ge(p_exp.h, p_exp.at(tt + 1))
                            for i, bank in enumerate((TR_PA, TR_PB)):
                                if i == 0:
                                    if followed:
                                        pe.wait_ge(q_sb.h, q_sb.at(tt + 2)); pe.wait_ge(kd_sb.h, kd_sb.at(2 * tt + 4))
                                else:
                                    pe.wait_ge(ot_lo.h, ot_lo.at(tt if t == 0 else tt - 1))
                                for r in range(4):
                                    last = nc.tensor.transpose(bank[:, r * P:(r + 1) * P],
                                                               SP[t % 2][:, 8 * i + 2 * r:8 * i + 2 * r + 2].rearrange("p h k -> p (h k)"), ident[:])
                                last.then_inc(pt_ps.h, 1)

                        def weigh(pe, tt, t):
                            pe.wait_ge(va_sb.h, va_sb.at(tt + 1)); pe.wait_ge(vd_sb.h, vd_sb.at(tt + 1))
                            pe.wait_ge(o_sb.h, o_sb.at(tt))
                            w_ = 2 * (DH1 + 1)
                            for r in range(PAIRS):
                                if r % 4 == 0:
                                    pe.wait_ge(pt_sb.h, pt_sb.at(2 * tt + 1 + r // 4))
                                for b in range(2):
                                    last = nc.tensor.matmul(O[b * T:(b + 1) * T, r * w_:(r + 1) * w_], PT[:, r, b * T:(b + 1) * T],
                                                            VB[t][:, b, r].rearrange("p a d -> p (a d)"), start=True, stop=True)
                            last.then_inc(o_ps.h, 1)

                        def out_t(pe, tt, t, back):
                            pe.wait_ge(o_sb.h, o_sb.at(tt + 1))
                            if back == 2:
                                pe.wait_ge(pt_sb.h, pt_sb.at(2 * tt + 4))
                            else:
                                pe.wait_ge(ot_lo.h, ot_lo.at(tt))
                            for g in range(DH):
                                last = nc.tensor.transpose(TR_TO[:, g * P:(g + 1) * P], OT[:, 8 * g:8 * g + 8].rearrange("p h d -> p (h d)"), ident[:])
                            last.then_inc(ot_ps.h, 1)

                        def project(m, half):
                            cols = slice(half * CH // 2, (half + 1) * CH // 2)
                            for k in range(DH):
                                last = split3(O2[:, m, cols], WO[0][:, k, m * P:(m + 1) * P], WO[1][:, k, m * P:(m + 1) * P],
                                              OH[:, k, cols], OL[:, k, cols], k == 0, k == DH - 1)
                            return last

                        def project_rest(c, more):
                            pe.wait_ge(o_sb.h, o_sb.at(TL * (c + 1)))
                            project(0, 0)
                            pe.wait_ge(ot_hi.h, ot_hi.at(TL * (c + 1)))
                            pe.wait_ge(ot_lo.h, ot_lo.at(TL * (c + 1)))
                            for m in (1, 0):
                                project(m, 1).then_inc(out_ready.h, 1)

                        def step(c, t, p, more, tail=False, first=False):
                            tt = c * TL + t
                            if ahead(t, more, tail, 2):
                                pe_proj(pe, tt + 2, (t + 2) % TL, c + (t + 2) // TL, (p + (t + 2) // TL) % 2, False)
                            if more or not tail:
                                pe.wait_ge(q_sb.h, q_sb.at(tt + 1))
                                pe.wait_ge(kd_sb.h, kd_sb.at(2 * tt + 2))
                                pe.wait_ge(s_sub.h, s_sub.at(tt))
                                for g in range(2):
                                    for b in range(2):
                                        last = nc.tensor.matmul(SB_[b * T:(b + 1) * T, g, :], QT[t % 2][:, g, b * T:(b + 1) * T],
                                                                KB[t % 2][:, g, b].rearrange("p h k -> p (h k)"), start=True, stop=True)
                                last.then_inc(s_ready.h, 1)
                            if more == 2 and t == 2:
                                fr.pe_mean(pe, c + 2)
                            if more == 2 and tail:
                                fr.pe_var(pe, c + 1)
                            prev = (t - 1) % TL
                            if not first:
                                weights_t(pe, tt - 1, prev, more or not tail)
                            if ahead(t, more, tail, 1):
                                qk_t(pe, tt + 1, (t + 1) % TL)
                            if t != 1 and not first:
                                out_t(pe, tt - 2, (t - 2) % TL, 2)
                            if ahead(t, more, tail, 2):
                                pe_v(pe, tt + 2, (t + 2) % TL, c + (t + 2) // TL, (p + (t + 2) // TL) % 2, False)
                            if not first:
                                if t == 1:
                                    pe.wait_ge(out_taken.h, out_taken.at(2 * c))
                                weigh(pe, tt - 1, prev)
                            if tail:
                                pe.wait_ge(ot_hi.h, ot_hi.at(tt - 2)); pe.wait_ge(ot_lo.h, ot_lo.at(tt - 2))
                                if more:
                                    pe.wait_ge(f_v.h, f_v.at(c + more))
                                project(1, 0)
                                out_t(pe, tt - 1, prev, 1)

                        for t in range(2):
                            pe_proj(pe, t, t, 0, 0, t == 0)
                            pe_v(pe, t, t, 0, 0, t == 0)
                        qk_t(pe, 0, 0)
                        step(0, 0, 0, 2, first=True)
                        chunks(pe, steps(step, project_rest))

                    @block.scalar
                    def _(act):
                        nc.scalar.preload_act_table_set(LN_EXP)
                        fr.act_all(act, 0, 0)
                        fr.act_all(act, 1, 1, early=True)
                        l_act(act)
                        act.wait_ge(step_p.h, step_p.at(2 * TL))

                        def oh(tt, t, c):
                            act.wait_ge(ot_ps.h, ot_ps.at(tt + 1))
                            if t == 0:
                                act.wait_ge(out_ready.h, out_ready.at(2 * c))
                            nc.scalar.activation(OH[:, :, t * P:(t + 1) * P], TR_TO[:, 0:2 * P].rearrange("p (g q) -> p g q", g=2),
                                                 ACT.Copy).then_inc(ot_hi.h, 1)

                        def q_t(tt, t):
                            act.wait_ge(t4_ps.h, t4_ps.at(tt + 1))
                            act.wait_ge(s_ready.h, s_ready.at(tt - 1))
                            nc.scalar.activation(QT[t % 2][:], TR_T4[:, 0:2 * P].rearrange("p (g q) -> p g q", g=2), ACT.Copy).then_inc(q_sb.h, 1)

                        def step(c, t, p, more, tail=False, first=False):
                            tt = c * TL + t
                            prev = (t - 1) % TL
                            if ahead(t, more, tail, 2):
                                act_square(act, tt + 2)
                                act_root(act, tt + 2)
                            if not first:
                                for i, bank in enumerate((TR_PA, TR_PB)):
                                    act.wait_ge(pt_ps.h, pt_ps.at(2 * tt - 1 + i))
                                    act.wait_ge(o_ps.h, o_ps.at(tt - 1))
                                    nc.scalar.activation(PT[:, 4 * i:4 * i + 4].rearrange("p r q -> p (r q)"), bank[:], ACT.Copy).then_inc(pt_sb.h, 1)
                            if more and t == 1:
                                fr.act_hh(act, c + 1, 1 - p)
                            if more == 2 and t == 3:
                                fr.act_sqh(act, c + 2)
                            if ahead(t, more, tail, 1):
                                q_t(tt + 1, (t + 1) % TL)
                            if t != 1 and not first:
                                oh(tt - 2, (t - 2) % TL, c)
                            if more or not tail:
                                act.wait_ge(s_sub.h, s_sub.at(tt + 1))
                                nc.scalar.activation(SP[t % 2][:], SP[t % 2][:], ACT.Exp, scale=DH1 ** -0.5).then_inc(p_exp.h, 1)
                            if ahead(t, more, tail, 2):
                                act_v(act, tt + 2, (t + 2) % TL)
                            if tail:
                                oh(tt - 1, prev, c)
                            if more == 2 and t == 2:
                                fr.act_square(act, c + 2)
                            if more == 2 and tail:
                                fr.act_rstd(act, c + 1)

                        for t in range(2):
                            act_square(act, t)
                            act_v(act, t, t)
                            act_root(act, t)
                        q_t(0, 0)
                        fr.act_rstd(act, 1)
                        step(0, 0, 0, 2, first=True)
                        chunks(act, steps(step, lambda c, more: None))

                    @block.vector
                    def _(dve):
                        fr.dve_all(dve, 0, 0)
                        fr.dve_all(dve, 1, 1, early=True)
                        fr.dve_v(dve, 1)
                        l_dve(dve)
                        dve.wait_ge(step_p.h, step_p.at(2 * TL))
                        dve.wait_ge(d_in.h, d_in.at(n_d))

                        def spread_k(tt, t):
                            dve.wait_ge(q_sb.h, q_sb.at(tt + 1))
                            dve.wait_ge(s_ready.h, s_ready.at(tt - 1))
                            for g in range(2):
                                src = TR_T4[:, (2 + g) * P:(3 + g) * P].rearrange("p (b k) -> p b k", b=2)
                                nc.vector.tensor_tensor(KB[t % 2][:, g], src.unsqueeze(2).to_broadcast([P, 2, 8, T]),
                                                        hmask[:].unsqueeze(1).unsqueeze(3).to_broadcast([P, 2, 8, T]), ALU.mult).then_inc(kd_sb.h, 1)

                        def ol(tt, t):
                            dve.wait_ge(ot_hi.h, ot_hi.at(tt + 1))
                            nc.vector.tensor_tensor(OL[:, :, t * P:(t + 1) * P], TR_TO[:, 0:2 * P].rearrange("p (g q) -> p g q", g=2),
                                                    OH[:, :, t * P:(t + 1) * P].bitcast(F32), ALU.subtract).then_inc(ot_lo.h, 1)

                        def step(c, t, p, more, tail=False, first=False):
                            tt = c * TL + t
                            prev = (t - 1) % TL
                            if ahead(t, more, tail, 2):
                                dve_sum(dve, tt + 2)
                            if more or not tail:
                                dve.wait_ge(s_ready.h, s_ready.at(tt + 1))
                                sv = SB_[:].rearrange("p g (h k) -> p (g h) k", k=T)
                                nc.vector.tensor_reduce(mx[:, t % 2], sv, AXX, ALU.max).then_inc(s_max.h, 1)
                            if ahead(t, more, tail, 2):
                                dve_qk(dve, tt + 2, (t + 2) % TL)
                            if more or not tail:
                                dve.wait_ge(s_max.h, s_max.at(tt + 1))
                                dve.wait_ge(pt_ps.h, pt_ps.at(2 * tt - 2))
                                nc.vector.tensor_tensor(SP[t % 2][:], sv, mx[:, t % 2].unsqueeze(2).to_broadcast([P, H, T]), ALU.subtract).then_inc(s_sub.h, 1)
                            if more == 2 and tail:
                                fr.dve_v(dve, c + 1)
                            if ahead(t, more, tail, 1):
                                spread_k(tt + 1, (t + 1) % TL)
                            if t != 1 and not first:
                                ol(tt - 2, (t - 2) % TL)
                            if more and t == 1:
                                fr.dve_hl(dve, c + 1, 1 - p)
                            if more == 2 and t == 2:
                                fr.dve_d(dve, c + 2)
                            if ahead(t, more, tail, 2):
                                dve_v(dve, tt + 2, (t + 2) % TL)
                            if not first:
                                dve.wait_ge(o_ps.h, o_ps.at(tt))
                                ov = O.rearrange("p (h d) -> p h d", d=DH1 + 1)
                                nc.vector.reciprocal(rs[:], ov[:, :, DH1]).then_inc(p_rec.h, 1)
                                dve.wait_ge(p_rec.h, p_rec.at(tt))
                                dve.wait_ge(ot_ps.h, ot_ps.at(tt - 1))
                                nc.vector.tensor_tensor(OT[:], ov[:, :, 0:DH1], rs[:].unsqueeze(2).to_broadcast([P, H, DH1]), ALU.mult).then_inc(o_sb.h, 1)
                            if tail:
                                ol(tt - 1, prev)
                            if more == 2 and tail:
                                fr.dve_norm(dve, c + 1)

                        def residual(c, more):
                            dve.wait_ge(x_added.h, x_added.at(c))
                            for i, m in enumerate((1, 0)):
                                dve.wait_ge(out_ready.h, out_ready.at(2 * c + i + 1))
                                residual_half(c, l, m, G_A, BC[f"b_out{l}"], RT, O2)

                        for t in range(2):
                            dve_sum(dve, t)
                            dve_v(dve, t, t)
                            dve_qk(dve, t, t)
                        spread_k(0, 0)
                        step(0, 0, 0, 2, first=True)
                        fr.dve_norm(dve, 1)
                        chunks(dve, steps(step, residual))

                    @block.gpsimd
                    def _(pool):
                        for i in range(TL):
                            nc.gpsimd.memset(VB[i][:], 0.0).then_inc(step_a.h, 1)
                        pool.wait_ge(step_a.h, step_a.at(TL))
                        for i in range(TL):
                            for half in range(2):
                                nc.gpsimd.memset(VB[i][half * T:(half + 1) * T, :, :, half, DH1], 1.0).then_inc(step_p.h, 1)
                                pool.wait_ge(step_p.h, step_p.at(2 * i + half + 1))
                        fr.pool_all(pool, 0)
                        fr.pool_all(pool, 1, early=True)
                        pool.wait_ge(d_in.h, d_in.at(n_d))
                        for t in range(2):
                            pool_rope(pool, t, t)

                        def step(c, t, p, more, tail=False, first=False):
                            tt = c * TL + t
                            if ahead(t, more, tail, 2):
                                pool_rope(pool, tt + 2, (t + 2) % TL)
                            if more == 2 and t == 2:
                                fr.pool_ss(pool, c + 2)
                            if more == 2 and t == 3:
                                fr.pool_sql(pool, c + 2)
                            if more == 2 and t == 0:
                                fr.pool_h(pool, c + 1, 1 - p)
                        step(0, 0, 0, 2, first=True)
                        chunks(pool, steps(step, lambda c, more: residual_pool(pool, c, RT)))
                fr.passed(); l_passed(); d_in.passed(n_d); step_p.passed(2 * TL); step_a.passed(TL)
                for c in (q_ps, v_ps, t4_ps, q_sb, va_sb, vd_sb, qk_n, rc, ra, s_ready, s_max, s_sub, p_exp, p_rec, o_ps, o_sb, ot_ps, ot_hi, ot_lo):
                    c.passed(NT)
                for c in (kd_sb, pt_ps, pt_sb, rb):
                    c.passed(2 * NT)
                if l == 1:
                    for c in (qk_w, sq_sb, ss_sum, ss_eps, ss_ln, ss_exp, ss_n1, ss_n2, ss_r):
                        c.passed(NT)
                out_ready.passed(2 * NCH); out_taken.passed(2 * NCH); x_added.passed(NCH)

        def low_rank():
            with ExitStack() as sc:
                A3 = sb("A3", [P, 2, DH, B * RANK], scope=sc)
                B3 = sb("B3", [P, 2, B * RANK // P, D], scope=sc)
                bmask = sb("bmask", [P, GB], scope=sc)
                Y = [[sb(f"Y{s}{i}", [P, CH], scope=sc) for i in range(2)] for s in range(2)]
                G3 = [sb(f"G3_{i}", [P, DH, CH], scope=sc) for i in range(2)]
                XO = [sb(f"XO_{i}", [P, DH, CH], scope=sc) for i in range(2)]
                YB = [[BK[0], BK[1]], [BK[2], BK[3]]]
                outT = io["out"].rearrange("(k p) n -> p k n", p=P)

                def mask(c):
                    return bmask[:, CB * (c % 2):CB * (c % 2) + CB].unsqueeze(2).to_broadcast([P, CB, T])

                with nc.Block() as block:
                    @block.sync
                    def _(sp):
                        for a in range(2):
                            sp.dma_start(A3[:, a], io["scrA"][a]).then_inc(d_in.h, 16)
                            sp.dma_start(B3[:, a], io["scrB"][a].rearrange("b (r d) -> (b r) d", r=RANK).rearrange("(g q) d -> q g d", q=P)).then_inc(d_in.h, 16)
                        sp.dma_start(bmask[:], io["bmask"]).then_inc(d_in.h, 16)
                        for c in range(NCH):
                            sp.wait_ge(x_added.h, x_added.at(2 * c + 2))
                            sp.dma_start(outT[:, :, c * CH:(c + 1) * CH], XO[c % 2][:]).then_inc(out_st[c % 2].h, 16)
                        sp.wait_ge(out_st[0].h, out_st[0].at(8 * NCH))
                        sp.wait_ge(out_st[1].h, out_st[1].at(8 * NCH))

                    @block.tensor
                    def _(pe):
                        pe.wait_ge(d_in.h, d_in.at(80))
                        for c in range(NCH):
                            g = c // 2
                            for s in range(2):
                                u = 2 * c + s
                                if c >= 1:
                                    pe.wait_ge(g_hi.h, g_hi.at(u - 1))
                                if s == 1:
                                    pe.wait_ge(g_act.h, g_act.at(2 * c + 2))
                                for k in range(DH):
                                    last = nc.tensor.matmul(YB[s][c % 2][:], A3[:, s, k, g * P:(g + 1) * P],
                                                            X[:, k, c * CH:(c + 1) * CH] if s == 0 else G3[c % 2][:, k],
                                                            start=(k == 0), stop=(k == DH - 1))
                                last.then_inc(a_ps.h, 1)
                                pe.wait_ge(g_hi.h, g_hi.at(u + 1))
                                if c >= 1:
                                    if s == 0:
                                        pe.wait_ge(g_act.h, g_act.at(2 * c))
                                    else:
                                        pe.wait_ge(x_added.h, x_added.at(2 * c))
                                for m in range(DH):
                                    last = nc.tensor.matmul((S2, O2)[s][:, m, :], B3[:, s, g, m * P:(m + 1) * P], Y[s][c % 2][:], start=True, stop=True)
                                    last.then_inc((s_ready, o_ps)[s].h, 1)

                    @block.scalar
                    def _(act):
                        for c in range(NCH):
                            if c >= 2:
                                act.wait_ge(a_ps.h, a_ps.at(2 * c - 2))
                            for m in range(DH):
                                act.wait_ge(s_ready.h, s_ready.at(2 * c + m + 1))
                                nc.scalar.activation(G3[c % 2][:, m], S2[:, m, :], ACT.Gelu).then_inc(g_act.h, 1)

                    @block.vector
                    def _(dve):
                        dve.wait_ge(d_in.h, d_in.at(80))
                        for c in range(NCH):
                            for s in range(2):
                                u = 2 * c + s
                                dve.wait_ge(a_ps.h, a_ps.at(u + 1))
                                if c >= 2:
                                    dve.wait_ge((s_ready, o_ps)[s].h, (s_ready, o_ps)[s].at(2 * c - 2))
                                nc.vector.tensor_tensor(Y[s][c % 2][:].rearrange("p (b t) -> p b t", t=T),
                                                        YB[s][c % 2][:].rearrange("p (b t) -> p b t", t=T), mask(c), ALU.mult).then_inc(g_hi.h, 1)
                            if c >= 2:
                                dve.wait_ge(out_st[c % 2].h, out_st[c % 2].at(16 * (c // 2)))
                            for m in range(DH):
                                dve.wait_ge(o_ps.h, o_ps.at(2 * c + m + 1))
                                nc.vector.tensor_tensor(XO[c % 2][:, m], O2[:, m, :], X[:, m, c * CH:(c + 1) * CH], ALU.add).then_inc(x_added.h, 1)

        attention0()
        feed_forward("b0", 0, "gelu", MLP // P, [io["l0_w1"]], io["l0_w2"], True, 1e-5, BC["b1_0"], BC["b2_0"])
        attention12(1)
        feed_forward("b1", 1, "swiglu", SWIP // P, [io["l1_w1"], io["l1_w3"]], io["l1_w2"], False, 1e-6, None, BC["zero"])
        attention12(2)
        feed_forward("b2", 2, "gelu", MLP // P, [io["l2_w1"]], io["l2_w2"], True, 1e-6, BC["b1_2"], BC["b2_2"])
        feed_forward("c2", 2, "gate", 4, [io["l2_tv"], io["l2_tg"]], io["l2_to"], False, 0.0, None, BC["b_tgo"])
        low_rank()


def kernel(**a):
    import concourse.bacc as bacc
    from concourse.bass_utils import run_bass_kernel_spmd

    a = {k: np.asarray(v) for k, v in a.items()}
    f = np.float32

    def cols(v):
        return v.reshape(-1, P).T

    def heads_apart(w, dh):
        return w.reshape(w.shape[0], PAIRS, 2, dh).transpose(0, 2, 1, 3).reshape(w.shape[0], -1)

    in1 = a["L1_cond_qkv_w"].T
    in2 = a["L2_cond_in_proj_w"].T
    b_in2 = a["L2_cond_in_proj_b"]

    def padded(w, axis):
        pad = [(0, 0), (0, 0)]
        pad[axis] = (0, SWIP - SWI)
        return np.pad(w, pad)

    inv = (f(1.0) / (f(10000.0) ** (np.arange(0, DH1, 2, dtype=f) / f(DH1)))).astype(f)
    ang = (np.arange(T, dtype=f)[:, None] * inv[None, :]).astype(f).astype(np.float64)
    cos, sin = np.cos(ang).astype(f), np.sin(ang).astype(f)
    rope2 = np.stack([np.concatenate([cos, cos], 1), np.concatenate([-sin, sin], 1)], 1)
    rope2 = np.concatenate([rope2, rope2], 0)
    two_pi = [6.28125, 0.0019350051879882812, 3.0199157663446e-07]
    freqs = [1.0, float(f(1.0) / (f(10000.0) ** f(0.5)))]
    w2 = a["L3_cond_W2"].reshape(D, 4, D, RANK).transpose(0, 1, 3, 2).reshape(D, -1)
    b2 = a["L3_cond_b2"].reshape(4, D, RANK)
    arrays = {
        "xT": a["x"].reshape(N, D).T,
        "condT": a["cond_1024"].T, "cond": a["cond_1024"],
        "pos": a["fside_BxSx3_0"].reshape(NT, P, 3).transpose(1, 0, 2),
        "w_mods": np.stack([a["L0_cond_W_mod"], a["L1_cond_ada_w"].T, a["L2_cond_film_w"].T]),
        "b_mods": np.stack([cols(a["L0_cond_b_mod"]), cols(a["L1_cond_ada_b"]), cols(a["L2_cond_film_b"])], 1),
        "norm_w": np.stack([cols(a["L1_cond_norm1_w"]), cols(a["L1_cond_norm2_w"])], 1),
        "ident": np.eye(P, dtype=f),
        "hmask": np.repeat(np.eye(8, dtype=f), DH1, 0),
        "bmask": np.repeat(np.eye(GB, dtype=f), RANK, 0),
        "rope2": rope2,
        "bias_cols": np.concatenate([cols(a[n]) for n in (
            "L0_cond_b_out", "L0_cond_b2", "L1_cond_proj_b", "L2_cond_out_b", "L2_cond_mlp_b2", "L2_cond_tg_out_b",
            "L0_cond_b1", "L2_cond_mlp_b1")] + [np.zeros((P, 6), f)], 1),
        "tg_b": cols(a["L2_cond_tg_fc_b"]),
        "ln_gb": np.stack([a["L3_cond_ln_g"], a["L3_cond_ln_b"]]),
        "l3_b1": cols(a["L3_cond_b1"]), "l3_w1": a["L3_cond_W1"], "l3_w2": w2,
        "l3_b2c": b2[[0, 2]].reshape(2, DH, P, RANK).transpose(2, 0, 1, 3),
        "l3_b2r": b2[[1, 3]].transpose(0, 2, 1).reshape(2, -1),
        "l0_wqk": a["L0_cond_W_qkv"][:, 0:2 * H * DH0], "l0_wv": heads_apart(a["L0_cond_W_qkv"][:, 2 * H * DH0:], DH0),
        "l0_wo": a["L0_cond_W_out"], "l0_w1": a["L0_cond_W1"], "l0_w2": a["L0_cond_W2"],
        "l1_wqk": in1[:, 0:2 * D], "l1_wv": heads_apart(in1[:, 2 * D:], DH1), "l1_wo": a["L1_cond_proj_w"].T,
        "l1_qkrow": np.concatenate([np.tile(a["L1_cond_q_norm_w"], (H, 1)), np.tile(a["L1_cond_k_norm_w"], (H, 1))], 0),
        "l1_w1": padded(a["L1_cond_w1"].T, 1), "l1_w3": padded(a["L1_cond_w3"].T, 1), "l1_w2": padded(a["L1_cond_w2"].T, 0),
        "l2_wqk": in2[:, 0:2 * D], "l2_wv": heads_apart(in2[:, 2 * D:], DH1), "l2_wo": a["L2_cond_out_w"].T,
        "l2_qkrow": b_in2[0:2 * D].reshape(2 * H, DH1),
        "l2_vrow": b_in2[2 * D:].reshape(PAIRS, 2, DH1).transpose(1, 0, 2),
        "l2_w1": a["L2_cond_mlp_w1"].T, "l2_w2": a["L2_cond_mlp_w2"].T,
        "l2_tv": a["L2_cond_tg_fc_w"].T[:, 0:2 * D], "l2_tg": a["L2_cond_tg_fc_w"].T[:, 2 * D:], "l2_to": a["L2_cond_tg_out_w"].T,
    }
    arrays = {k: np.ascontiguousarray(v) for k, v in arrays.items()}
    nc = bacc.Bacc("TRN2", target_bir_lowering=False, num_devices=1)
    io = {k: nc.dram_tensor(k + "_dram", v.shape, F32, kind="ExternalInput").ap() for k, v in arrays.items()}
    io["out"] = nc.dram_tensor("out_dram", (D, N), F32, kind="ExternalOutput").ap()
    io["scrA"] = nc.dram_tensor("scrA_dram", (2, P, DH, B * RANK), F32, kind="Internal").ap()
    io["scrB"] = nc.dram_tensor("scrB_dram", (2, B, D * RANK), F32, kind="Internal").ap()
    io["two_pi"], io["freqs"] = two_pi, freqs
    cond_stack_kernel(nc, io)
    r = run_bass_kernel_spmd(nc, [{k + "_dram": v for k, v in arrays.items()}], core_ids=[0])
    return r.results[0]["out_dram"].T.reshape(B, T, D)
```
